# Optimizing a Trainium2 kernel written in Bass

```python
import numpy as np
import jax
import jax.numpy as jnp

def _softmax(x, axis=-1):
    return jax.nn.softmax(x, axis=axis)

def _gelu(x):
    return jax.nn.gelu(x, approximate=True)

def _silu(x):
    return jax.nn.silu(x)

def _sigmoid(x):
    return jax.nn.sigmoid(x)

def _layernorm(x, axis=-1, eps=1e-05):
    m = jnp.mean(x, axis=axis, keepdims=True)
    v = jnp.var(x, axis=axis, keepdims=True)
    return (x - m) / jnp.sqrt(v + eps)

def _scatter_add(tgt, idx, src, axis=0):
    return tgt.at[idx].add(src)

def _segment_sum(src, seg, n):
    return jax.ops.segment_sum(src, seg, n)
kernel_name = 'mk_vit_tower_d2_tok_img1024_r4_707bb9'

def setup_inputs(seed: int=0):
    np.random.seed(seed)
    _w = jnp.asarray

    def _rec_inputs():
        import jax
        import jax.numpy as jnp
        _rk = jax.random.key(seed)
        x = -0.000392918 + 0.999932 * jax.random.normal(jax.random.fold_in(_rk, 1), (16, 256, 256, 1), jnp.float32)
        return x
    x = _rec_inputs()

    def _L0_tok_setup():
        import jax, jax.numpy as jnp
        import numpy as np
        INV_SQRT2 = 0.7071067811865476
        LEVEL = 3

        def _split(x, axis):
            ax = axis % x.ndim
            sl0 = [slice(None)] * x.ndim
            sl0[ax] = slice(0, None, 2)
            sl1 = [slice(None)] * x.ndim
            sl1[ax] = slice(1, None, 2)
            x0, x1 = (x[tuple(sl0)], x[tuple(sl1)])
            return ((x0 + x1) * INV_SQRT2, (x0 - x1) * INV_SQRT2)

        def _merge(lo, hi, axis):
            ax = axis % lo.ndim
            e = (lo + hi) * INV_SQRT2
            o = (lo - hi) * INV_SQRT2
            s = jnp.stack([e, o], axis=ax + 1)
            shape = list(lo.shape)
            shape[ax] *= 2
            return s.reshape(shape)

        def _dwt2(x):
            lo, hi = _split(x, -1)
            a, h = _split(lo, -2)
            v, d = _split(hi, -2)
            return (a, h, v, d)

        def _idwt2(a, h, v, d):
            lo = _merge(a, h, -2)
            hi = _merge(v, d, -2)
            return _merge(lo, hi, -1)
        key = jax.random.key(seed)
        ks = jax.random.split(key, 8)
        B, H, W = (16, 256, 256)
        x = jax.random.normal(ks[0], (B, H, W, 1), dtype=jnp.float32)
        na = H // 8 * (W // 8)
        n2 = H // 4 * (W // 4)
        n1 = H // 2 * (W // 2)
        scale = 0.02
        Wa = jax.random.normal(ks[1], (na, 1), dtype=jnp.float32) * scale
        ba = jnp.zeros((1,), jnp.float32)
        Wd1 = jax.random.normal(ks[2], (3 * na, 3), dtype=jnp.float32) * scale
        bd1 = jnp.zeros((3,), jnp.float32)
        Wd2 = jax.random.normal(ks[3], (3 * n2, 3), dtype=jnp.float32) * scale
        bd2 = jnp.zeros((3,), jnp.float32)
        Wd3 = jax.random.normal(ks[4], (3 * n1, 3), dtype=jnp.float32) * scale
        bd3 = jnp.zeros((3,), jnp.float32)
        return {'x': x, 'Wa': Wa, 'ba': ba, 'Wd1': Wd1, 'bd1': bd1, 'Wd2': Wd2, 'bd2': bd2, 'Wd3': Wd3, 'bd3': bd3}
    _L0_tok_all = _L0_tok_setup()
    _L0_tok_in = {k: v for k, v in _L0_tok_all.items() if k in ('Wa', 'ba', 'Wd1', 'bd1', 'Wd2', 'bd2', 'Wd3', 'bd3')}
    del _L0_tok_all

    def _L0_attn_setup():
        import jax, jax.numpy as jnp
        import numpy as np
        EPS = 1e-08

        def unit_projection(x):
            f = jnp.fft.fft(x)
            f = f / (jnp.abs(f) + EPS)
            return jnp.fft.ifft(f).real

        def bind(a, b):
            return jnp.fft.ifft(jnp.fft.fft(a) * jnp.fft.fft(b)).real

        def unbind(s, a):
            return jnp.fft.ifft(jnp.fft.fft(s) * jnp.conj(jnp.fft.fft(a))).real
        key = jax.random.key(seed)
        B, S, D = (4, 1024, 256)
        ks = jax.random.split(key, 7)
        scale = 1.0 / np.sqrt(D)
        x = jax.random.normal(ks[0], (B, S, D), dtype=jnp.float32)
        Wq = jax.random.uniform(ks[1], (D, D), jnp.float32, -scale, scale)
        bq = jax.random.uniform(ks[2], (D,), jnp.float32, -scale, scale)
        Wk = jax.random.uniform(ks[3], (D, D), jnp.float32, -scale, scale)
        bk = jax.random.uniform(ks[4], (D,), jnp.float32, -scale, scale)
        Wv = jax.random.uniform(ks[5], (D, D), jnp.float32, -scale, scale)
        bv = jax.random.uniform(ks[6], (D,), jnp.float32, -scale, scale)
        return {'x': x, 'Wq': Wq, 'bq': bq, 'Wk': Wk, 'bk': bk, 'Wv': Wv, 'bv': bv}
    _L0_attn_all = _L0_attn_setup()
    _L0_attn_in = {k: v for k, v in _L0_attn_all.items() if k in ('Wq', 'bq', 'Wk', 'bk', 'Wv', 'bv')}
    del _L0_attn_all

    def _L0_ffn_setup():
        import jax, jax.numpy as jnp
        import numpy as np
        ALPHA = 1.702
        LIMIT = 7.0
        TOPK = 2
        D, I, E = (256, 512, 8)
        B, S = (2, 512)

        def swiglu(x):
            g = x[..., ::2]
            l = x[..., 1::2]
            g = jnp.minimum(g, LIMIT)
            l = jnp.clip(l, -LIMIT, LIMIT)
            return g * jax.nn.sigmoid(ALPHA * g) * (l + 1.0)
        key = jax.random.key(seed)
        ks = jax.random.split(key, 16)
        sc = 0.02
        n = lambda k, shape, s=sc: jax.random.normal(k, shape, dtype=jnp.float32) * s
        return {'x': jax.random.normal(ks[0], (B, S, D), dtype=jnp.float32), 'gate_w': n(ks[1], (E, D)), 'gate_b': n(ks[2], (E,)), 'w1': n(ks[3], (E, D, 2 * I)), 'b1': n(ks[4], (E, 2 * I)), 'w3': n(ks[5], (E, D, 2 * I)), 'b3': n(ks[6], (E, 2 * I)), 'w2': n(ks[7], (E, I, D)), 'b2': n(ks[8], (E, D)), 'sw1': n(ks[9], (D, 2 * I)), 'sb1': n(ks[10], (2 * I,)), 'sw3': n(ks[11], (D, 2 * I)), 'sb3': n(ks[12], (2 * I,)), 'sw2': n(ks[13], (I, D)), 'sb2': n(ks[14], (D,))}
    _L0_ffn_all = _L0_ffn_setup()
    _L0_ffn_in = {k: v for k, v in _L0_ffn_all.items() if k in ('gate_w', 'gate_b', 'w1', 'b1', 'w3', 'b3', 'w2', 'b2', 'sw1', 'sb1', 'sw3', 'sb3', 'sw2', 'sb2')}
    del _L0_ffn_all

    def _L1_attn_setup():
        import jax, jax.numpy as jnp
        import numpy as np
        B, T, C = (8, 512, 256)
        NL, LID = (12, 1)
        H = 4 * C

        def _ln(x, g, b):
            m = x.mean(-1, keepdims=True)
            v = ((x - m) ** 2).mean(-1, keepdims=True)
            return (x - m) * jax.lax.rsqrt(v + 1e-05) * g + b

        def _shift(x):
            return jnp.pad(x, ((0, 0), (1, 0), (0, 0)))[:, :-1]

        def _wkv(time_decay, time_first, k, v):
            w = -jnp.exp(time_decay)
            kt = jnp.moveaxis(k, 1, 0)
            vt = jnp.moveaxis(v, 1, 0)
            Bb, Cc = (k.shape[0], k.shape[2])
            init = (jnp.zeros((Bb, Cc), k.dtype), jnp.zeros((Bb, Cc), k.dtype), jnp.full((Bb, Cc), -1e+38, k.dtype))

            def step(carry, kv_t):
                aa, bb, pp = carry
                kk, vv = kv_t
                ww = time_first + kk
                p = jnp.maximum(pp, ww)
                e1 = jnp.exp(pp - p)
                e2 = jnp.exp(ww - p)
                out = (e1 * aa + e2 * vv) / (e1 * bb + e2)
                ww2 = pp + w
                p2 = jnp.maximum(ww2, kk)
                e1b = jnp.exp(ww2 - p2)
                e2b = jnp.exp(kk - p2)
                return ((e1b * aa + e2b * vv, e1b * bb + e2b, p2), out)
            _, out = jax.lax.scan(step, init, (kt, vt))
            return jnp.moveaxis(out, 0, 1)
        key = jax.random.key(seed)
        ks = jax.random.split(key, 8)
        f = lambda i, shape: 0.02 * jax.random.normal(ks[i], shape, jnp.float32)
        r01 = LID / (NL - 1)
        r10 = 1.0 - LID / NL
        h = np.arange(C, dtype=np.float64)
        decay = (-5 + 8 * (h / (C - 1)) ** (0.7 + 1.3 * r01)).astype(np.float32)
        zig = np.array([(i + 1) % 3 - 1 for i in range(C)]) * 0.5
        tfirst = (np.ones(C) * np.log(0.3) + zig).astype(np.float32)
        xpos = h / C
        tmk = (xpos ** r10).astype(np.float32)
        tmv = (xpos ** r10 + 0.3 * r01).astype(np.float32)
        tmr = (xpos ** (0.5 * r10)).astype(np.float32)
        cm = (xpos ** r10).astype(np.float32)
        return dict(x=jax.random.normal(ks[0], (B, T, C), jnp.float32), ln1_g=jnp.ones(C, jnp.float32), ln1_b=jnp.zeros(C, jnp.float32), ln2_g=jnp.ones(C, jnp.float32), ln2_b=jnp.zeros(C, jnp.float32), time_decay=jnp.asarray(decay), time_first=jnp.asarray(tfirst), time_mix_k=jnp.asarray(tmk), time_mix_v=jnp.asarray(tmv), time_mix_r=jnp.asarray(tmr), att_Wk=f(1, (C, C)), att_Wv=f(2, (C, C)), att_Wr=f(3, (C, C)), att_Wo=f(4, (C, C)), cm_k=jnp.asarray(cm), cm_r=jnp.asarray(cm), ffn_Wk=f(5, (H, C)), ffn_Wr=f(6, (C, C)), ffn_Wv=f(7, (C, H)))
    _L1_attn_all = _L1_attn_setup()
    _L1_attn_in = {k: v for k, v in _L1_attn_all.items() if k in ('ln1_g', 'ln1_b', 'ln2_g', 'ln2_b', 'time_decay', 'time_first', 'time_mix_k', 'time_mix_v', 'time_mix_r', 'att_Wk', 'att_Wv', 'att_Wr', 'att_Wo', 'cm_k', 'cm_r', 'ffn_Wk', 'ffn_Wr', 'ffn_Wv')}
    del _L1_attn_all

    def _L1_ffn_setup():
        import jax, jax.numpy as jnp
        import numpy as np
        EPS = 1e-08

        def _ternary_linear(x, w):
            alpha = jnp.mean(jnp.abs(w))
            w_t = jnp.sign(w) * (jnp.abs(w) > 0.5 * alpha).astype(w.dtype)
            w_q = w + jax.lax.stop_gradient(w_t - w)
            d = x.shape[-1]
            rms = jnp.sqrt(jnp.sum(x * x, axis=-1, keepdims=True)) / jnp.sqrt(jnp.asarray(d, x.dtype))
            x_norm = x / (rms + EPS)
            return jnp.einsum('bsd,fd->bsf', x_norm, w_q)
        key = jax.random.key(seed)
        k1, k2, k3 = jax.random.split(key, 3)
        d_model, d_ff = (256, 1024)
        B, S = (4, 1024)
        x = jax.random.normal(k1, (B, S, d_model), dtype=jnp.float32)
        w_up = jax.random.normal(k2, (d_ff, d_model), dtype=jnp.float32) * 0.02
        w_down = jax.random.normal(k3, (d_model, d_ff), dtype=jnp.float32) * 0.02
        return {'x': x, 'w_up': w_up, 'w_down': w_down}
    _L1_ffn_all = _L1_ffn_setup()
    _L1_ffn_in = {k: v for k, v in _L1_ffn_all.items() if k in ('w_up', 'w_down')}
    del _L1_ffn_all
    return {'x': x, 'L0_tok_Wa': _L0_tok_in['Wa'], 'L0_tok_ba': _L0_tok_in['ba'], 'L0_tok_Wd1': _L0_tok_in['Wd1'], 'L0_tok_bd1': _L0_tok_in['bd1'], 'L0_tok_Wd2': _L0_tok_in['Wd2'], 'L0_tok_bd2': _L0_tok_in['bd2'], 'L0_tok_Wd3': _L0_tok_in['Wd3'], 'L0_tok_bd3': _L0_tok_in['bd3'], 'L0_attn_Wq': _L0_attn_in['Wq'], 'L0_attn_bq': _L0_attn_in['bq'], 'L0_attn_Wk': _L0_attn_in['Wk'], 'L0_attn_bk': _L0_attn_in['bk'], 'L0_attn_Wv': _L0_attn_in['Wv'], 'L0_attn_bv': _L0_attn_in['bv'], 'L0_ffn_gate_w': _L0_ffn_in['gate_w'], 'L0_ffn_gate_b': _L0_ffn_in['gate_b'], 'L0_ffn_w1': _L0_ffn_in['w1'], 'L0_ffn_b1': _L0_ffn_in['b1'], 'L0_ffn_w3': _L0_ffn_in['w3'], 'L0_ffn_b3': _L0_ffn_in['b3'], 'L0_ffn_w2': _L0_ffn_in['w2'], 'L0_ffn_b2': _L0_ffn_in['b2'], 'L0_ffn_sw1': _L0_ffn_in['sw1'], 'L0_ffn_sb1': _L0_ffn_in['sb1'], 'L0_ffn_sw3': _L0_ffn_in['sw3'], 'L0_ffn_sb3': _L0_ffn_in['sb3'], 'L0_ffn_sw2': _L0_ffn_in['sw2'], 'L0_ffn_sb2': _L0_ffn_in['sb2'], 'L1_attn_ln1_g': _L1_attn_in['ln1_g'], 'L1_attn_ln1_b': _L1_attn_in['ln1_b'], 'L1_attn_ln2_g': _L1_attn_in['ln2_g'], 'L1_attn_ln2_b': _L1_attn_in['ln2_b'], 'L1_attn_time_decay': _L1_attn_in['time_decay'], 'L1_attn_time_first': _L1_attn_in['time_first'], 'L1_attn_time_mix_k': _L1_attn_in['time_mix_k'], 'L1_attn_time_mix_v': _L1_attn_in['time_mix_v'], 'L1_attn_time_mix_r': _L1_attn_in['time_mix_r'], 'L1_attn_att_Wk': _L1_attn_in['att_Wk'], 'L1_attn_att_Wv': _L1_attn_in['att_Wv'], 'L1_attn_att_Wr': _L1_attn_in['att_Wr'], 'L1_attn_att_Wo': _L1_attn_in['att_Wo'], 'L1_attn_cm_k': _L1_attn_in['cm_k'], 'L1_attn_cm_r': _L1_attn_in['cm_r'], 'L1_attn_ffn_Wk': _L1_attn_in['ffn_Wk'], 'L1_attn_ffn_Wr': _L1_attn_in['ffn_Wr'], 'L1_attn_ffn_Wv': _L1_attn_in['ffn_Wv'], 'L1_ffn_w_up': _L1_ffn_in['w_up'], 'L1_ffn_w_down': _L1_ffn_in['w_down']}

def reference(x, L0_tok_Wa, L0_tok_ba, L0_tok_Wd1, L0_tok_bd1, L0_tok_Wd2, L0_tok_bd2, L0_tok_Wd3, L0_tok_bd3, L0_attn_Wq, L0_attn_bq, L0_attn_Wk, L0_attn_bk, L0_attn_Wv, L0_attn_bv, L0_ffn_gate_w, L0_ffn_gate_b, L0_ffn_w1, L0_ffn_b1, L0_ffn_w3, L0_ffn_b3, L0_ffn_w2, L0_ffn_b2, L0_ffn_sw1, L0_ffn_sb1, L0_ffn_sw3, L0_ffn_sb3, L0_ffn_sw2, L0_ffn_sb2, L1_attn_ln1_g, L1_attn_ln1_b, L1_attn_ln2_g, L1_attn_ln2_b, L1_attn_time_decay, L1_attn_time_first, L1_attn_time_mix_k, L1_attn_time_mix_v, L1_attn_time_mix_r, L1_attn_att_Wk, L1_attn_att_Wv, L1_attn_att_Wr, L1_attn_att_Wo, L1_attn_cm_k, L1_attn_cm_r, L1_attn_ffn_Wk, L1_attn_ffn_Wr, L1_attn_ffn_Wv, L1_ffn_w_up, L1_ffn_w_down):
    import jax
    import jax.numpy as jnp

    def _L0_tok_ref(x, Wa, ba, Wd1, bd1, Wd2, bd2, Wd3, bd3):
        import jax, jax.numpy as jnp
        import numpy as np
        INV_SQRT2 = 0.7071067811865476
        LEVEL = 3

        def _split(x, axis):
            ax = axis % x.ndim
            sl0 = [slice(None)] * x.ndim
            sl0[ax] = slice(0, None, 2)
            sl1 = [slice(None)] * x.ndim
            sl1[ax] = slice(1, None, 2)
            x0, x1 = (x[tuple(sl0)], x[tuple(sl1)])
            return ((x0 + x1) * INV_SQRT2, (x0 - x1) * INV_SQRT2)

        def _merge(lo, hi, axis):
            ax = axis % lo.ndim
            e = (lo + hi) * INV_SQRT2
            o = (lo - hi) * INV_SQRT2
            s = jnp.stack([e, o], axis=ax + 1)
            shape = list(lo.shape)
            shape[ax] *= 2
            return s.reshape(shape)

        def _dwt2(x):
            lo, hi = _split(x, -1)
            a, h = _split(lo, -2)
            v, d = _split(hi, -2)
            return (a, h, v, d)

        def _idwt2(a, h, v, d):
            lo = _merge(a, h, -2)
            hi = _merge(v, d, -2)
            return _merge(lo, hi, -1)
        img = x[..., 0]
        B = img.shape[0]
        details = []
        cur = img
        for _ in range(LEVEL):
            cur, h, v, d = _dwt2(cur)
            details.append((h, v, d))
        aw = jax.nn.sigmoid(cur.reshape(B, -1) @ Wa + ba)
        rec = cur * aw[:, :, None]
        det_params = [(Wd1, bd1), (Wd2, bd2), (Wd3, bd3)]
        for (h, v, d), (Wd, bd) in zip(reversed(details), det_params):
            flat = jnp.stack([h, v, d], axis=1).reshape(B, -1)
            w = jax.nn.softmax(flat @ Wd + bd, axis=-1)
            rec = _idwt2(rec, h * w[:, 0, None, None], v * w[:, 1, None, None], d * w[:, 2, None, None])
        return rec

    def _L0_attn_ref(x, Wq, bq, Wk, bk, Wv, bv):
        import jax, jax.numpy as jnp
        import numpy as np
        EPS = 1e-08

        def unit_projection(x):
            f = jnp.fft.fft(x)
            f = f / (jnp.abs(f) + EPS)
            return jnp.fft.ifft(f).real

        def bind(a, b):
            return jnp.fft.ifft(jnp.fft.fft(a) * jnp.fft.fft(b)).real

        def unbind(s, a):
            return jnp.fft.ifft(jnp.fft.fft(s) * jnp.conj(jnp.fft.fft(a))).real
        query = unit_projection(jnp.einsum('bsd,ed->bse', x, Wq) + bq)
        keys = unit_projection(jnp.einsum('bsd,ed->bse', x, Wk) + bk)
        values = unit_projection(jnp.einsum('bsd,ed->bse', x, Wv) + bv)
        x_k = bind(keys, values)
        s = jnp.cumsum(x_k, axis=1)
        out = unbind(s, query)
        return out

    def _L0_ffn_ref(x, gate_w, gate_b, w1, b1, w3, b3, w2, b2, sw1, sb1, sw3, sb3, sw2, sb2):
        import jax, jax.numpy as jnp
        import numpy as np
        ALPHA = 1.702
        LIMIT = 7.0
        TOPK = 2
        D, I, E = (256, 512, 8)
        B, S = (2, 512)

        def swiglu(x):
            g = x[..., ::2]
            l = x[..., 1::2]
            g = jnp.minimum(g, LIMIT)
            l = jnp.clip(l, -LIMIT, LIMIT)
            return g * jax.nn.sigmoid(ALPHA * g) * (l + 1.0)
        b, s, d = x.shape
        xt = x.reshape(-1, d)
        scores = jax.nn.softmax(xt @ gate_w.T, axis=-1)
        biased = scores + gate_b
        _, idx = jax.lax.top_k(biased, TOPK)
        weights = jnp.take_along_axis(scores, idx, axis=-1)
        comb = (weights[..., None] * jax.nn.one_hot(idx, E, dtype=xt.dtype)).sum(1)

        def body(acc, p):
            ew1, eb1, ew3, eb3, ew2, eb2, ce = p
            h = swiglu((xt @ ew1 + eb1) * (xt @ ew3 + eb3))
            return (acc + ce[:, None] * (h @ ew2 + eb2), None)
        routed, _ = jax.lax.scan(body, jnp.zeros_like(xt), (w1, b1, w3, b3, w2, b2, comb.T))
        shared = swiglu((xt @ sw1 + sb1) * (xt @ sw3 + sb3)) @ sw2 + sb2
        return (routed + shared).reshape(b, s, d)

    def _L1_attn_ref(x, ln1_g, ln1_b, ln2_g, ln2_b, time_decay, time_first, time_mix_k, time_mix_v, time_mix_r, att_Wk, att_Wv, att_Wr, att_Wo, cm_k, cm_r, ffn_Wk, ffn_Wr, ffn_Wv):
        import jax, jax.numpy as jnp
        import numpy as np
        B, T, C = (8, 512, 256)
        NL, LID = (12, 1)
        H = 4 * C

        def _ln(x, g, b):
            m = x.mean(-1, keepdims=True)
            v = ((x - m) ** 2).mean(-1, keepdims=True)
            return (x - m) * jax.lax.rsqrt(v + 1e-05) * g + b

        def _shift(x):
            return jnp.pad(x, ((0, 0), (1, 0), (0, 0)))[:, :-1]

        def _wkv(time_decay, time_first, k, v):
            w = -jnp.exp(time_decay)
            kt = jnp.moveaxis(k, 1, 0)
            vt = jnp.moveaxis(v, 1, 0)
            Bb, Cc = (k.shape[0], k.shape[2])
            init = (jnp.zeros((Bb, Cc), k.dtype), jnp.zeros((Bb, Cc), k.dtype), jnp.full((Bb, Cc), -1e+38, k.dtype))

            def step(carry, kv_t):
                aa, bb, pp = carry
                kk, vv = kv_t
                ww = time_first + kk
                p = jnp.maximum(pp, ww)
                e1 = jnp.exp(pp - p)
                e2 = jnp.exp(ww - p)
                out = (e1 * aa + e2 * vv) / (e1 * bb + e2)
                ww2 = pp + w
                p2 = jnp.maximum(ww2, kk)
                e1b = jnp.exp(ww2 - p2)
                e2b = jnp.exp(kk - p2)
                return ((e1b * aa + e2b * vv, e1b * bb + e2b, p2), out)
            _, out = jax.lax.scan(step, init, (kt, vt))
            return jnp.moveaxis(out, 0, 1)
        xa = _ln(x, ln1_g, ln1_b)
        xx = _shift(xa)
        xk = xa * time_mix_k + xx * (1 - time_mix_k)
        xv = xa * time_mix_v + xx * (1 - time_mix_v)
        xr = xa * time_mix_r + xx * (1 - time_mix_r)
        k = jnp.einsum('btc,oc->bto', xk, att_Wk)
        v = jnp.einsum('btc,oc->bto', xv, att_Wv)
        r = jnp.einsum('btc,oc->bto', xr, att_Wr)
        rwkv = jax.nn.sigmoid(r) * _wkv(time_decay, time_first, k, v)
        x = x + jnp.einsum('bto,co->btc', rwkv, att_Wo)
        xc = _ln(x, ln2_g, ln2_b)
        xx2 = _shift(xc)
        xk2 = xc * cm_k + xx2 * (1 - cm_k)
        xr2 = xc * cm_r + xx2 * (1 - cm_r)
        kk = jnp.square(jax.nn.relu(jnp.einsum('btc,hc->bth', xk2, ffn_Wk)))
        kv = jnp.einsum('bth,ch->btc', kk, ffn_Wv)
        rkv = jax.nn.sigmoid(jnp.einsum('btc,oc->bto', xr2, ffn_Wr)) * kv
        return x + rkv

    def _L1_ffn_ref(x, w_up, w_down):
        import jax, jax.numpy as jnp
        import numpy as np
        EPS = 1e-08

        def _ternary_linear(x, w):
            alpha = jnp.mean(jnp.abs(w))
            w_t = jnp.sign(w) * (jnp.abs(w) > 0.5 * alpha).astype(w.dtype)
            w_q = w + jax.lax.stop_gradient(w_t - w)
            d = x.shape[-1]
            rms = jnp.sqrt(jnp.sum(x * x, axis=-1, keepdims=True)) / jnp.sqrt(jnp.asarray(d, x.dtype))
            x_norm = x / (rms + EPS)
            return jnp.einsum('bsd,fd->bsf', x_norm, w_q)
        h = jax.nn.gelu(_ternary_linear(x, w_up), approximate=False)
        return _ternary_linear(h, w_down)
    h = _L0_tok_ref(x, L0_tok_Wa, L0_tok_ba, L0_tok_Wd1, L0_tok_bd1, L0_tok_Wd2, L0_tok_bd2, L0_tok_Wd3, L0_tok_bd3)
    h = h + _L0_attn_ref(_layernorm(h, axis=-1), L0_attn_Wq, L0_attn_bq, L0_attn_Wk, L0_attn_bk, L0_attn_Wv, L0_attn_bv)
    h = h + _L0_ffn_ref(_layernorm(h, axis=-1), L0_ffn_gate_w, L0_ffn_gate_b, L0_ffn_w1, L0_ffn_b1, L0_ffn_w3, L0_ffn_b3, L0_ffn_w2, L0_ffn_b2, L0_ffn_sw1, L0_ffn_sb1, L0_ffn_sw3, L0_ffn_sb3, L0_ffn_sw2, L0_ffn_sb2)
    h = h + _L1_attn_ref(_layernorm(h, axis=-1), L1_attn_ln1_g, L1_attn_ln1_b, L1_attn_ln2_g, L1_attn_ln2_b, L1_attn_time_decay, L1_attn_time_first, L1_attn_time_mix_k, L1_attn_time_mix_v, L1_attn_time_mix_r, L1_attn_att_Wk, L1_attn_att_Wv, L1_attn_att_Wr, L1_attn_att_Wo, L1_attn_cm_k, L1_attn_cm_r, L1_attn_ffn_Wk, L1_attn_ffn_Wr, L1_attn_ffn_Wv)
    h = h + _L1_ffn_ref(_layernorm(h, axis=-1), L1_ffn_w_up, L1_ffn_w_down)
    return h

_drawn_inputs = setup_inputs


def setup_inputs(seed=0):
    import zlib

    import numpy as np

    out = dict(_drawn_inputs(seed))
    spreads = {'L0_tok_bd1': (0.0, 0.1),
     'L0_tok_bd2': (0.0, 0.1),
     'L0_tok_bd3': (0.0, 0.386),
     'L1_attn_ln1_g': (1.0, 0.6),
     'L1_attn_ln1_b': (0.0, 0.8),
     'L1_attn_ln2_g': (1.0, 0.6),
     'L1_attn_ln2_b': (0.0, 0.8)}
    factors = {'L0_ffn_gate_w': 7.994,
     'L0_ffn_gate_b': 8.0,
     'L0_ffn_w1': 8.0,
     'L0_ffn_b1': 8.0,
     'L0_ffn_w3': 8.0,
     'L0_ffn_b3': 8.0,
     'L0_ffn_w2': 8.0,
     'L0_ffn_b2': 8.0,
     'L0_ffn_sb1': 64.0,
     'L0_ffn_sb3': 64.0,
     'L0_ffn_sb2': 52.852,
     'L1_attn_time_decay': 6.281,
     'L1_attn_time_first': 8.0,
     'L1_attn_time_mix_k': 8.0,
     'L1_attn_time_mix_v': 8.0,
     'L1_attn_time_mix_r': 8.0,
     'L1_attn_att_Wk': 8.0,
     'L1_attn_att_Wv': 4.241,
     'L1_attn_att_Wr': 8.0,
     'L1_attn_att_Wo': 4.243,
     'L1_attn_cm_k': 6.847,
     'L1_attn_cm_r': 8.0,
     'L1_attn_ffn_Wk': 4.107,
     'L1_attn_ffn_Wr': 8.0,
     'L1_attn_ffn_Wv': 3.694,
     'L0_ffn_sw1': 5.356,
     'L0_ffn_sw3': 5.967,
     'L0_ffn_sw2': 5.36}
    for name, (base, spread) in spreads.items():
        noise = np.random.default_rng([zlib.crc32(name.encode()), seed]).standard_normal(out[name].shape)
        drawn = base * np.exp(spread * noise) if base else spread * noise
        out[name] = jnp.asarray(drawn.astype(out[name].dtype))
    for name, factor in factors.items():
        out[name] = (out[name] * factor).astype(out[name].dtype)
    return out
```

```python
from contextlib import ExitStack

import concourse.bass as bass
from concourse import mybir

F32 = mybir.dt.float32
F32R = mybir.dt.float32r
ALU = mybir.AluOpType
ACT = mybir.ActivationFunctionType
AX = mybir.AxisListType

P = 128
B, S, D = 16, 256, 256
KT = D // P
NT = B * S // P
BT = 4
NB = NT // BT
BLK = BT * P
BI = BLK // S
TI = S // P
XS = S + 2
LN_EPS = 1e-5
E, TOPK, I = 8, 2, 512


def ds(start, size):
    return bass.ds(start, size)


class Chip:

    def __init__(self, nc, ctx):
        self.nc, self.ctx = nc, ctx
        self.h = ctx.enter_context(nc.sbuf_tensor("h", [P, NT, D], F32))
        self.mv = ctx.enter_context(nc.sbuf_tensor("mean_var", [P, NT, 2], F32))
        self.ident = ctx.enter_context(nc.sbuf_tensor("ident", [P, P], F32))

    def x_block(self, part, kt, i):
        return part[:, kt, ds(BI * i, BI), 1:1 + S]

    def x_shifted(self, part, kt, i):
        return part[:, kt, ds(BI * i, BI), 0:S]


class TileStats:
    PER = 2 * BT + 3

    def __init__(self, name, sb, sem):
        self.stats = sb(name + "_parts", [P, BT, 6])
        self.mean_var = sb(name + "_mean_var", [P, BT, 2])
        self.tick = sb(name + "_tick", [P, 2])
        self.done = sem(name + "_done")

    def block(self, dve, rows, mv, i):
        base = self.PER * i
        dve.wait_ge(self.done, base)
        dve.memset(self.tick[:, 0:1], 0.0).then_inc(self.done, 1)
        for t in range(BT):
            dve.bn_stats(self.stats[:, t], rows[:, ds(BT * i + t, 1)]).then_inc(self.done, 1)
        dve.wait_ge(self.done, base + BT + 1)
        dve.memset(self.tick[:, 1:2], 0.0).then_inc(self.done, 1)
        for t in range(BT):
            dve.bn_aggr(self.mean_var[:, t], self.stats[:, t]).then_inc(self.done, 1)
        dve.wait_ge(self.done, base + 2 * BT + 2)
        dve.tensor_scalar(mv[:, ds(BT * i, BT)], self.mean_var[:], 1.0, None, ALU.mult).then_inc(self.done, 1)

    def finish(self, dve):
        dve.wait_ge(self.done, self.PER * NB)


def split_matmuls(pe, out, weights, moving, first=True, last=True):
    n = len(weights)
    for k in range(n):
        (w_hi, w_lo), (m_hi, m_lo) = weights[k], moving[k]
        pe.matmul(out, w_hi, m_hi, start=(first and k == 0), stop=False)
        pe.matmul(out, w_hi, m_lo, start=False, stop=False)
        mm = pe.matmul(out, w_lo, m_hi, start=False, stop=(last and k == n - 1))
    return mm


def stage_semaphores(nc, ctx):
    taken = []
    ctx.callback(nc.all_engine_barrier)
    ctx.callback(lambda: nc.clear_and_free_semaphores(taken))

    def sem(name):
        taken.append(nc.alloc_semaphore(name))
        return taken[-1]

    return sem


def wavelet_stage(chip, x, wd, wa, bias, h_rows, consts):
    nc = chip.nc
    NQ = 4
    ROWS, COLS = [4, 2, 1], [128, 64, 32]
    NW = 10
    with ExitStack() as ctx:
        def sb(name, shape, dt=F32):
            return ctx.enter_context(nc.sbuf_tensor(name, shape, dt))

        sem = stage_semaphores(nc, ctx)

        img = chip.h[:].rearrange("p (q r) c -> p q r c", q=NQ)
        lo_row = sb("lo_row", [P, 4, 256])
        hi_row = sb("hi_row", [P, 4, 256])
        avg = [sb(f"avg{n}", [P, NQ, ROWS[n], COLS[n]]) for n in range(3)]
        det = [sb(f"det{n}", [P, NQ, 3, ROWS[n] * COLS[n]]) for n in range(3)]
        w_det = [sb(f"w_det{n}", [P, 3, 3 * ROWS[n] * COLS[n]]) for n in range(3)]
        w_avg = sb("w_avg", [P, COLS[2]])
        prod = sb("prod", [P, 2, 3 * ROWS[0] * COLS[0]])
        parts = sb("parts", [P, NQ, NW])
        group = sb("group", [P, P])
        scale_in = sb("scale_in", [P, NW])
        scale_out = sb("scale_out", [P, NW])
        biases = sb("biases", [P, NW])
        logits = sb("logits", [P, NQ, NW])
        top = sb("top", [P, NQ, 3])
        wts = sb("wts", [P, NQ, NW])
        neg = sb("neg", [P, NQ, NW])
        tmp = sb("tmp", [P, 512])
        up = [sb(f"up{n}", [P, ROWS[n] * 2, COLS[n] * 2]) for n in range(3)]
        sums = ctx.enter_context(nc.psum_tensor("sums", [P, NQ * NW], F32))

        stats = TileStats("wave_stats", sb, sem)
        s_img = [sem(f"img_loaded{q}") for q in range(NQ)]
        s_const = sem("wavelet_consts_loaded")
        s_dve = sem("wavelet_dve")
        s_parts = sem("parts_ready")
        s_sums = sem("sums_ready")
        s_logit = sem("logits_ready")
        s_exp = sem("exp_ready")
        s_row = sem("rows_ready")
        s_store = [sem(f"rows_stored{q}") for q in range(NQ)]
        s_h = [sem(f"h_loaded{q}") for q in range(NQ)]
        n_const = 0

        with nc.Block() as block:
            @block.sync
            def _(sp):
                nonlocal n_const
                for q in range(NQ):
                    sp.dma_start(img[:, q], x[ds(q * P, P), :].rearrange("p (r c) -> p r c", r=8)).then_inc(s_img[q], 16)
                for n in range(3):
                    for b in range(4):
                        sp.dma_start(w_det[n][32 * b:32 * b + 32, :, :], wd[n].rearrange("g (j s) -> g j s", j=3)).then_inc(s_const, 16)
                for b in range(4):
                    sp.dma_start(w_avg[32 * b:32 * b + 32, :], wa).then_inc(s_const, 16)
                sp.dma_start(biases[:, :], bias.partition_broadcast(P)).then_inc(s_const, 16)
                sp.dma_start(scale_in[:, :], consts["scale_in"]).then_inc(s_const, 16)
                sp.dma_start(scale_out[:, :], consts["scale_out"]).then_inc(s_const, 16)
                sp.dma_start(group[:, :], consts["group"]).then_inc(s_const, 16)
                sp.dma_start(chip.ident[:, :], consts["ident"]).then_inc(s_const, 16)
                n_const = 16 * (12 + 4 + 5)
                for q in range(NQ):
                    sp.wait_ge(s_row, q + 1)
                    sp.dma_start(h_rows[ds(q * 4 * S, 4 * S), :].rearrange("(p r) c -> p r c", r=8), img[:, q]).then_inc(s_store[q], 16)
                for q in range(NQ):
                    sp.wait_ge(s_store[q], 16)
                    t = q * 4 * TI
                    sp.dma_start(chip.h[:, t:t + 4 * TI, :],
                                 h_rows[ds(q * 4 * S, 4 * S), :].rearrange("(t p) c -> p t c", p=P)).then_inc(s_h[q], 16)

            @block.tensor
            def _(pe):
                pe.wait_ge(s_const, n_const)
                pe.wait_ge(s_parts, 1)
                pe.matmul(sums[:, :], group[:, :], parts[:].rearrange("p q w -> p (q w)"), start=True, stop=True).then_inc(s_sums, 1)

            @block.scalar
            def _(act):
                act.wait_ge(s_logit, 1)
                act.activation(wts[:, :, 0:9], logits[:, :, 0:9], ACT.Exp).then_inc(s_exp, 1)
                act.activation(wts[:, :, 9:10], logits[:, :, 9:10], ACT.Sigmoid).then_inc(s_exp, 1)

            @block.vector
            def _(dve):
                done = 0

                def step(ins):
                    nonlocal done
                    done += 1
                    ins.then_inc(s_dve, 1)

                def settled():
                    dve.wait_ge(s_dve, done)

                step(dve.memset(parts[:], 0.0))
                for q in range(NQ):
                    dve.wait_ge(s_img[q], 16)
                    for n in range(3):
                        src = img[:, q] if n == 0 else avg[n - 1][:, q]
                        R, C = ROWS[n], COLS[n]
                        rows = src.rearrange("p (r two) c -> p r two c", two=2)
                        lo_r, hi_r = lo_row[:, 0:R, 0:2 * C], hi_row[:, 0:R, 0:2 * C]
                        if n:
                            settled()
                        step(dve.tensor_tensor(lo_r, rows[:, :, 0], rows[:, :, 1], ALU.add))
                        step(dve.tensor_tensor(hi_r, rows[:, :, 0], rows[:, :, 1], ALU.subtract))
                        settled()
                        lo_c = lo_r.rearrange("p r (c two) -> p r c two", two=2)
                        hi_c = hi_r.rearrange("p r (c two) -> p r c two", two=2)
                        d = det[n][:, q].rearrange("p s (r c) -> p s r c", r=R)
                        step(dve.tensor_tensor(avg[n][:, q], lo_c[:, :, :, 0], lo_c[:, :, :, 1], ALU.add))
                        step(dve.tensor_tensor(d[:, 0], hi_c[:, :, :, 0], hi_c[:, :, :, 1], ALU.add))
                        step(dve.tensor_tensor(d[:, 1], lo_c[:, :, :, 0], lo_c[:, :, :, 1], ALU.subtract))
                        step(dve.tensor_tensor(d[:, 2], hi_c[:, :, :, 0], hi_c[:, :, :, 1], ALU.subtract))
                    settled()
                dve.wait_ge(s_const, n_const)
                k = 0
                for q in range(NQ):
                    for n in range(3):
                        for j in range(3):
                            m = 3 * ROWS[n] * COLS[n]
                            if k >= 2:
                                dve.wait_ge(s_dve, done - 1)
                            step(dve.tensor_tensor_reduce(prod[:, k % 2, 0:m], det[n][:, q].rearrange("p s c -> p (s c)"), w_det[n][:, j], 1.0, 0.0,
                                                          ALU.mult, ALU.add, parts[:, q, 3 * n + j:3 * n + j + 1]))
                            k += 1
                    dve.wait_ge(s_dve, done - 1)
                    step(dve.tensor_tensor_reduce(prod[:, k % 2, 0:COLS[2]], avg[2][:, q, 0], w_avg[:, :], 1.0, 0.0,
                                                  ALU.mult, ALU.add, parts[:, q, 9:10]))
                    k += 1
                settled()
                dve.engine_nop().then_inc(s_parts, 1)
                dve.wait_ge(s_sums, 1)

                def per_image(c):
                    return c[:, :].unsqueeze(1).to_broadcast([P, NQ, NW])

                step(dve.tensor_tensor(logits[:], sums[:, :].rearrange("p (q w) -> p q w", q=NQ), per_image(scale_in), ALU.mult))
                settled()
                step(dve.tensor_tensor(logits[:], logits[:], per_image(biases), ALU.add))
                settled()
                l3 = logits[:, :, 0:9].rearrange("p q (l j) -> p q l j", j=3)
                w3 = wts[:, :, 0:9].rearrange("p q (l j) -> p q l j", j=3)
                t3 = top[:].unsqueeze(3).to_broadcast([P, NQ, 3, 3])
                step(dve.tensor_reduce(top[:], l3, AX.X, ALU.max))
                settled()
                step(dve.tensor_tensor(l3, l3, t3, ALU.subtract))
                settled()
                dve.engine_nop().then_inc(s_logit, 1)
                dve.wait_ge(s_exp, 2)
                step(dve.tensor_reduce(top[:], w3, AX.X, ALU.add))
                settled()
                step(dve.reciprocal(top[:], top[:]))
                settled()
                step(dve.tensor_tensor(w3, w3, t3, ALU.mult))
                settled()
                step(dve.tensor_tensor(wts[:], wts[:], per_image(scale_out), ALU.mult))
                settled()
                step(dve.tensor_scalar(neg[:], wts[:], -1.0, None, ALU.mult))
                for q in range(NQ):
                    for n in (2, 1, 0):
                        R, C = ROWS[n], COLS[n]
                        d = det[n][:, q].rearrange("p s (r c) -> p s r c", r=R)
                        w = wts[:, q, 3 * n:3 * n + 3]
                        settled()
                        if n == 2:
                            step(dve.tensor_scalar(avg[2][:, q], avg[2][:, q], wts[:, q, 9:10], None, ALU.mult))
                            coarse = avg[2][:, q]
                        else:
                            coarse = up[n + 1][:, :, :]
                        t = tmp[:, 0:R * C].rearrange("p (r c) -> p r c", r=R)
                        step(dve.tensor_scalar(t, d[:, 2], w[:, 2:3], None, ALU.mult))
                        settled()
                        s_c = lo_row[:, 0:R, 0:2 * C].rearrange("p r (c two) -> p r c two", two=2)
                        d_c = hi_row[:, 0:R, 0:2 * C].rearrange("p r (c two) -> p r c two", two=2)
                        for e, wv, op in ((0, wts, ALU.add), (1, neg, ALU.subtract)):
                            step(dve.scalar_tensor_tensor(out=s_c[:, :, :, e], in0=d[:, 1], scalar=wv[:, q, 3 * n + 1:3 * n + 2],
                                                          in1=coarse, op0=ALU.mult, op1=ALU.add))
                            step(dve.scalar_tensor_tensor(out=d_c[:, :, :, e], in0=d[:, 0], scalar=w[:, 0:1],
                                                          in1=t, op0=ALU.mult, op1=op))
                        settled()
                        out = (img[:, q] if n == 0 else up[n][:, :, :]).rearrange("p (r two) c -> p r two c", two=2)
                        s_r, d_r = lo_row[:, 0:R, 0:2 * C], hi_row[:, 0:R, 0:2 * C]
                        step(dve.tensor_tensor(out[:, :, 0], s_r, d_r, ALU.add))
                        step(dve.tensor_tensor(out[:, :, 1], s_r, d_r, ALU.subtract))
                    settled()
                    dve.engine_nop().then_inc(s_row, 1)
                step(dve.memset(chip.x_hi[:, :, :, 0:1].bitcast(F32), 0.0))
                step(dve.memset(chip.x_lo[:, :, :, 0:1].bitcast(F32), 0.0))
                with dve.Fori(0, NB, 1) as i:
                    for q in range(NQ):
                        dve.wait_ge(s_h[q], 16)
                    stats.block(dve, chip.h, chip.mv, i)
                stats.finish(dve)
                settled()


def attention_stage(chip, a):
    nc = chip.nc
    EPS = 1e-8
    NF = D + 2
    Q, K, V = 0, 1, 2
    ORDER = (K, V, Q)
    with ExitStack() as ctx:
        def sb(name, shape, dt=F32):
            return ctx.enter_context(nc.sbuf_tensor(name, shape, dt))

        def ps(name, shape):
            return ctx.enter_context(nc.psum_tensor(name, shape, F32))

        sem = stage_semaphores(nc, ctx)

        w_raw = sb("w_raw", [P, 3, KT, D])
        fourier = sb("fourier", [P, KT, NF])
        inv_raw = sb("inv_raw", [P, 2, D])
        inv_hi = sb("inv_hi", [P, 2, D], F32R)
        inv_lo = sb("inv_lo", [P, 2, D], F32R)
        b_raw = sb("b_raw", [P, KT, 4])
        alt_cols = sb("alt_cols", [P, P])
        alt_row = sb("alt_row", [P, D])
        tri = sb("tri", [P, P])
        ones = sb("ones", [P, P])
        wf_hi = sb("wf_hi", [P, KT, 3, D], F32R)
        wf_lo = sb("wf_lo", [P, KT, 3, D], F32R)
        w_nyq = sb("w_nyq", [P, KT, 4])
        b_f = sb("b_f", [P, 3, 4])
        rstd = sb("rstd", [P, NT])
        xn = sb("xn", [P, BT, D])
        x_full = sb("x_full", [P, KT, BLK])
        sq = sb("sq", [P, 3, 2, BLK])
        mag = sb("mag", [P, 3, BLK])
        unit = sb("unit", [P, 3, 2, BLK])
        m = sb("m", [P, 4, BLK])
        cum = sb("cum", [P, 2, BLK])
        o = sb("o", [P, 4, BLK])
        o_hi = sb("o_hi", [P, 2, BLK], F32R)
        o_lo = sb("o_lo", [P, 2, BLK], F32R)
        nyq = sb("nyq", [P, BT, 3])
        nyq_r = sb("nyq_r", [P, BT, 3])
        nyq_p = sb("nyq_p", [P, BI, TI])
        nyq_z = sb("nyq_z", [P, BT])
        p_t = ps("p_t", [P, BLK])
        p_j = [[ps(f"p_j{n}{r}", [P, BLK]) for r in range(2)] for n in range(2)]
        p_o = ps("p_o", [P, BT, D])
        p_n = ps("p_n", [P, 512])
        BANK = {K: 0, V: 1, Q: 0}

        stats = TileStats("attn_stats", sb, sem)
        s_ld = sem("attn_loaded")
        s_wf = sem("fourier_weights")
        s_we = sem("fourier_weights_kept")
        s_prep = sem("prep_dve")
        s_var = sem("variance_ready")
        s_std = sem("std_ready")
        s_ready = sem("rstd_ready")
        s_xn = sem("xn_ready")
        s_tr = sem("transposed")
        s_hi = sem("x_hi_ready")
        s_xf = sem("x_full_ready")
        s_lo = sem("x_lo_ready")
        s_pj = sem("projected")
        s_nq = sem("nyquist_projected")
        s_nc = sem("nyquist_chain")
        s_np = sem("nyquist_product")
        s_z = sem("nyquist_unbound")
        s_cum = sem("nyquist_summed")
        s_sq = sem("squares_ready")
        s_sum = sem("power_ready")
        s_mag = sem("magnitude_ready")
        s_r = sem("reciprocal_chain")
        s_u = sem("units_ready")
        s_m = sem("products_dve")
        s_mp = sem("products_pool")
        s_c = sem("running_sums")
        s_ot = sem("unbound_dve")
        s_op = sem("unbound_pool")
        s_os = sem("unbound_ready")
        s_oh = sem("o_hi_ready")
        s_ol = sem("o_lo_ready")
        s_y = sem("y_ready")
        s_hz = sem("h_plus_nyquist")
        s_h = sem("h_updated")
        s_nu = sem("nyquist_units")

        with nc.Block() as block:
            @block.sync
            def _(sp):
                for dst, src in ((w_raw[:], a["w_qkv"].rearrange("(w k p) d -> p w k d", w=3, p=P)),
                                 (fourier[:], a["fourier"].rearrange("(k p) f -> p k f", p=P)),
                                 (inv_raw[:], a["inverse"].rearrange("(k p) d -> p k d", p=P)),
                                 (b_raw[:], a["b_qkv"].rearrange("(k p) w -> p k w", p=P)),
                                 (alt_cols[:], a["alt_cols"]), (alt_row[:], a["alt_row"]),
                                 (tri[:], a["tri"]), (ones[:], a["ones"])):
                    sp.dma_start(dst, src).then_inc(s_ld, 16)

            @block.tensor
            def _(pe):
                pe.wait_ge(s_ld, 16 * 8)
                for n in range(3 * KT):
                    w, mt = n // KT, n % KT
                    if n >= 4:
                        pe.wait_ge(s_we, n - 3)
                    out = p_j[n // 2 % 2][n % 2][:, 0:NF]
                    for k in range(KT):
                        mm = pe.matmul(out, w_raw[:, w, k, mt * P:(mt + 1) * P], fourier[:, k], start=(k == 0), stop=(k == KT - 1))
                    mm.then_inc(s_wf, 1)
                for part in range(3):
                    for k in range(KT):
                        lhs = alt_cols[:, :] if part == 2 else fourier[:, k, part * P:(part + 1) * P]
                        mm = pe.matmul(p_n[:, 4 * part:4 * part + 4], lhs, b_raw[:, k], start=(k == 0), stop=(k == KT - 1))
                mm.then_inc(s_wf, 1)

                def transposes(i):
                    pe.wait_ge(s_xn, BT * (i + 1))
                    for kt in range(KT):
                        pe.wait_ge(s_lo, KT * i + kt)
                        for t in range(BT):
                            mm = pe.transpose(p_t[:, t * P:(t + 1) * P], xn[:, t, kt * P:(kt + 1) * P], chip.ident[:, :])
                        mm.then_inc(s_tr, 1)

                def nyquist(i):
                    pe.wait_ge(s_xf, KT * (i + 1))
                    pe.wait_ge(s_z, i)
                    for t in range(BT):
                        for k in range(KT):
                            mm = pe.matmul(p_n[:, 4 * t:4 * t + 4], x_full[:, k, t * P:(t + 1) * P], w_nyq[:, k], start=(k == 0), stop=(k == KT - 1))
                    mm.then_inc(s_nq, 1)

                def back(i):
                    pe.wait_ge(s_lo, KT * (i + 1))
                    for n, w in enumerate(ORDER):
                        pe.wait_ge(s_u, 6 * i if n < 2 else 6 * i + 2)
                        for ri in range(2):
                            split_matmuls(pe, p_j[BANK[w]][ri][:, :],
                                          [(wf_hi[:, k, w, ri * P:(ri + 1) * P], wf_lo[:, k, w, ri * P:(ri + 1) * P]) for k in range(KT)],
                                          [(chip.x_block(chip.x_hi, k, i), chip.x_block(chip.x_lo, k, i)) for k in range(KT)]).then_inc(s_pj, 1)
                    pe.wait_ge(s_np, i + 1)
                    pe.matmul(p_n[:, 32:32 + BI], tri[:, :], nyq_p[:, :, 0], start=True, stop=True)
                    pe.matmul(p_n[:, 40:40 + BI], ones[:, :], nyq_p[:, :, 0], start=True, stop=False)
                    pe.matmul(p_n[:, 40:40 + BI], tri[:, :], nyq_p[:, :, 1], start=False, stop=True).then_inc(s_cum, 1)
                    pe.wait_ge(s_ol, 2 * (i + 1))
                    pe.wait_ge(s_h, BT * i)
                    for t in range(BT):
                        split_matmuls(pe, p_o[:, t], [(o_hi[:, r, t * P:(t + 1) * P], o_lo[:, r, t * P:(t + 1) * P]) for r in range(2)],
                                      [(inv_hi[:, r], inv_lo[:, r]) for r in range(2)]).then_inc(s_y, 1)

                pe.wait_ge(s_ready, 1)
                transposes(0)
                with pe.Fori(0, NB - 1, 1) as i:
                    nyquist(i)
                    transposes(i + 1)
                    back(i)
                nyquist(NB - 1)
                back(NB - 1)

            @block.scalar
            def _(act):
                act.wait_ge(s_var, 1)
                act.activation(rstd[:, :], rstd[:, :], ACT.Sqrt).then_inc(s_std, 1)

                def front(i):
                    for kt in range(KT):
                        act.wait_ge(s_tr, KT * i + kt + 1)
                        act.activation(chip.x_block(chip.x_hi, kt, i), p_t[:, :].rearrange("p (b s) -> p b s", b=BI), ACT.Copy).then_inc(s_hi, 1)
                        act.wait_ge(s_nq, i)
                        act.activation(x_full[:, kt], p_t[:, :], ACT.Copy).then_inc(s_xf, 1)

                def back(i):
                    def squares(n):
                        w = ORDER[n]
                        act.wait_ge(s_pj, 6 * i + 2 * n + 2)
                        for ri in range(2):
                            ins = act.activation(sq[:, w, ri], p_j[BANK[w]][ri][:, :], ACT.Square, bias=b_f[:, ri, w:w + 1])
                        ins.then_inc(s_sq, 1)

                    def root(n):
                        w = ORDER[n]
                        act.wait_ge(s_sum, 3 * i + n + 1)
                        act.activation(mag[:, w], mag[:, w], ACT.Sqrt).then_inc(s_mag, 1)

                    squares(0)
                    squares(1)
                    root(0)
                    root(1)
                    squares(2)
                    root(2)
                    for r in range(2):
                        act.wait_ge(s_os, 2 * i + r + 1)
                        act.wait_ge(s_y, BT * i)
                        act.activation(o_hi[:, r], o[:, 2 * r], ACT.Copy).then_inc(s_oh, 1)

                front(0)
                with act.Fori(0, NB - 1, 1) as i:
                    front(i + 1)
                    back(i)
                back(NB - 1)

            @block.gpsimd
            def _(pool):
                with pool.Fori(0, NB, 1) as i:
                    pool.wait_ge(s_u, 6 * i + 4)
                    pool.wait_ge(s_c, 4 * i)
                    pool.tensor_tensor(m[:, 1], unit[:, K, 1], unit[:, V, 1], ALU.mult).then_inc(s_mp, 1)
                    pool.tensor_tensor(m[:, 3], unit[:, K, 1], unit[:, V, 0], ALU.mult).then_inc(s_mp, 1)
                    pool.wait_ge(s_c, 4 * (i + 1))
                    pool.wait_ge(s_u, 6 * (i + 1))
                    pool.wait_ge(s_os, 2 * i)
                    pool.tensor_tensor(o[:, 3], cum[:, 0], unit[:, Q, 1], ALU.mult).then_inc(s_op, 1)

            @block.vector
            def _(dve):
                dve.tensor_scalar(rstd[:, :], chip.mv[:, :, 1], LN_EPS, None, ALU.add).then_inc(s_var, 1)
                dve.wait_ge(s_std, 1)
                dve.reciprocal(rstd[:, :], rstd[:, :]).then_inc(s_ready, 1)
                dve.wait_ge(s_ld, 16 * 8)
                dve.tensor_copy(inv_hi[:], inv_raw[:]).then_inc(s_prep, 1)
                dve.wait_ge(s_prep, 1)
                dve.tensor_tensor(inv_lo[:], inv_raw[:], inv_hi[:].bitcast(F32), ALU.subtract).then_inc(s_prep, 1)
                for n in range(3 * KT):
                    w, mt = n // KT, n % KT
                    src = p_j[n // 2 % 2][n % 2]
                    dve.wait_ge(s_wf, n + 1)
                    dve.tensor_copy(wf_hi[:, mt, w], src[:, 0:D]).then_inc(s_prep, 1)
                    dve.tensor_copy(w_nyq[:, mt, w:w + 1], src[:, D:D + 1]).then_inc(s_prep, 1)
                    dve.wait_ge(s_prep, 2 + 2 * n + 1)
                    dve.tensor_tensor(wf_lo[:, mt, w], src[:, 0:D], wf_hi[:, mt, w].bitcast(F32), ALU.subtract).then_inc(s_we, 1)
                dve.memset(w_nyq[:, :, 3:4], 0.0).then_inc(s_prep, 1)
                dve.wait_ge(s_wf, 3 * KT + 1)
                dve.tensor_copy(b_f[:], p_n[:, 0:12].rearrange("p (a w) -> p a w", a=3)).then_inc(s_prep, 1)
                dve.wait_ge(s_prep, 2 + 6 * KT + 2)

                def front(i):
                    dve.wait_ge(s_tr, KT * i)
                    for t in range(BT):
                        dve.tensor_scalar(xn[:, t:t + 1], chip.h[:, ds(BT * i + t, 1)], chip.mv[:, ds(BT * i + t, 1), 0], rstd[:, ds(BT * i + t, 1)],
                                          ALU.subtract, ALU.mult).then_inc(s_xn, 1)
                    for kt in range(KT):
                        dve.wait_ge(s_hi, KT * i + kt + 1)
                        dve.wait_ge(s_xf, KT * i + kt + 1)
                        dve.tensor_tensor(chip.x_block(chip.x_lo, kt, i), p_t[:, :].rearrange("p (b s) -> p b s", b=BI),
                                          chip.x_block(chip.x_hi, kt, i).bitcast(F32), ALU.subtract).then_inc(s_lo, 1)

                def back(i):
                    def power(n):
                        w = ORDER[n]
                        dve.wait_ge(s_sq, 3 * i + n + 1)
                        dve.tensor_tensor(mag[:, w], sq[:, w, 0], sq[:, w, 1], ALU.add).then_inc(s_sum, 1)

                    def units(n):
                        w = ORDER[n]
                        dve.wait_ge(s_mag, 3 * i + n + 1)
                        dve.tensor_scalar(mag[:, w], mag[:, w], EPS, None, ALU.add).then_inc(s_r, 1)
                        dve.wait_ge(s_r, 6 * i + 2 * n + 1)
                        dve.reciprocal(mag[:, w], mag[:, w]).then_inc(s_r, 1)
                        dve.wait_ge(s_r, 6 * i + 2 * n + 2)
                        if n == 2:
                            dve.wait_ge(s_op, i)
                        elif n == 0:
                            dve.wait_ge(s_mp, 2 * i)
                        for ri in range(2):
                            dve.scalar_tensor_tensor(out=unit[:, w, ri], in0=p_j[BANK[w]][ri][:, :], scalar=b_f[:, ri, w:w + 1],
                                                     in1=mag[:, w], op0=ALU.add, op1=ALU.mult).then_inc(s_u, 1)

                    power(0)
                    power(1)
                    units(0)
                    bias = b_f[:, 2, 0:3].unsqueeze(1).to_broadcast([P, BT, 3])
                    dve.wait_ge(s_nq, i + 1)
                    dve.tensor_tensor(nyq[:], p_n[:, 0:4 * BT].rearrange("p (t w) -> p t w", t=BT)[:, :, 0:3], bias, ALU.add).then_inc(s_nc, 1)
                    dve.wait_ge(s_nc, 5 * i + 1)
                    dve.tensor_scalar(nyq_r[:], nyq[:], -1.0, None, ALU.mult).then_inc(s_nc, 1)
                    dve.wait_ge(s_nc, 5 * i + 2)
                    dve.tensor_tensor(nyq_r[:], nyq_r[:], nyq[:], ALU.max).then_inc(s_nc, 1)
                    dve.wait_ge(s_nc, 5 * i + 3)
                    dve.tensor_scalar(nyq_r[:], nyq_r[:], EPS, None, ALU.add).then_inc(s_nc, 1)
                    dve.wait_ge(s_nc, 5 * i + 4)
                    dve.reciprocal(nyq_r[:], nyq_r[:]).then_inc(s_nc, 1)
                    dve.wait_ge(s_nc, 5 * i + 5)
                    dve.tensor_tensor(nyq[:], nyq[:], nyq_r[:], ALU.mult).then_inc(s_nu, 1)
                    dve.wait_ge(s_nu, i + 1)
                    dve.tensor_tensor(nyq_p[:], nyq[:, :, K].rearrange("p (b h) -> p b h", b=BI), nyq[:, :, V].rearrange("p (b h) -> p b h", b=BI),
                                      ALU.mult).then_inc(s_np, 1)
                    units(1)
                    power(2)
                    dve.wait_ge(s_u, 6 * i + 4)
                    dve.tensor_tensor(m[:, 0], unit[:, K, 0], unit[:, V, 0], ALU.mult).then_inc(s_m, 1)
                    dve.tensor_tensor(m[:, 2], unit[:, K, 0], unit[:, V, 1], ALU.mult).then_inc(s_m, 1)
                    units(2)
                    dve.wait_ge(s_cum, i + 1)
                    z = nyq_z[:, :].rearrange("p (b h) -> p h b", b=BI)
                    c = p_n[:, 32:48].rearrange("p (h b) -> p h b", h=2)[:, :, 0:BI]
                    dve.tensor_tensor(z, c, nyq[:, :, Q].rearrange("p (b h) -> p h b", b=BI), ALU.mult).then_inc(s_z, 1)
                    dve.wait_ge(s_m, 2 * (i + 1))
                    dve.wait_ge(s_mp, 2 * (i + 1))
                    for ri, op in ((0, ALU.subtract), (1, ALU.add)):
                        for b in range(BI):
                            dve.tensor_tensor_scan(cum[:, ri, b * S:(b + 1) * S], m[:, 2 * ri, b * S:(b + 1) * S], m[:, 2 * ri + 1, b * S:(b + 1) * S],
                                                   initial=0.0, op0=ALU.add, op1=op).then_inc(s_c, 1)
                    dve.wait_ge(s_c, 4 * (i + 1))
                    dve.wait_ge(s_u, 6 * (i + 1))
                    dve.wait_ge(s_oh, 2 * i)
                    dve.tensor_tensor(o[:, 0], cum[:, 0], unit[:, Q, 0], ALU.mult).then_inc(s_ot, 1)
                    dve.tensor_tensor(o[:, 1], cum[:, 1], unit[:, Q, 1], ALU.mult).then_inc(s_ot, 1)
                    dve.tensor_tensor(o[:, 2], cum[:, 1], unit[:, Q, 0], ALU.mult).then_inc(s_ot, 1)
                    dve.wait_ge(s_ot, 3 * i + 2)
                    dve.tensor_tensor(o[:, 0], o[:, 0], o[:, 1], ALU.add).then_inc(s_os, 1)
                    dve.wait_ge(s_ot, 3 * i + 3)
                    dve.wait_ge(s_op, i + 1)
                    dve.tensor_tensor(o[:, 2], o[:, 2], o[:, 3], ALU.subtract).then_inc(s_os, 1)
                    dve.wait_ge(s_y, BT * i)
                    for r in range(2):
                        dve.wait_ge(s_oh, 2 * i + r + 1)
                        dve.tensor_tensor(o_lo[:, r], o[:, 2 * r], o_hi[:, r].bitcast(F32), ALU.subtract).then_inc(s_ol, 1)
                    dve.wait_ge(s_z, i + 1)
                    for t in range(BT):
                        h = chip.h[:, ds(BT * i + t, 1)]
                        dve.scalar_tensor_tensor(out=h, in0=alt_row[:, :].unsqueeze(1), scalar=nyq_z[:, t:t + 1], in1=h, op0=ALU.mult, op1=ALU.add).then_inc(s_hz, 1)
                    for t in range(BT):
                        h = chip.h[:, ds(BT * i + t, 1)]
                        dve.wait_ge(s_hz, BT * i + t + 1)
                        dve.wait_ge(s_y, BT * i + t // 2 * 2 + 2)
                        dve.tensor_tensor(h, h, p_o[:, t:t + 1], ALU.add).then_inc(s_h, 1)
                    dve.wait_ge(s_h, BT * (i + 1))
                    stats.block(dve, chip.h, chip.mv, i)

                front(0)
                with dve.Fori(0, NB - 1, 1) as i:
                    front(i + 1)
                    back(i)
                back(NB - 1)
                stats.finish(dve)


def gate_stage(chip, a, comb):
    nc = chip.nc
    with ExitStack() as ctx:
        def sb(name, shape, dt=F32):
            return ctx.enter_context(nc.sbuf_tensor(name, shape, dt))

        def ps(name, shape):
            return ctx.enter_context(nc.psum_tensor(name, shape, F32))

        sem = stage_semaphores(nc, ctx)

        rstd = sb("rstd_g", [P, NT])
        xn = sb("xn_g", [P, BT, D])
        x_full = sb("x_full_g", [P, KT, BLK])
        w_gate = sb("w_gate", [P, KT, E])
        b_gate = sb("b_gate", [P, E])
        b_out = sb("b_out", [E + 1, D])
        before = sb("before", [P, E, E])
        score = sb("score", [P, NT, E])
        biased = sb("biased", [P, NT, E])
        red = sb("red", [P, NT])
        wins = sb("wins", [P, NT, E, E])
        ties = sb("ties", [P, NT, E, E])
        rank = sb("rank", [P, NT, E])
        comb_blk = sb("comb_blk", [P, BT, E + 1])
        comb_t = sb("comb_t", [E + 1, BLK])
        p_t = [ps(f"p_t_g{k}", [P, BLK]) for k in range(KT)]
        p_g = ps("p_g", [P, BT, E])
        p_c = ps("p_c", [P, BLK])
        p_b = ps("p_b", [P, BT, D])

        s_ld = sem("gate_loaded")
        s_var = sem("g_variance_ready")
        s_std = sem("g_std_ready")
        s_ready = sem("g_rstd_ready")
        s_xn = sem("g_xn_ready")
        s_tr = sem("g_transposed")
        s_hi = sem("g_x_hi_ready")
        s_xf = sem("g_x_full_ready")
        s_lo = sem("g_x_lo_ready")
        s_gt = sem("gate_projected")
        s_sc = sem("scores_kept")
        s_ch = sem("gate_chain")
        s_mx = sem("gate_max_taken")
        s_ex = sem("gate_exp")
        s_cb = sem("comb_ready")
        s_cc = sem("comb_block_ready")
        s_ct = sem("comb_transposed")
        s_ck = sem("comb_t_kept")
        s_bm = sem("biases_mixed")
        s_ba = sem("biases_added")

        with nc.Block() as block:
            @block.sync
            def _(sp):
                for dst, src in ((w_gate[:], a["gate_w"].rearrange("(k p) e -> p k e", p=P)),
                                 (b_gate[:], a["gate_b"].partition_broadcast(P)),
                                 (b_out[:], a["b_out"]), (before[:], a["before"].rearrange("p (e f) -> p e f", e=E))):
                    sp.dma_start(dst, src).then_inc(s_ld, 16)

            @block.tensor
            def _(pe):
                pe.wait_ge(s_ld, 64)
                pe.wait_ge(s_ready, 1)
                with pe.Fori(0, NB, 1) as i:
                    pe.wait_ge(s_xn, BT * (i + 1))
                    pe.wait_ge(s_lo, KT * i)
                    for kt in range(KT):
                        for t in range(BT):
                            mm = pe.transpose(p_t[kt][:, t * P:(t + 1) * P], xn[:, t, kt * P:(kt + 1) * P], chip.ident[:, :])
                        mm.then_inc(s_tr, 1)
                    pe.wait_ge(s_xf, KT * (i + 1))
                    pe.wait_ge(s_sc, i)
                    for t in range(BT):
                        for k in range(KT):
                            mm = pe.matmul(p_g[:, t], x_full[:, k, t * P:(t + 1) * P], w_gate[:, k], start=(k == 0), stop=(k == KT - 1))
                    mm.then_inc(s_gt, 1)
                pe.wait_ge(s_cb, 1)
                with pe.Fori(0, NB, 1) as i:
                    pe.wait_ge(s_cc, i + 1)
                    pe.wait_ge(s_ck, i)
                    for t in range(BT):
                        mm = pe.transpose(p_c[0:E + 1, t * P:(t + 1) * P], comb_blk[:, t], chip.ident[:, :])
                    mm.then_inc(s_ct, 1)
                    pe.wait_ge(s_ck, i + 1)
                    pe.wait_ge(s_ba, BT * i)
                    for t in range(BT):
                        pe.matmul(p_b[:, t], comb_t[:, t * P:(t + 1) * P], b_out[:, :], start=True, stop=True).then_inc(s_bm, 1)

            @block.scalar
            def _(act):
                act.wait_ge(s_var, 1)
                act.activation(rstd[:, :], rstd[:, :], ACT.Sqrt).then_inc(s_std, 1)
                with act.Fori(0, NB, 1) as i:
                    act.wait_ge(s_gt, i)
                    for kt in range(KT):
                        act.wait_ge(s_tr, KT * i + kt + 1)
                        act.activation(chip.x_block(chip.x_hi, kt, i), p_t[kt][:, :].rearrange("p (b s) -> p b s", b=BI), ACT.Copy).then_inc(s_hi, 1)
                        act.activation(x_full[:, kt], p_t[kt][:, :], ACT.Copy).then_inc(s_xf, 1)
                act.wait_ge(s_mx, 1)
                act.activation(score[:], score[:], ACT.Exp).then_inc(s_ex, 1)

            @block.vector
            def _(dve):
                dve.tensor_scalar(rstd[:, :], chip.mv[:, :, 1], LN_EPS, None, ALU.add).then_inc(s_var, 1)
                dve.wait_ge(s_std, 1)
                dve.reciprocal(rstd[:, :], rstd[:, :]).then_inc(s_ready, 1)
                dve.wait_ge(s_ready, 1)
                with dve.Fori(0, NB, 1) as i:
                    dve.wait_ge(s_tr, KT * i)
                    for t in range(BT):
                        dve.tensor_scalar(xn[:, t:t + 1], chip.h[:, ds(BT * i + t, 1)], chip.mv[:, ds(BT * i + t, 1), 0], rstd[:, ds(BT * i + t, 1)],
                                          ALU.subtract, ALU.mult).then_inc(s_xn, 1)
                    for kt in range(KT):
                        dve.wait_ge(s_xf, KT * i + kt + 1)
                        dve.tensor_tensor(chip.x_block(chip.x_lo, kt, i), p_t[kt][:, :].rearrange("p (b s) -> p b s", b=BI),
                                          chip.x_block(chip.x_hi, kt, i).bitcast(F32), ALU.subtract).then_inc(s_lo, 1)
                    dve.wait_ge(s_gt, i + 1)
                    dve.tensor_copy(score[:, ds(BT * i, BT)], p_g[:]).then_inc(s_sc, 1)
                n = 0

                def chain(ins):
                    nonlocal n
                    n += 1
                    ins.then_inc(s_ch, 1)
                    dve.wait_ge(s_ch, n)

                per_token = red[:, :].unsqueeze(2).to_broadcast([P, NT, E])
                dve.wait_ge(s_sc, NB)
                chain(dve.tensor_reduce(red[:, :], score[:], AX.X, ALU.max))
                dve.tensor_tensor(score[:], score[:], per_token, ALU.subtract).then_inc(s_mx, 1)
                dve.wait_ge(s_ex, 1)
                chain(dve.tensor_reduce(red[:, :], score[:], AX.X, ALU.add))
                chain(dve.reciprocal(red[:, :], red[:, :]))
                chain(dve.tensor_tensor(score[:], score[:], per_token, ALU.mult))
                dve.wait_ge(s_ld, 64)
                chain(dve.tensor_tensor(biased[:], score[:], b_gate[:, :].unsqueeze(1).to_broadcast([P, NT, E]), ALU.add))
                mine = biased[:].unsqueeze(3).to_broadcast([P, NT, E, E])
                theirs = biased[:].unsqueeze(2).to_broadcast([P, NT, E, E])
                chain(dve.tensor_tensor(wins[:], theirs, mine, ALU.is_gt))
                chain(dve.tensor_tensor(ties[:], theirs, mine, ALU.is_equal))
                chain(dve.tensor_tensor(ties[:], ties[:], before[:].unsqueeze(1).to_broadcast([P, NT, E, E]), ALU.mult))
                chain(dve.tensor_tensor(wins[:], wins[:], ties[:], ALU.add))
                chain(dve.tensor_reduce(rank[:], wins[:], AX.X, ALU.add))
                chain(dve.scalar_tensor_tensor(out=comb[:, 0:E].rearrange("p e t -> p t e"), in0=rank[:], scalar=TOPK - 0.5, in1=score[:],
                                               op0=ALU.is_lt, op1=ALU.mult))
                dve.memset(comb[:, E:E + 1], 1.0).then_inc(s_cb, 1)
                with dve.Fori(0, NB, 1) as i:
                    dve.wait_ge(s_cb, 1)
                    dve.wait_ge(s_ct, i)
                    dve.tensor_copy(comb_blk[:].rearrange("p t e -> p e t"), comb[:, :, ds(BT * i, BT)]).then_inc(s_cc, 1)
                    dve.wait_ge(s_ct, i + 1)
                    dve.wait_ge(s_bm, BT * i)
                    dve.tensor_copy(comb_t[:, :], p_c[0:E + 1, :]).then_inc(s_ck, 1)
                    for t in range(BT):
                        h = chip.h[:, ds(BT * i + t, 1)]
                        dve.wait_ge(s_bm, BT * i + t // 2 * 2 + 2)
                        dve.tensor_tensor(h, h, p_b[:, t:t + 1], ALU.add).then_inc(s_ba, 1)


def experts_stage(chip, a, comb):
    nc = chip.nc
    ALPHA, LIMIT = 1.702, 7.0
    NE = E + 1
    NJ = I // P
    G1, G3, L1, L3 = range(4)
    with ExitStack() as ctx:
        def sb(name, shape, dt=F32):
            return ctx.enter_context(nc.sbuf_tensor(name, shape, dt))

        def ps(name, shape):
            return ctx.enter_context(nc.psum_tensor(name, shape, F32))

        sem = stage_semaphores(nc, ctx)

        w13_raw = sb("w13_raw", [P, KT, NJ, 4 * P])
        w13_hi = sb("w13_hi", [P, KT, NJ, 4 * P], F32R)
        w13_lo = sb("w13_lo", [P, KT, NJ, 4 * P], F32R)
        w2_raw = sb("w2_raw", [P, NJ, D])
        w2_hi = sb("w2_hi", [P, NJ, D], F32R)
        w2_lo = sb("w2_lo", [P, NJ, D], F32R)
        b13 = sb("b13", [P, NE * NJ * 4])
        lin = sb("lin", [P, 2, BLK])
        g = sb("g", [P, BLK])
        li = sb("li", [P, BLK])
        sg = sb("sg", [P, BLK])
        gl = sb("gl", [P, BLK])
        hid = sb("hid", [P, 2, BLK])
        hid_hi = sb("hid_hi", [P, NJ, BLK], F32R)
        hid_lo = sb("hid_lo", [P, NJ, BLK], F32R)
        p1 = [ps(f"p1_{h}", [P, BLK]) for h in range(2)]
        p3 = [ps(f"p3_{h}", [P, BLK]) for h in range(2)]
        p_y = ps("p_y", [P, BT, D])

        s_b = sem("b13_loaded")
        s_r13 = sem("w13_loaded")
        s_r2 = sem("w2_loaded")
        s_h13 = sem("w13_hi_ready")
        s_c13 = sem("w13_split")
        s_h2 = sem("w2_hi_ready")
        s_c2 = sem("w2_split")
        s_ph = sem("halves_projected")
        s_lin = sem("lin_ready")
        s_st = sem("halves_multiplied")
        s_gm = sem("g_limited")
        s_lc = sem("l_limited")
        s_gl = sem("gl_ready")
        s_sg = sem("sigmoid_ready")
        s_hm = sem("hidden_ready")
        s_hh = sem("hidden_hi_ready")
        s_hl = sem("hidden_lo_ready")
        s_w2 = [sem(f"w2_applied{j}") for j in range(NJ)]
        s_out = sem("expert_added")

        def b_col(e, j, q):
            return b13[:, ds(e * (NJ * 4) + (4 * j + q), 1)]

        with nc.Block() as block:
            @block.sync
            def _(sp):
                sp.dma_start(b13[:, :], a["b13"]).then_inc(s_b, 16)
                with sp.Fori(0, NE, 1) as e:
                    sp.wait_ge(s_c13, NJ * e)
                    sp.dma_start(w13_raw[:], a["w13"][ds(e * P, P), :].rearrange("p (k j c) -> p k j c", k=KT, j=NJ)).then_inc(s_r13, 16)
                    sp.wait_ge(s_c2, e)
                    sp.dma_start(w2_raw[:], a["w2"][ds(e * P, P), :].rearrange("p (j d) -> p j d", j=NJ)).then_inc(s_r2, 16)

            @block.tensor
            def _(pe):
                def half(e, n, i, j, hf, first=False):
                    pe.wait_ge(s_c13, NJ * e + j + 1)
                    if not first:
                        pe.wait_ge(s_st, 2 * NJ * n + 2 * j + hf - 1)
                    for q, out in ((2 * hf, p1[hf]), (2 * hf + 1, p3[hf])):
                        mm = split_matmuls(pe, out[:, :], [(w13_hi[:, k, j, q * P:(q + 1) * P], w13_lo[:, k, j, q * P:(q + 1) * P]) for k in range(KT)],
                                           [(chip.x_block(chip.x_hi, k, i), chip.x_block(chip.x_lo, k, i)) for k in range(KT)])
                    mm.then_inc(s_ph, 1)

                def down(e, n, j):
                    pe.wait_ge(s_hl, NJ * n + j + 1)
                    if j == 0:
                        pe.wait_ge(s_out, BT * n)
                        pe.wait_ge(s_c2, e + 1)
                    for t in range(BT):
                        hi, lo = hid_hi[:, j, t * P:(t + 1) * P], hid_lo[:, j, t * P:(t + 1) * P]
                        pe.matmul(p_y[:, t], hi, w2_hi[:, j], start=(j == 0 and t % 2 == 0), stop=False, skip_group_check=True)
                        pe.matmul(p_y[:, t], hi, w2_lo[:, j], start=False, stop=False, skip_group_check=True)
                        mm = pe.matmul(p_y[:, t], lo, w2_hi[:, j], start=False, stop=(j == NJ - 1), skip_group_check=True)
                    mm.then_inc(s_w2[j], 1)

                def block_of(e, i, e_next, i_next):
                    n = e * NB + i
                    for j in range(1, NJ):
                        half(e, n, i, j, 0)
                        half(e, n, i, j, 1)
                        down(e, n, j - 1)
                    if e_next is not None:
                        half(e_next, n + 1, i_next, 0, 0)
                    down(e, n, NJ - 1)
                    if e_next is not None:
                        half(e_next, n + 1, i_next, 0, 1)

                half(0, 0, 0, 0, 0, first=True)
                half(0, 0, 0, 0, 1, first=True)
                with pe.Fori(0, NE - 1, 1) as e:
                    with pe.Fori(0, NB - 1, 1) as i:
                        block_of(e, i, e, i + 1)
                    block_of(e, NB - 1, e + 1, 0)
                with pe.Fori(0, NB - 1, 1) as i:
                    block_of(NE - 1, i, NE - 1, i + 1)
                block_of(NE - 1, NB - 1, None, None)

            def each_block(eng, body, split13, split2):
                for j in range(NJ):
                    split13(0, j)
                split2(0)
                with eng.Fori(0, NE - 1, 1) as e:
                    with eng.Fori(0, NB - 1, 1) as i:
                        body(e, i, None)
                    body(e, NB - 1, lambda j: split13(e + 1, j))
                    split2(e + 1)
                with eng.Fori(0, NB, 1) as i:
                    body(NE - 1, i, None)

            @block.scalar
            def _(act):
                act.wait_ge(s_b, 16)

                def split13(e, j):
                    act.wait_ge(s_r13, 16 * (e + 1))
                    act.activation(w13_hi[:, :, j], w13_raw[:, :, j], ACT.Copy).then_inc(s_h13, 1)

                def split2(e):
                    act.wait_ge(s_r2, 16 * (e + 1))
                    act.wait_ge(s_w2[NJ - 1], NB * e)
                    act.activation(w2_hi[:], w2_raw[:], ACT.Copy).then_inc(s_h2, 1)

                def body(e, i, after):
                    n = e * NB + i
                    for j in range(NJ):
                        for hf in range(2):
                            act.wait_ge(s_ph, 2 * NJ * n + 2 * j + hf + 1)
                            act.wait_ge(s_st, 2 * NJ * n if j == 0 else 2 * NJ * n + 2 * j + hf - 1)
                            act.activation(lin[:, hf], p1[hf][:, :], ACT.Identity, bias=b_col(e, j, 2 * hf)).then_inc(s_lin, 1)
                            if hf == 0:
                                act.wait_ge(s_gm, NJ * n + j + 1)
                                act.wait_ge(s_hm, NJ * n + j)
                                act.activation(sg[:, :], g[:, :], ACT.Sigmoid, scale=ALPHA).then_inc(s_sg, 1)
                        act.wait_ge(s_hm, NJ * n + j + 1)
                        act.wait_ge(s_w2[j], n)
                        act.activation(hid_hi[:, j], hid[:, j % 2], ACT.Copy).then_inc(s_hh, 1)
                        if after:
                            after(j)

                each_block(act, body, split13, split2)

            @block.vector
            def _(dve):
                dve.wait_ge(s_b, 16)

                def split13(e, j):
                    dve.wait_ge(s_h13, NJ * e + j + 1)
                    dve.tensor_tensor(w13_lo[:, :, j], w13_raw[:, :, j], w13_hi[:, :, j].bitcast(F32), ALU.subtract).then_inc(s_c13, 1)

                def split2(e):
                    dve.wait_ge(s_h2, e + 1)
                    dve.tensor_tensor(w2_lo[:], w2_raw[:], w2_hi[:].bitcast(F32), ALU.subtract).then_inc(s_c2, 1)

                def body(e, i, after):
                    n = e * NB + i

                    def low(j):
                        dve.wait_ge(s_hh, NJ * n + j + 1)
                        dve.tensor_tensor(hid_lo[:, j], hid[:, j % 2], hid_hi[:, j].bitcast(F32), ALU.subtract).then_inc(s_hl, 1)

                    for j in range(NJ):
                        k = NJ * n + j
                        dve.wait_ge(s_lin, 2 * k + 1)
                        dve.wait_ge(s_gl, k)
                        dve.scalar_tensor_tensor(out=g[:, :], in0=p3[0][:, :], scalar=b_col(e, j, G3), in1=lin[:, 0], op0=ALU.add, op1=ALU.mult).then_inc(s_st, 1)
                        dve.wait_ge(s_st, 2 * k + 1)
                        dve.tensor_scalar(g[:, :], g[:, :], LIMIT, None, ALU.min).then_inc(s_gm, 1)
                        if j:
                            low(j - 1)
                        dve.wait_ge(s_lin, 2 * k + 2)
                        dve.scalar_tensor_tensor(out=li[:, :], in0=p3[1][:, :], scalar=b_col(e, j, L3), in1=lin[:, 1], op0=ALU.add, op1=ALU.mult).then_inc(s_st, 1)
                        dve.wait_ge(s_st, 2 * k + 2)
                        dve.tensor_scalar(li[:, :], li[:, :], LIMIT, -LIMIT, ALU.min, ALU.max).then_inc(s_lc, 1)
                        dve.wait_ge(s_lc, k + 1)
                        dve.wait_ge(s_gm, k + 1)
                        dve.scalar_tensor_tensor(out=gl[:, :], in0=li[:, :], scalar=1.0, in1=g[:, :], op0=ALU.add, op1=ALU.mult).then_inc(s_gl, 1)
                        dve.wait_ge(s_gl, k + 1)
                        dve.wait_ge(s_sg, k + 1)
                        dve.tensor_tensor(hid[:, j % 2], gl[:, :], sg[:, :], ALU.mult).then_inc(s_hm, 1)
                        dve.wait_ge(s_hm, k + 1)
                        if after:
                            after(j)
                    low(NJ - 1)
                    dve.wait_ge(s_w2[NJ - 1], n + 1)
                    for t in range(BT):
                        h = chip.h[:, ds(BT * i + t, 1)]
                        dve.scalar_tensor_tensor(out=h, in0=p_y[:, t:t + 1], scalar=comb2[:, ds(e * NT + BT * i + t, 1)], in1=h,
                                                 op0=ALU.mult, op1=ALU.add).then_inc(s_out, 1)

                comb2 = comb[:].rearrange("p e t -> p (e t)")
                each_block(dve, body, split13, split2)


def ring_block(part, kt, i, first=1):
    return part[:, kt, ds(BI * (i % 2), BI), first:first + S]


def by_image(tile):
    return tile.rearrange("p (b s) -> p b s", b=BI)


def time_mix_stage(chip, a, x1, mv1):
    nc = chip.nc
    KV = 3
    NO_STATE = -1e38
    with ExitStack() as ctx:
        def sb(name, shape, dt=F32):
            return ctx.enter_context(nc.sbuf_tensor(name, shape, dt))

        def ps(name, shape):
            return ctx.enter_context(nc.psum_tensor(name, shape, F32))

        sem = stage_semaphores(nc, ctx)

        x_hi = sb("xa_hi", [P, KT, 2 * BI, XS], F32R)
        x_lo = sb("xa_lo", [P, KT, 2 * BI, XS], F32R)
        wm_hi = sb("wm_hi", [P, KT, 2, KV, D], F32R)
        wm_lo = sb("wm_lo", [P, KT, 2, KV, D], F32R)
        wo_hi = sb("wo_hi", [P, KT, D], F32R)
        wo_lo = sb("wo_lo", [P, KT, D], F32R)
        vecs = sb("vecs", [P, KT, 8])
        one_m = sb("one_m", [P, KT, KV])
        decay = sb("decay", [P, KT])
        rstd = sb("rstd1", [P, 2, NT])
        s_vec = sem("vectors_loaded")
        s_pd = sem("mix_prep_dve")
        s_pa = sem("mix_prep_act")
        s_bs = sem("variance_ready1")
        h_stats = TileStats("h_stats", sb, sem)
        x1_stats = TileStats("x1_stats", sb, sem)

        with nc.sbuf_tensor("wm_raw", [P, KT, KV, D], F32) as w_raw, nc.sbuf_tensor("wo_raw", [P, KT, D], F32) as wo_raw, \
                nc.sbuf_tensor("wm_f", [P, KT, 2, KV, D], F32) as w_f, nc.Block() as block:
            @block.sync
            def _(sp):
                for dst, src in ((vecs[:], a["mix_vecs"].rearrange("(k p) v -> p k v", p=P)),
                                 (w_raw[:], a["w_kvr"].rearrange("(k p) (v o) -> p k v o", p=P, v=KV)),
                                 (wo_raw[:], a["w_o"].rearrange("(k p) o -> p k o", p=P))):
                    sp.dma_start(dst, src).then_inc(s_vec, 16)

            @block.scalar
            def _(act):
                act.wait_ge(s_vec, 48)
                act.activation(decay[:, :], vecs[:, :, 5], ACT.Exp).then_inc(s_pa, 1)
                act.wait_ge(s_pd, 1)
                act.activation(rstd[:], rstd[:], ACT.Sqrt).then_inc(s_pa, 1)

            @block.vector
            def _(dve):
                with dve.Fori(0, NB, 1) as i:
                    h_stats.block(dve, chip.h, chip.mv, i)
                h_stats.finish(dve)
                dve.tensor_scalar(rstd[:, 0], chip.mv[:, :, 1], LN_EPS, None, ALU.add).then_inc(s_bs, 1)
                dve.wait_ge(s_bs, 1)
                dve.scalar_tensor_tensor(out=rstd[:, 1], in0=rstd[:, 0], scalar=LN_EPS, in1=chip.mv[:, :, 1], op0=ALU.mult, op1=ALU.add).then_inc(s_pd, 1)
                dve.wait_ge(s_pa, 2)
                dve.reciprocal(rstd[:], rstd[:]).then_inc(s_pd, 1)
                dve.tensor_scalar(decay[:, :], decay[:, :], -1.0, None, ALU.mult).then_inc(s_pd, 1)
                dve.tensor_scalar(one_m[:], vecs[:, :, 0:KV], -1.0, 1.0, ALU.mult, ALU.add).then_inc(s_pd, 1)
                dve.memset(x_hi[:, :, :, 0:1].bitcast(F32), 0.0).then_inc(s_pd, 1)
                dve.memset(x_lo[:, :, :, 0:1].bitcast(F32), 0.0).then_inc(s_pd, 1)
                dve.wait_ge(s_pd, 4)
                for k in range(KT):
                    for v in range(KV):
                        dve.tensor_scalar(w_f[:, k, 0, v], w_raw[:, k, v], vecs[:, k, v:v + 1], None, ALU.mult).then_inc(s_pd, 1)
                        dve.tensor_scalar(w_f[:, k, 1, v], w_raw[:, k, v], one_m[:, k, v:v + 1], None, ALU.mult).then_inc(s_pd, 1)
                dve.wait_ge(s_pd, 6 + 2 * KT * KV)
                dve.tensor_copy(wm_hi[:].rearrange("p k m v d -> p (k m v d)"), w_f[:].rearrange("p k m v d -> p (k m v d)")).then_inc(s_pd, 1)
                dve.tensor_copy(wo_hi[:], wo_raw[:]).then_inc(s_pd, 1)
                dve.wait_ge(s_pd, 6 + 2 * KT * KV + 2)
                dve.tensor_tensor(wm_lo[:].rearrange("p k m v d -> p (k m v d)"), w_f[:].rearrange("p k m v d -> p (k m v d)"),
                                  wm_hi[:].bitcast(F32).rearrange("p k m v d -> p (k m v d)"), ALU.subtract).then_inc(s_pd, 1)
                dve.tensor_tensor(wo_lo[:], wo_raw[:], wo_hi[:].bitcast(F32), ALU.subtract).then_inc(s_pd, 1)

        def pair(name, shape):
            return [sb(f"{name}{m}", shape) for m in range(KT)]

        xn = sb("xn1", [P, BT, D])
        xa = sb("xa", [P, KT, BLK])
        key, val, gate = pair("key", [P, BLK]), pair("val", [P, BLK]), pair("gate", [P, BLK])
        top = pair("top_state", [P, BI, S + 1])
        keep, add = pair("keep", [P, BLK]), pair("add", [P, BLK])
        mix = pair("mix", [P, 2, BLK])
        addv = pair("addv", [P, BLK])
        num_s, den_s = pair("num_state", [P, BI, S + 1]), pair("den_state", [P, BI, S + 1])
        rw_hi = sb("rw_hi", [P, KT, BLK], F32R)
        rw_lo = sb("rw_lo", [P, KT, BLK], F32R)
        p_t = [ps(f"p_t1_{k}", [P, BLK]) for k in range(KT)]
        p_j = [ps(f"p_j1_{k}", [P, BLK]) for k in range(4)]
        p_y = ps("p_y1", [P, BT, D])
        BANK = [0, 1, 2, 3, 0, 1]

        s_x1 = sem("x1_ready")
        s_xn = sem("xn1_ready")
        s_tr = sem("transposed1")
        s_xa = sem("xa_ready")
        s_xh = sem("xa_hi_ready")
        s_xl = sem("xa_lo_ready")
        s_pj = sem("kvr_projected")
        s_kv = sem("kvr_kept")
        s_top = sem("top_scanned")
        s_kd = sem("keep_exponent")
        s_ad = sem("add_exponent")
        s_md = sem("mix_exponents")
        s_ch = sem("mix_chain")
        s_ke = sem("keep_ready")
        s_ae = sem("add_ready")
        s_me = sem("mix_ready")
        s_av = sem("addv_ready")
        s_sc = sem("states_scanned")
        s_n2 = sem("token_part_ready")
        s_nd = sem("num_den_chain")
        s_dn = sem("den_ready")
        s_ln = sem("log_den_ready")
        s_y0 = sem("first_guess_ready")
        s_q = sem("gated_num_ready")
        s_nw = sem("newton_chain")
        s_rw = sem("rwkv_ready")
        s_rh = sem("rwkv_hi_ready")
        s_rl = sem("rwkv_lo_ready")
        s_y = sem("wo_applied")
        s_xu = sem("x1_updated")
        s_zero = sem("initial_states")

        with nc.Block() as block:
            @block.tensor
            def _(pe):
                def transposes(i):
                    pe.wait_ge(s_xn, BT * (i + 1))
                    pe.wait_ge(s_xa, KT * i)
                    for kt in range(KT):
                        for t in range(BT):
                            mm = pe.transpose(p_t[kt][:, t * P:(t + 1) * P], xn[:, t, kt * P:(kt + 1) * P], chip.ident[:, :])
                        mm.then_inc(s_tr, 1)

                def back(i):
                    pe.wait_ge(s_xl, KT * (i + 1))
                    for n in range(2 * KV):
                        m, v = n // KV, n % KV
                        pe.wait_ge(s_kv, 6 * i + max(n - 3, 0))
                        w, x = [], []
                        for k in range(KT):
                            for shifted in range(2):
                                w.append((wm_hi[:, k, shifted, v, m * P:(m + 1) * P], wm_lo[:, k, shifted, v, m * P:(m + 1) * P]))
                                x.append((ring_block(x_hi, k, i, 1 - shifted), ring_block(x_lo, k, i, 1 - shifted)))
                        split_matmuls(pe, p_j[BANK[n]][:, :], w, x).then_inc(s_pj, 1)
                    pe.wait_ge(s_rl, KT * (i + 1))
                    pe.wait_ge(s_xu, BT * i)
                    for t in range(BT):
                        split_matmuls(pe, p_y[:, t], [(rw_hi[:, k, t * P:(t + 1) * P], rw_lo[:, k, t * P:(t + 1) * P]) for k in range(KT)],
                                      [(wo_hi[:, k], wo_lo[:, k]) for k in range(KT)]).then_inc(s_y, 1)

                transposes(0)
                with pe.Fori(0, NB - 1, 1) as i:
                    transposes(i + 1)
                    back(i)
                back(NB - 1)

            @block.scalar
            def _(act):
                def front(i):
                    act.wait_ge(s_xl, KT * i)
                    for kt in range(KT):
                        act.wait_ge(s_tr, KT * i + kt + 1)
                        act.activation(xa[:, kt], p_t[kt][:, :], ACT.Identity, bias=vecs[:, kt, 4:5], scale=vecs[:, kt, 3:4]).then_inc(s_xa, 1)
                    for kt in range(KT):
                        act.wait_ge(s_xa, KT * i + kt + 1)
                        act.activation(ring_block(x_hi, kt, i), by_image(xa[:, kt]), ACT.Copy).then_inc(s_xh, 1)

                def back(i):
                    act.wait_ge(s_rw, KT * i)
                    for m in range(KT):
                        for v, dst in enumerate((key[m], val[m])):
                            act.wait_ge(s_pj, 6 * i + KV * m + v + 1)
                            act.activation(dst[:, :], p_j[BANK[KV * m + v]][:, :], ACT.Copy).then_inc(s_kv, 1)
                        act.wait_ge(s_pj, 6 * i + KV * m + 3)
                        act.activation(gate[m][:, :], p_j[BANK[KV * m + 2]][:, :], ACT.Sigmoid).then_inc(s_kv, 1)
                    for m in range(KT):
                        act.wait_ge(s_kd, KT * i + m + 1)
                        act.activation(keep[m][:, :], keep[m][:, :], ACT.Exp).then_inc(s_ke, 1)
                        act.wait_ge(s_ad, KT * i + m + 1)
                        act.activation(add[m][:, :], add[m][:, :], ACT.Exp).then_inc(s_ae, 1)
                        act.wait_ge(s_md, KT * i + m + 1)
                        act.activation(mix[m][:], mix[m][:], ACT.Exp).then_inc(s_me, 1)
                    for m in range(KT):
                        act.wait_ge(s_dn, KT * i + m + 1)
                        act.activation(key[m][:, :], mix[m][:, 0], ACT.Ln).then_inc(s_ln, 1)
                        act.wait_ge(s_ln, KT * i + m + 1)
                        act.activation(key[m][:, :], key[m][:, :], ACT.Exp, scale=-1.0).then_inc(s_y0, 1)
                    for m in range(KT):
                        act.wait_ge(s_rw, KT * i + m + 1)
                        act.wait_ge(s_y, BT * i)
                        act.activation(rw_hi[:, m], addv[m][:, :], ACT.Copy).then_inc(s_rh, 1)

                front(0)
                with act.Fori(0, NB - 1, 1) as i:
                    front(i + 1)
                    back(i)
                back(NB - 1)

            @block.gpsimd
            def _(pool):
                def front(i):
                    for kt in range(KT):
                        pool.wait_ge(s_xh, KT * i + kt + 1)
                        pool.tensor_tensor(ring_block(x_lo, kt, i), by_image(xa[:, kt]), ring_block(x_hi, kt, i).bitcast(F32), ALU.subtract).then_inc(s_xl, 1)

                def back(i):
                    for m in range(KT):
                        pool.wait_ge(s_top, BI * (KT * i + m + 1))
                        pool.tensor_tensor(by_image(add[m][:, :]), by_image(key[m][:, :]), top[m][:, :, 1:], ALU.subtract).then_inc(s_ad, 1)
                    for m in range(KT):
                        pool.wait_ge(s_ae, KT * i + m + 1)
                        pool.tensor_tensor(addv[m][:, :], add[m][:, :], val[m][:, :], ALU.mult).then_inc(s_av, 1)
                    for m in range(KT):
                        pool.wait_ge(s_me, KT * i + m + 1)
                        pool.wait_ge(s_av, KT * i + m + 1)
                        pool.tensor_tensor(val[m][:, :], mix[m][:, 1], val[m][:, :], ALU.mult).then_inc(s_n2, 1)
                    for m in range(KT):
                        pool.wait_ge(s_rh, KT * i + m + 1)
                        pool.tensor_tensor(rw_lo[:, m], addv[m][:, :], rw_hi[:, m].bitcast(F32), ALU.subtract).then_inc(s_rl, 1)

                front(0)
                with pool.Fori(0, NB - 1, 1) as i:
                    front(i + 1)
                    back(i)
                back(NB - 1)

            @block.vector
            def _(dve):
                for m in range(KT):
                    dve.memset(top[m][:, :, 0:1], NO_STATE).then_inc(s_zero, 1)
                    dve.memset(num_s[m][:, :, 0:1], 0.0).then_inc(s_zero, 1)
                    dve.memset(den_s[m][:, :, 0:1], 0.0).then_inc(s_zero, 1)
                dve.wait_ge(s_zero, 3 * KT)

                def front(i):
                    dve.wait_ge(s_tr, KT * i)
                    for t in range(BT):
                        tile = ds(BT * i + t, 1)
                        dve.tensor_scalar(xn[:, t:t + 1], chip.h[:, tile], chip.mv[:, tile, 0], rstd[:, 1, tile], ALU.subtract, ALU.mult).then_inc(s_xn, 1)
                    for t in range(BT):
                        tile = ds(BT * i + t, 1)
                        dve.tensor_scalar(x1[:, tile], chip.h[:, tile], chip.mv[:, tile, 0], rstd[:, 0, tile], ALU.subtract, ALU.mult).then_inc(s_x1, 1)

                def back(i):
                    two = KT * i
                    for m in range(KT):
                        u = vecs[:, m, 6:7]
                        before, after = top[m][:, :, 0:S], top[m][:, :, 1:]
                        dve.wait_ge(s_kv, 6 * i + KV * m + 1)
                        for b in range(BI):
                            dve.tensor_tensor_scan(top[m][:, b, 1:], decay[:, m:m + 1].to_broadcast([P, S]), key[m][:, b * S:(b + 1) * S],
                                                   initial=NO_STATE, op0=ALU.add, op1=ALU.max).then_inc(s_top, 1)
                        dve.wait_ge(s_top, BI * (two + m + 1))
                        dve.scalar_tensor_tensor(out=by_image(keep[m][:, :]), in0=before, scalar=decay[:, m:m + 1], in1=after,
                                                 op0=ALU.add, op1=ALU.subtract).then_inc(s_kd, 1)
                        dve.scalar_tensor_tensor(out=by_image(mix[m][:, 1]), in0=by_image(key[m][:, :]), scalar=u, in1=before,
                                                 op0=ALU.add, op1=ALU.subtract).then_inc(s_ch, 1)
                        dve.wait_ge(s_ch, 2 * (two + m) + 1)
                        dve.tensor_scalar(mix[m][:, 0], mix[m][:, 1], 0.0, -1.0, ALU.max, ALU.mult).then_inc(s_ch, 1)
                        dve.wait_ge(s_ch, 2 * (two + m) + 2)
                        dve.tensor_scalar(mix[m][:, 1], mix[m][:, 1], 0.0, None, ALU.min).then_inc(s_md, 1)
                    for m in range(KT):
                        dve.wait_ge(s_ke, two + m + 1)
                        dve.wait_ge(s_ae, two + m + 1)
                        for b in range(BI):
                            dve.tensor_tensor_scan(den_s[m][:, b, 1:], keep[m][:, b * S:(b + 1) * S], add[m][:, b * S:(b + 1) * S],
                                                   initial=0.0, op0=ALU.mult, op1=ALU.add).then_inc(s_sc, 1)
                        dve.wait_ge(s_av, two + m + 1)
                        for b in range(BI):
                            dve.tensor_tensor_scan(num_s[m][:, b, 1:], keep[m][:, b * S:(b + 1) * S], addv[m][:, b * S:(b + 1) * S],
                                                   initial=0.0, op0=ALU.mult, op1=ALU.add).then_inc(s_sc, 1)
                    for m in range(KT):
                        base = 3 * (two + m)
                        dve.wait_ge(s_me, two + m + 1)
                        dve.wait_ge(s_sc, 2 * BI * (two + m + 1))
                        dve.tensor_tensor(by_image(addv[m][:, :]), by_image(mix[m][:, 0]), num_s[m][:, :, 0:S], ALU.mult).then_inc(s_nd, 1)
                        dve.tensor_tensor(by_image(mix[m][:, 0]), by_image(mix[m][:, 0]), den_s[m][:, :, 0:S], ALU.mult).then_inc(s_nd, 1)
                        dve.wait_ge(s_nd, base + 2)
                        dve.tensor_tensor(mix[m][:, 0], mix[m][:, 0], mix[m][:, 1], ALU.add).then_inc(s_dn, 1)
                        dve.wait_ge(s_n2, two + m + 1)
                        dve.tensor_tensor(addv[m][:, :], addv[m][:, :], val[m][:, :], ALU.add).then_inc(s_nd, 1)
                        dve.wait_ge(s_nd, base + 3)
                        dve.wait_ge(s_kv, 6 * i + KV * m + 3)
                        dve.tensor_tensor(addv[m][:, :], addv[m][:, :], gate[m][:, :], ALU.mult).then_inc(s_q, 1)
                    for m in range(KT):
                        base = 2 * (two + m)
                        dve.wait_ge(s_y0, two + m + 1)
                        dve.wait_ge(s_dn, two + m + 1)
                        dve.tensor_tensor(mix[m][:, 0], mix[m][:, 0], key[m][:, :], ALU.mult).then_inc(s_nw, 1)
                        dve.wait_ge(s_nw, base + 1)
                        dve.scalar_tensor_tensor(out=mix[m][:, 0], in0=mix[m][:, 0], scalar=2.0, in1=key[m][:, :], op0=ALU.subtract, op1=ALU.mult).then_inc(s_nw, 1)
                        dve.wait_ge(s_nw, base + 2)
                        dve.wait_ge(s_q, two + m + 1)
                        dve.scalar_tensor_tensor(out=addv[m][:, :], in0=addv[m][:, :], scalar=-1.0, in1=mix[m][:, 0], op0=ALU.mult, op1=ALU.mult).then_inc(s_rw, 1)
                    for t in range(BT):
                        tile = ds(BT * i + t, 1)
                        dve.wait_ge(s_y, BT * i + t // 2 * 2 + 2)
                        dve.tensor_tensor(x1[:, tile], x1[:, tile], p_y[:, t:t + 1], ALU.add).then_inc(s_xu, 1)
                    dve.wait_ge(s_xu, BT * (i + 1))
                    x1_stats.block(dve, x1, mv1, i)

                front(0)
                with dve.Fori(0, NB - 1, 1) as i:
                    front(i + 1)
                    back(i)
                back(NB - 1)
                x1_stats.finish(dve)


def channel_mix_stage(chip, a, x1, mv1):
    nc = chip.nc
    NH = 4 * D // P
    with ExitStack() as ctx:
        def sb(name, shape, dt=F32):
            return ctx.enter_context(nc.sbuf_tensor(name, shape, dt))

        def ps(name, shape):
            return ctx.enter_context(nc.psum_tensor(name, shape, F32))

        sem = stage_semaphores(nc, ctx)

        wk_hi = sb("wk_hi", [P, KT, NH * P], F32R)
        wk_lo = sb("wk_lo", [P, KT, NH * P], F32R)
        wv_hi = sb("wv_hi", [P, NH, D], F32R)
        wv_lo = sb("wv_lo", [P, NH, D], F32R)
        wr_hi = sb("wr_hi", [P, KT, D], F32R)
        wr_lo = sb("wr_lo", [P, KT, D], F32R)
        vecs = sb("vecs2", [P, KT, 4])
        one_m = sb("one_m2", [P, KT, 2])
        rstd = sb("rstd2", [P, NT])
        xc = sb("xc", [P, KT, BI, XS])
        s_vec = sem("vectors2_loaded")
        s_pd = sem("cm_prep_dve")
        s_pa = sem("cm_prep_act")

        with nc.sbuf_tensor("wk_raw", [P, KT, NH * P], F32) as wk_raw, nc.sbuf_tensor("wv_raw", [P, NH, D], F32) as wv_raw, \
                nc.sbuf_tensor("wr_raw", [P, KT, D], F32) as wr_raw, nc.Block() as block:
            @block.sync
            def _(sp):
                for dst, src in ((vecs[:], a["cm_vecs"].rearrange("(k p) v -> p k v", p=P)),
                                 (wr_raw[:], a["w_r2"].rearrange("(k p) o -> p k o", p=P)),
                                 (wk_raw[:], a["w_k2"].rearrange("(k p) o -> p k o", p=P)),
                                 (wv_raw[:], a["w_v2"].rearrange("(k p) o -> p k o", p=P))):
                    sp.dma_start(dst, src).then_inc(s_vec, 16)

            @block.scalar
            def _(act):
                act.wait_ge(s_pd, 1)
                act.activation(rstd[:, :], rstd[:, :], ACT.Sqrt).then_inc(s_pa, 1)
                act.wait_ge(s_vec, 64)
                act.activation(wk_hi[:], wk_raw[:], ACT.Copy).then_inc(s_pa, 1)
                act.activation(wv_hi[:], wv_raw[:], ACT.Copy).then_inc(s_pa, 1)
                act.activation(wr_hi[:], wr_raw[:], ACT.Copy).then_inc(s_pa, 1)

            @block.vector
            def _(dve):
                dve.tensor_scalar(rstd[:, :], mv1[:, :, 1], LN_EPS, None, ALU.add).then_inc(s_pd, 1)
                dve.memset(xc[:, :, :, 0:1], 0.0).then_inc(s_pd, 1)
                dve.wait_ge(s_pa, 1)
                dve.reciprocal(rstd[:, :], rstd[:, :]).then_inc(s_pd, 1)
                dve.wait_ge(s_vec, 64)
                dve.tensor_scalar(one_m[:], vecs[:, :, 0:2], -1.0, 1.0, ALU.mult, ALU.add).then_inc(s_pd, 1)
                for n, (lo, raw, hi) in enumerate(((wk_lo, wk_raw, wk_hi), (wv_lo, wv_raw, wv_hi), (wr_lo, wr_raw, wr_hi))):
                    dve.wait_ge(s_pa, n + 2)
                    dve.tensor_tensor(lo[:], raw[:], hi[:].bitcast(F32), ALU.subtract).then_inc(s_pd, 1)

        xn = sb("xn2", [P, BT, D])
        old = sb("old", [P, 2, KT, BLK])
        mixed = sb("mixed", [P, 2, KT, BLK])
        xk_hi = sb("xk_hi", [P, KT, 2, BLK], F32R)
        xk_lo = sb("xk_lo", [P, KT, 2, BLK], F32R)
        xr_hi = sb("xr_hi", [P, KT, BLK], F32R)
        xr_lo = sb("xr_lo", [P, KT, BLK], F32R)
        pos = sb("pos", [P, 2, BLK])
        sqr = sb("sqr", [P, 2, BLK])
        hid_hi = sb("hid2_hi", [P, NH, BLK], F32R)
        hid_lo = sb("hid2_lo", [P, NH, BLK], F32R)
        gate = sb("gate2", [P, BT, D])
        stats = TileStats("h_stats2", sb, sem)
        p_t = [ps(f"p_t2_{k}", [P, BLK]) for k in range(KT)]
        p_u = [ps(f"p_u2_{k}", [P, BLK]) for k in range(2)]
        p_y = ps("p_y2", [P, BT, D])
        p_r = ps("p_r2", [P, BT, D])

        s_xn = sem("xn2_ready")
        s_tr = sem("transposed2")
        s_xc = sem("xc_ready")
        s_old = sem("old_ready")
        s_mx = sem("mixed_ready")
        s_xh = sem("x2_hi_ready")
        s_xl = sem("x2_lo_ready")
        s_r = sem("r_projected")
        s_g = sem("gate2_ready")
        s_up = sem("up_projected")
        s_po = sem("relu_ready")
        s_sq = sem("square_ready")
        s_hh = sem("hid2_hi_ready")
        s_hl = sem("hid2_lo_ready")
        s_dn = [sem(f"down_applied{j}") for j in range(NH)]
        s_hx = sem("h_plus_x1")
        s_ry = sem("gated")
        s_h = sem("h_updated2")

        with nc.Block() as block:
            @block.tensor
            def _(pe):
                def transposes(i):
                    pe.wait_ge(s_xn, BT * (i + 1))
                    pe.wait_ge(s_xc, KT * i)
                    for kt in range(KT):
                        for t in range(BT):
                            mm = pe.transpose(p_t[kt][:, t * P:(t + 1) * P], xn[:, t, kt * P:(kt + 1) * P], chip.ident[:, :])
                        mm.then_inc(s_tr, 1)

                def up(i, j):
                    if j >= 2:
                        pe.wait_ge(s_po, NH * i + j - 1)
                    else:
                        pe.wait_ge(s_po, NH * i)
                    split_matmuls(pe, p_u[j % 2][:, :], [(wk_hi[:, k, j * P:(j + 1) * P], wk_lo[:, k, j * P:(j + 1) * P]) for k in range(KT)],
                                  [(xk_hi[:, k, ds(i % 2, 1)], xk_lo[:, k, ds(i % 2, 1)]) for k in range(KT)]).then_inc(s_up, 1)

                def down(i, j):
                    pe.wait_ge(s_hl, NH * i + j + 1)
                    if j == 0:
                        pe.wait_ge(s_ry, BT * i)
                    for t in range(BT):
                        hi, lo = hid_hi[:, j, t * P:(t + 1) * P], hid_lo[:, j, t * P:(t + 1) * P]
                        pe.matmul(p_y[:, t], hi, wv_hi[:, j], start=(j == 0 and t % 2 == 0), stop=False, skip_group_check=True)
                        pe.matmul(p_y[:, t], hi, wv_lo[:, j], start=False, stop=False, skip_group_check=True)
                        mm = pe.matmul(p_y[:, t], lo, wv_hi[:, j], start=False, stop=(j == NH - 1), skip_group_check=True)
                    mm.then_inc(s_dn[j], 1)

                def back(i):
                    pe.wait_ge(s_xl, 2 * KT * (i + 1))
                    pe.wait_ge(s_g, 2 * i)
                    for t in range(BT):
                        mm = split_matmuls(pe, p_r[:, t], [(xr_hi[:, k, t * P:(t + 1) * P], xr_lo[:, k, t * P:(t + 1) * P]) for k in range(KT)],
                                           [(wr_hi[:, k], wr_lo[:, k]) for k in range(KT)])
                        if t % 2:
                            mm.then_inc(s_r, 1)
                    up(i, 0)
                    for j in range(1, NH):
                        up(i, j)
                        down(i, j - 1)
                    down(i, NH - 1)

                transposes(0)
                with pe.Fori(0, NB - 1, 1) as i:
                    transposes(i + 1)
                    back(i)
                back(NB - 1)

            @block.scalar
            def _(act):
                def front(i):
                    act.wait_ge(s_mx, 2 * KT * i)
                    for kt in range(KT):
                        act.wait_ge(s_tr, KT * i + kt + 1)
                        act.activation(xc[:, kt, :, 1:1 + S], by_image(p_t[kt][:, :]), ACT.Identity, bias=vecs[:, kt, 3:4], scale=vecs[:, kt, 2:3]).then_inc(s_xc, 1)
                    act.wait_ge(s_xc, KT * (i + 1))
                    for kt in range(KT):
                        for v in range(2):
                            act.activation(by_image(old[:, v, kt]), xc[:, kt, :, 0:S], ACT.Copy, scale=one_m[:, kt, v:v + 1]).then_inc(s_old, 1)
                    act.wait_ge(s_r, 2 * i)
                    for kt in range(KT):
                        for v in range(2):
                            act.wait_ge(s_mx, 2 * KT * i + 2 * kt + v + 1)
                            dst = xk_hi[:, kt, ds(i % 2, 1)] if v == 0 else xr_hi[:, kt:kt + 1]
                            act.activation(dst, mixed[:, v, kt:kt + 1], ACT.Copy).then_inc(s_xh, 1)

                def back(i):
                    act.wait_ge(s_h, BT * i)
                    for n in range(2):
                        act.wait_ge(s_r, 2 * i + n + 1)
                        act.activation(gate[:, 2 * n:2 * n + 2], p_r[:, 2 * n:2 * n + 2], ACT.Sigmoid).then_inc(s_g, 1)
                    for j in range(NH):
                        act.wait_ge(s_up, NH * i + j + 1)
                        act.wait_ge(s_sq, NH * i + max(j - 1, 0))
                        act.activation(pos[:, j % 2], p_u[j % 2][:, :], ACT.Relu).then_inc(s_po, 1)
                        if j:
                            act.wait_ge(s_sq, NH * i + j)
                            act.wait_ge(s_dn[j - 1], i)
                            act.activation(hid_hi[:, j - 1], sqr[:, (j - 1) % 2], ACT.Copy).then_inc(s_hh, 1)
                    act.wait_ge(s_sq, NH * i + NH)
                    act.wait_ge(s_dn[NH - 1], i)
                    act.activation(hid_hi[:, NH - 1], sqr[:, (NH - 1) % 2], ACT.Copy).then_inc(s_hh, 1)

                front(0)
                with act.Fori(0, NB - 1, 1) as i:
                    front(i + 1)
                    back(i)
                back(NB - 1)

            @block.gpsimd
            def _(pool):
                def front(i):
                    for kt in range(KT):
                        for v in range(2):
                            pool.wait_ge(s_xh, 2 * KT * i + 2 * kt + v + 1)
                            hi = xk_hi[:, kt, ds(i % 2, 1)] if v == 0 else xr_hi[:, kt:kt + 1]
                            dst = xk_lo[:, kt, ds(i % 2, 1)] if v == 0 else xr_lo[:, kt:kt + 1]
                            pool.tensor_tensor(dst, mixed[:, v, kt:kt + 1], hi.bitcast(F32), ALU.subtract).then_inc(s_xl, 1)
                    for t in range(BT):
                        tile = ds(BT * i + t, 1)
                        pool.tensor_tensor(chip.h[:, tile], chip.h[:, tile], x1[:, tile], ALU.add).then_inc(s_hx, 1)

                with pool.Fori(0, NB, 1) as i:
                    front(i)

            @block.vector
            def _(dve):
                def front(i):
                    dve.wait_ge(s_tr, KT * i)
                    for t in range(BT):
                        tile = ds(BT * i + t, 1)
                        dve.tensor_scalar(xn[:, t:t + 1], x1[:, tile], mv1[:, tile, 0], rstd[:, tile], ALU.subtract, ALU.mult).then_inc(s_xn, 1)
                    dve.wait_ge(s_xl, 2 * KT * i)
                    for kt in range(KT):
                        for v in range(2):
                            dve.wait_ge(s_old, 2 * KT * i + 2 * kt + v + 1)
                            dve.scalar_tensor_tensor(out=by_image(mixed[:, v, kt]), in0=xc[:, kt, :, 1:1 + S], scalar=vecs[:, kt, v:v + 1],
                                                     in1=by_image(old[:, v, kt]), op0=ALU.mult, op1=ALU.add).then_inc(s_mx, 1)

                def back(i):
                    def low(j):
                        dve.wait_ge(s_hh, NH * i + j + 1)
                        dve.tensor_tensor(hid_lo[:, j], sqr[:, j % 2], hid_hi[:, j].bitcast(F32), ALU.subtract).then_inc(s_hl, 1)

                    for j in range(NH):
                        dve.wait_ge(s_po, NH * i + j + 1)
                        dve.wait_ge(s_hl, NH * i + max(j - 1, 0))
                        dve.tensor_tensor(sqr[:, j % 2], pos[:, j % 2], pos[:, j % 2], ALU.mult).then_inc(s_sq, 1)
                        if j:
                            low(j - 1)
                    low(NH - 1)
                    dve.wait_ge(s_g, 2 * (i + 1))
                    dve.wait_ge(s_dn[NH - 1], i + 1)
                    for t in range(BT):
                        dve.tensor_tensor(gate[:, t], gate[:, t], p_y[:, t], ALU.mult).then_inc(s_ry, 1)
                    dve.wait_ge(s_hx, BT * (i + 1))
                    for t in range(BT):
                        h = chip.h[:, ds(BT * i + t, 1)]
                        dve.wait_ge(s_ry, BT * i + t + 1)
                        dve.tensor_tensor(h, h, gate[:, t:t + 1], ALU.add).then_inc(s_h, 1)
                    dve.wait_ge(s_h, BT * (i + 1))
                    stats.block(dve, chip.h, chip.mv, i)

                front(0)
                with dve.Fori(0, NB - 1, 1) as i:
                    front(i + 1)
                    back(i)
                back(NB - 1)
                stats.finish(dve)


def ternary_stage(chip, a, out):
    nc = chip.nc
    EPS = 1e-8
    NH = 4 * D // P
    with ExitStack() as ctx:
        def sb(name, shape, dt=F32):
            return ctx.enter_context(nc.sbuf_tensor(name, shape, dt))

        def ps(name, shape):
            return ctx.enter_context(nc.psum_tensor(name, shape, F32))

        sem = stage_semaphores(nc, ctx)

        x_hi = sb("xt_hi", [P, KT, 2 * BI, XS], F32R)
        x_lo = sb("xt_lo", [P, KT, 2 * BI, XS], F32R)
        w_up = sb("w_up", [P, KT, NH * P], F32R)
        w_down = sb("w_down", [P, NH, D], F32R)
        ones = sb("ones3", [P, P])
        root = sb("root", [P, 2, NT])
        scale = sb("scale3", [P, NT])
        s_ld = sem("ternary_loaded")
        s_pd = sem("ternary_prep_dve")
        s_tot = sem("weight_sums")
        s_pa = sem("ternary_prep_act")

        with nc.sbuf_tensor("up_raw", [P, KT, NH * P], F32) as up_raw, nc.sbuf_tensor("down_raw", [P, NH, D], F32) as down_raw, \
                nc.sbuf_tensor("above", [P, KT * NH * P], F32) as above, nc.sbuf_tensor("below", [P, KT * NH * P], F32) as below, \
                nc.sbuf_tensor("abs_sum", [P, 2], F32) as abs_sum, nc.sbuf_tensor("limits", [P, 2, 2], F32) as limits, \
                nc.psum_tensor("total", [P, 2], F32) as total, nc.Block() as block:
            @block.sync
            def _(sp):
                for dst, src in ((up_raw[:], a["w_up"].rearrange("(k p) o -> p k o", p=P)),
                                 (down_raw[:], a["w_down"].rearrange("(k p) o -> p k o", p=P)), (ones[:], a["ones"])):
                    sp.dma_start(dst, src).then_inc(s_ld, 16)

            @block.tensor
            def _(pe):
                pe.wait_ge(s_pd, 2)
                pe.matmul(total[:, :], ones[:, :], abs_sum[:, :], start=True, stop=True).then_inc(s_tot, 1)

            @block.scalar
            def _(act):
                act.wait_ge(s_pa, 1)
                act.activation(root[:], root[:], ACT.Sqrt).then_inc(s_pa, 1)

            @block.vector
            def _(dve):
                dve.wait_ge(s_ld, 48)
                for n, raw in enumerate((up_raw, down_raw)):
                    dve.tensor_reduce(abs_sum[:, n:n + 1], raw[:], AX.XY, ALU.add, apply_absolute_value=True).then_inc(s_pd, 1)
                dve.tensor_copy(root[:, 0], chip.mv[:, :, 1]).then_inc(s_pd, 1)
                dve.wait_ge(s_pd, 3)
                dve.tensor_scalar(root[:, 1], chip.mv[:, :, 1], LN_EPS, None, ALU.add).then_inc(s_pa, 1)
                dve.wait_ge(s_pa, 2)
                dve.scalar_tensor_tensor(out=scale[:, :], in0=root[:, 1], scalar=EPS, in1=root[:, 0], op0=ALU.mult, op1=ALU.add).then_inc(s_pd, 1)
                dve.wait_ge(s_pd, 4)
                dve.reciprocal(scale[:, :], scale[:, :]).then_inc(s_pd, 1)
                dve.wait_ge(s_tot, 1)
                half_mean = 0.5 / (D * NH * P)
                dve.tensor_scalar(limits[:, 0], total[:, :], half_mean, None, ALU.mult).then_inc(s_pd, 1)
                dve.tensor_scalar(limits[:, 1], total[:, :], -half_mean, None, ALU.mult).then_inc(s_pd, 1)
                n = 7
                for k, (raw, dst) in enumerate(((up_raw, w_up), (down_raw, w_down))):
                    flat = raw[:].rearrange("p a b -> p (a b)")
                    dve.wait_ge(s_pd, n)
                    dve.tensor_scalar(above[:, :], flat, limits[:, 0, k:k + 1], None, ALU.is_gt).then_inc(s_pd, 1)
                    dve.tensor_scalar(below[:, :], flat, limits[:, 1, k:k + 1], None, ALU.is_lt).then_inc(s_pd, 1)
                    dve.wait_ge(s_pd, n + 2)
                    dve.tensor_tensor(dst[:].rearrange("p a b -> p (a b)"), above[:, :], below[:, :], ALU.subtract).then_inc(s_pd, 1)
                    n += 3

        xn = sb("xn3", [P, BT, D])
        act_out = sb("act_out", [P, 2, BLK])
        squares = sb("squares", [P, 2, BLK])
        hid_hi = sb("hid3_hi", [P, NH, BLK], F32R)
        hid_lo = sb("hid3_lo", [P, NH, BLK], F32R)
        rms = sb("rms", [P, BT])
        p_t = [ps(f"p_t3_{k}", [P, BLK]) for k in range(KT)]
        p_u = [ps(f"p_u3_{k}", [P, BLK]) for k in range(2)]
        p_y = ps("p_y3", [P, BT, D])
        p_s = ps("p_s3", [P, BT])

        s_xn = sem("xn3_ready")
        s_tr = sem("transposed3")
        s_xh = sem("x3_hi_ready")
        s_xl = sem("x3_lo_ready")
        s_up = sem("up3_projected")
        s_ge = sem("gelu_ready")
        s_sq = sem("gelu_squared")
        s_hh = sem("hid3_hi_ready")
        s_hl = sem("hid3_lo_ready")
        s_ss = sem("squares_summed")
        s_dn = [sem(f"down3_applied{j}") for j in range(NH)]
        s_rt = sem("rms_ready")
        s_rc = sem("rms_chain")
        s_h = sem("h_updated3")
        s_o = sem("out_stored")

        with nc.Block() as block:
            @block.sync
            def _(sp):
                with sp.Fori(0, NB, 1) as i:
                    sp.wait_ge(s_h, BT * (i + 1))
                    sp.dma_start(out[ds(i * BLK, BLK), :].rearrange("(t p) c -> p t c", p=P), chip.h[:, ds(BT * i, BT)]).then_inc(s_o, 16)
                sp.wait_ge(s_o, 16 * NB)

            @block.tensor
            def _(pe):
                def transposes(i):
                    pe.wait_ge(s_xn, BT * (i + 1))
                    pe.wait_ge(s_xl, KT * i)
                    for kt in range(KT):
                        for t in range(BT):
                            mm = pe.transpose(p_t[kt][:, t * P:(t + 1) * P], xn[:, t, kt * P:(kt + 1) * P], chip.ident[:, :])
                        mm.then_inc(s_tr, 1)

                def up(i, j):
                    pe.wait_ge(s_ge, NH * i + max(j - 1, 0))
                    for k in range(KT):
                        w = w_up[:, k, j * P:(j + 1) * P]
                        pe.matmul(p_u[j % 2][:, :], w, ring_block(x_hi, k, i), start=(k == 0), stop=False)
                        mm = pe.matmul(p_u[j % 2][:, :], w, ring_block(x_lo, k, i), start=False, stop=(k == KT - 1))
                    mm.then_inc(s_up, 1)

                def down(i, j):
                    if j == 0:
                        pe.wait_ge(s_rt, i)
                        pe.wait_ge(s_rc, 3 * i)
                        pe.wait_ge(s_h, BT * i)
                    pe.wait_ge(s_sq, NH * i + j + 1)
                    for t in range(BT):
                        mm = pe.matmul(p_s[:, t:t + 1], squares[:, j % 2, t * P:(t + 1) * P], ones[:, 0:1],
                                       start=(j == 0 and t == 0), stop=(j == NH - 1), skip_group_check=True)
                    mm.then_inc(s_ss, 1)
                    pe.wait_ge(s_hl, NH * i + j + 1)
                    for t in range(BT):
                        pe.matmul(p_y[:, t], hid_hi[:, j, t * P:(t + 1) * P], w_down[:, j], start=(j == 0 and t % 2 == 0), stop=False, skip_group_check=True)
                        mm = pe.matmul(p_y[:, t], hid_lo[:, j, t * P:(t + 1) * P], w_down[:, j], start=False, stop=(j == NH - 1), skip_group_check=True)
                    mm.then_inc(s_dn[j], 1)

                def back(i):
                    pe.wait_ge(s_xl, KT * (i + 1))
                    up(i, 0)
                    for j in range(1, NH):
                        up(i, j)
                        down(i, j - 1)
                    down(i, NH - 1)

                transposes(0)
                with pe.Fori(0, NB - 1, 1) as i:
                    transposes(i + 1)
                    back(i)
                back(NB - 1)

            @block.scalar
            def _(act):
                def front(i):
                    for kt in range(KT):
                        act.wait_ge(s_tr, KT * i + kt + 1)
                        act.activation(ring_block(x_hi, kt, i), by_image(p_t[kt][:, :]), ACT.Copy).then_inc(s_xh, 1)

                def back(i):
                    def high(j):
                        act.wait_ge(s_ge, NH * i + j + 1)
                        act.wait_ge(s_dn[j], i)
                        act.activation(hid_hi[:, j], act_out[:, j % 2], ACT.Copy).then_inc(s_hh, 1)

                    for j in range(NH):
                        act.wait_ge(s_up, NH * i + j + 1)
                        act.wait_ge(s_hl, NH * i + max(j - 1, 0))
                        act.wait_ge(s_sq, NH * i + max(j - 1, 0))
                        act.activation(act_out[:, j % 2], p_u[j % 2][:, :], ACT.Gelu).then_inc(s_ge, 1)
                        high(j)
                    act.wait_ge(s_ss, NH * (i + 1))
                    act.wait_ge(s_h, BT * i)
                    act.activation(rms[:, :], p_s[:, :], ACT.Sqrt, scale=1.0 / (NH * P)).then_inc(s_rt, 1)

                front(0)
                with act.Fori(0, NB - 1, 1) as i:
                    front(i + 1)
                    back(i)
                back(NB - 1)

            @block.gpsimd
            def _(pool):
                with pool.Fori(0, NB, 1) as i:
                    for j in range(NH):
                        pool.wait_ge(s_ge, NH * i + j + 1)
                        pool.wait_ge(s_ss, NH * i + max(j - 1, 0))
                        pool.tensor_tensor(squares[:, j % 2], act_out[:, j % 2], act_out[:, j % 2], ALU.mult).then_inc(s_sq, 1)

            @block.vector
            def _(dve):
                def front(i):
                    dve.wait_ge(s_tr, KT * i)
                    for t in range(BT):
                        tile = ds(BT * i + t, 1)
                        dve.tensor_scalar(xn[:, t:t + 1], chip.h[:, tile], chip.mv[:, tile, 0], scale[:, tile], ALU.subtract, ALU.mult).then_inc(s_xn, 1)
                    for kt in range(KT):
                        dve.wait_ge(s_xh, KT * i + kt + 1)
                        dve.tensor_tensor(ring_block(x_lo, kt, i), by_image(p_t[kt][:, :]), ring_block(x_hi, kt, i).bitcast(F32), ALU.subtract).then_inc(s_xl, 1)

                def back(i):
                    for j in range(NH):
                        dve.wait_ge(s_hh, NH * i + j + 1)
                        dve.tensor_tensor(hid_lo[:, j], act_out[:, j % 2], hid_hi[:, j].bitcast(F32), ALU.subtract).then_inc(s_hl, 1)
                    dve.wait_ge(s_rt, i + 1)
                    dve.tensor_scalar(rms[:, :], rms[:, :], EPS, None, ALU.add).then_inc(s_rc, 1)
                    dve.wait_ge(s_rc, 3 * i + 1)
                    dve.reciprocal(rms[:, :], rms[:, :]).then_inc(s_rc, 1)
                    dve.wait_ge(s_rc, 3 * i + 2)
                    dve.wait_ge(s_dn[NH - 1], i + 1)
                    for t in range(BT):
                        h = chip.h[:, ds(BT * i + t, 1)]
                        dve.scalar_tensor_tensor(out=h, in0=p_y[:, t:t + 1], scalar=rms[:, t:t + 1], in1=h, op0=ALU.mult, op1=ALU.add).then_inc(s_h, 1)
                    dve.engine_nop().then_inc(s_rc, 1)

                front(0)
                with dve.Fori(0, NB - 1, 1) as i:
                    front(i + 1)
                    back(i)
                back(NB - 1)


def build_program(nc, a, out, scratch, stop=9, start=0):
    with ExitStack() as ctx:
        chip = Chip(nc, ctx)
        with nc.sbuf_tensor("x_hi", [P, KT, B, XS], F32R) as chip.x_hi, nc.sbuf_tensor("x_lo", [P, KT, B, XS], F32R) as chip.x_lo:
            wavelet_stage(chip, a["x"], [a["wd_fine"], a["wd_mid"], a["wd_coarse"]], a["wa"], a["wave_bias"], scratch["h_rows"], a)
            if stop > 0:
                attention_stage(chip, a)
            if stop > 1:
                with nc.sbuf_tensor("comb", [P, E + 1, NT], F32) as comb:
                    gate_stage(chip, a, comb)
                    experts_stage(chip, a, comb)
        if stop > 2:
            with nc.sbuf_tensor("x1", [P, NT, D], F32) as x1, nc.sbuf_tensor("mv1", [P, NT, 2], F32) as mv1:
                time_mix_stage(chip, a, x1, mv1)
                channel_mix_stage(chip, a, x1, mv1)
        if stop <= 3:
            return store_h(chip, out)
        ternary_stage(chip, a, out)


def store_h(chip, out):
    nc = chip.nc
    with nc.semaphore("out_stored") as s_out, nc.Block() as block:
        @block.sync
        def _(sp):
            sp.dma_start(out.rearrange("(t p) c -> p t c", p=P), chip.h[:]).then_inc(s_out, 16)
            sp.wait_ge(s_out, 16)


def layout(inputs):
    import numpy as np

    f = {k: np.asarray(v) for k, v in inputs.items()}
    a = {"x": f["x"].reshape(B * S // 8, 8 * 256)}
    for name, w, rows, cols in (("wd_fine", f["L0_tok_Wd3"], 4, 128), ("wd_mid", f["L0_tok_Wd2"], 2, 64), ("wd_coarse", f["L0_tok_Wd1"], 1, 32)):
        a[name] = w.reshape(3, 32, rows, cols, 3).transpose(1, 4, 0, 2, 3).reshape(32, -1)
    a["wa"] = f["L0_tok_Wa"].reshape(32, 32)
    a["wave_bias"] = np.concatenate([f["L0_tok_bd3"], f["L0_tok_bd2"], f["L0_tok_bd1"], f["L0_tok_ba"]])
    level = np.array([1, 1, 1, 2, 2, 2, 3, 3, 3, 3])
    a["scale_in"] = np.broadcast_to(0.5 ** level, (P, 10)).astype(np.float32)
    a["scale_out"] = np.broadcast_to(0.25 ** level, (P, 10)).astype(np.float32)
    a["group"] = np.kron(np.eye(4), np.ones((32, 32))).astype(np.float32)
    a["ident"] = np.eye(P, dtype=np.float32)
    a["w_qkv"] = np.concatenate([f["L0_attn_Wq"], f["L0_attn_Wk"], f["L0_attn_Wv"]])
    a["b_qkv"] = np.stack([f["L0_attn_bq"], f["L0_attn_bk"], f["L0_attn_bv"], np.zeros(D, np.float32)], axis=1)
    e, n = np.arange(D)[:, None], np.arange(P)[None, :]
    turn = 2 * np.pi * (e * n % D) / D
    sign = np.where(np.arange(D) % 2, -1.0, 1.0)
    a["fourier"] = np.concatenate([np.cos(turn), -np.sin(turn), sign[:, None], np.zeros((D, 1))], axis=1).astype(np.float32)
    twice = np.where(np.arange(P) == 0, 1.0, 2.0)[:, None] / D
    a["inverse"] = np.concatenate([twice * np.cos(turn).T, -twice * np.sin(turn).T]).astype(np.float32)
    a["alt_cols"] = np.broadcast_to(sign[:P, None], (P, P)).astype(np.float32)
    a["alt_row"] = np.broadcast_to(sign[None, :] / D, (P, D)).astype(np.float32)
    a["tri"] = np.triu(np.ones((P, P), np.float32))
    a["ones"] = np.ones((P, P), np.float32)
    a["gate_w"] = f["L0_ffn_gate_w"].T
    a["gate_b"] = f["L0_ffn_gate_b"]
    a["b_out"] = np.concatenate([f["L0_ffn_b2"], f["L0_ffn_sb2"][None]])
    a["before"] = np.broadcast_to(np.tril(np.ones((E, E), np.float32), -1).reshape(1, -1), (P, E * E))
    w1 = np.concatenate([f["L0_ffn_w1"], f["L0_ffn_sw1"][None]]).reshape(E + 1, KT, P, I // P, P, 2)
    w3 = np.concatenate([f["L0_ffn_w3"], f["L0_ffn_sw3"][None]]).reshape(E + 1, KT, P, I // P, P, 2)
    a["w13"] = np.stack([w1, w3], axis=-1).transpose(0, 2, 1, 3, 5, 6, 4).reshape((E + 1) * P, -1)
    b1 = np.concatenate([f["L0_ffn_b1"], f["L0_ffn_sb1"][None]]).reshape(E + 1, I // P, P, 2)
    b3 = np.concatenate([f["L0_ffn_b3"], f["L0_ffn_sb3"][None]]).reshape(E + 1, I // P, P, 2)
    a["b13"] = np.stack([b1, b3], axis=-1).transpose(2, 0, 1, 3, 4).reshape(P, -1)
    w2 = np.concatenate([f["L0_ffn_w2"], f["L0_ffn_sw2"][None]]).reshape(E + 1, I // P, P, D)
    a["w2"] = w2.transpose(0, 2, 1, 3).reshape((E + 1) * P, -1)
    g = {k[8:]: v for k, v in f.items() if k.startswith("L1_attn_")}
    zero = np.zeros(D, np.float32)
    a["mix_vecs"] = np.stack([g["time_mix_k"], g["time_mix_v"], g["time_mix_r"], g["ln1_g"], g["ln1_b"], g["time_decay"], g["time_first"], zero], axis=1)
    a["w_kvr"] = np.concatenate([g["att_Wk"].T, g["att_Wv"].T, g["att_Wr"].T], axis=1)
    a["w_o"] = g["att_Wo"].T
    a["cm_vecs"] = np.stack([g["cm_k"], g["cm_r"], g["ln2_g"], g["ln2_b"]], axis=1)
    a["w_r2"] = g["ffn_Wr"].T
    a["w_k2"] = g["ffn_Wk"].T
    a["w_v2"] = g["ffn_Wv"].T
    a["w_up"] = f["L1_ffn_w_up"].T
    a["w_down"] = f["L1_ffn_w_down"].T
    return {k: np.ascontiguousarray(v) for k, v in a.items()}


def kernel(stop=9, runner=None, **inputs):
    import numpy as np
    import concourse.bacc as bacc
    from concourse.bass_utils import run_bass_kernel_spmd

    arrays = layout(inputs)
    nc = bacc.Bacc("TRN2", target_bir_lowering=False, num_devices=1)
    args = {k: nc.dram_tensor(f"in_{k}", v.shape, mybir.dt.from_np(v.dtype), kind="ExternalInput").ap() for k, v in arrays.items()}
    out = nc.dram_tensor("out_h", (B * S, D), F32, kind="ExternalOutput").ap()
    scratch = {"h_rows": nc.dram_tensor("h_rows", (B * S, D), F32, kind="Internal").ap()}
    build_program(nc, args, out, scratch, stop)
    feed = {f"in_{k}": v for k, v in arrays.items()}
    if runner:
        return runner(nc, feed, ["out_h"])
    r = run_bass_kernel_spmd(nc, [feed], core_ids=[0])
    return r.results[0]["out_h"].reshape(B, S, D)
```

```python
from contextlib import ExitStack

import concourse.bass as bass
from concourse import mybir

F32 = mybir.dt.float32
F32R = mybir.dt.float32r
ALU = mybir.AluOpType
ACT = mybir.ActivationFunctionType
AX = mybir.AxisListType

P = 128
B, S, D = 16, 256, 256
KT = D // P
NT = B * S // P
BT = 4
NB = NT // BT
BLK = BT * P
BI = BLK // S
TI = S // P
XS = S + 2
LN_EPS = 1e-5
E, TOPK, I = 8, 2, 512
NJ = I // P
NRB = TOPK * NT // BT + E
SWIGLU_ALPHA, SWIGLU_LIMIT = 1.702, 7.0
U32, I32 = mybir.dt.uint32, mybir.dt.int32


def ds(start, size):
    return bass.ds(start, size)


class Chip:

    def __init__(self, nc, ctx):
        self.nc, self.ctx = nc, ctx
        self.h = ctx.enter_context(nc.sbuf_tensor("h", [P, NT, D], F32))
        self.mv = ctx.enter_context(nc.sbuf_tensor("mean_var", [P, NT, 2], F32))
        self.ident = ctx.enter_context(nc.sbuf_tensor("ident", [P, P], F32))

    def x_block(self, part, kt, i):
        return part[:, kt, ds(BI * i, BI), 1:1 + S]

    def x_shifted(self, part, kt, i):
        return part[:, kt, ds(BI * i, BI), 0:S]


class TileStats:
    PER = 2 * BT + 3

    def __init__(self, name, sb, sem):
        self.stats = sb(name + "_parts", [P, BT, 6])
        self.mean_var = sb(name + "_mean_var", [P, BT, 2])
        self.tick = sb(name + "_tick", [P, 2])
        self.done = sem(name + "_done")

    def block(self, dve, rows, mv, i):
        base = self.PER * i
        dve.wait_ge(self.done, base)
        dve.memset(self.tick[:, 0:1], 0.0).then_inc(self.done, 1)
        for t in range(BT):
            dve.bn_stats(self.stats[:, t], rows[:, ds(BT * i + t, 1)]).then_inc(self.done, 1)
        dve.wait_ge(self.done, base + BT + 1)
        dve.memset(self.tick[:, 1:2], 0.0).then_inc(self.done, 1)
        for t in range(BT):
            dve.bn_aggr(self.mean_var[:, t], self.stats[:, t]).then_inc(self.done, 1)
        dve.wait_ge(self.done, base + 2 * BT + 2)
        dve.tensor_scalar(mv[:, ds(BT * i, BT)], self.mean_var[:], 1.0, None, ALU.mult).then_inc(self.done, 1)

    def finish(self, dve):
        dve.wait_ge(self.done, self.PER * NB)


def split_matmuls(pe, out, weights, moving, first=True, last=True):
    n = len(weights)
    for k in range(n):
        (w_hi, w_lo), (m_hi, m_lo) = weights[k], moving[k]
        pe.matmul(out, w_hi, m_hi, start=(first and k == 0), stop=False)
        pe.matmul(out, w_hi, m_lo, start=False, stop=False)
        mm = pe.matmul(out, w_lo, m_hi, start=False, stop=(last and k == n - 1))
    return mm


def stage_semaphores(nc, ctx):
    taken = []
    ctx.callback(nc.all_engine_barrier)
    ctx.callback(lambda: nc.clear_and_free_semaphores(taken))

    def sem(name):
        taken.append(nc.alloc_semaphore(name))
        return taken[-1]

    return sem


def wavelet_stage(chip, x, wd, wa, bias, h_rows, slot_x, consts):
    nc = chip.nc
    NQ = 4
    ROWS, COLS = [4, 2, 1], [128, 64, 32]
    NW = 10
    with ExitStack() as ctx:
        def sb(name, shape, dt=F32):
            return ctx.enter_context(nc.sbuf_tensor(name, shape, dt))

        sem = stage_semaphores(nc, ctx)

        img = chip.h[:].rearrange("p (q r) c -> p q r c", q=NQ)
        lo_row = sb("lo_row", [P, 4, 256])
        hi_row = sb("hi_row", [P, 4, 256])
        avg = [sb(f"avg{n}", [P, NQ, ROWS[n], COLS[n]]) for n in range(3)]
        det = [sb(f"det{n}", [P, NQ, 3, ROWS[n] * COLS[n]]) for n in range(3)]
        w_det = [sb(f"w_det{n}", [P, 3, 3 * ROWS[n] * COLS[n]]) for n in range(3)]
        w_avg = sb("w_avg", [P, COLS[2]])
        prod = sb("prod", [P, 2, 3 * ROWS[0] * COLS[0]])
        parts = sb("parts", [P, NQ, NW])
        group = sb("group", [P, P])
        scale_in = sb("scale_in", [P, NW])
        scale_out = sb("scale_out", [P, NW])
        biases = sb("biases", [P, NW])
        logits = sb("logits", [P, NQ, NW])
        top = sb("top", [P, NQ, 3])
        wts = sb("wts", [P, NQ, NW])
        neg = sb("neg", [P, NQ, NW])
        tmp = sb("tmp", [P, 512])
        up = [sb(f"up{n}", [P, ROWS[n] * 2, COLS[n] * 2]) for n in range(3)]
        sums = ctx.enter_context(nc.psum_tensor("sums", [P, NQ * NW], F32))

        stats = TileStats("wave_stats", sb, sem)
        s_img = [sem(f"img_loaded{q}") for q in range(NQ)]
        zeros = sb("zeros", [P, BT * D])
        s_zero = sem("zeros_ready")
        s_zeroed = sem("slots_zeroed")
        s_const = sem("wavelet_consts_loaded")
        s_dve = sem("wavelet_dve")
        s_parts = sem("parts_ready")
        s_sums = sem("sums_ready")
        s_logit = sem("logits_ready")
        s_exp = sem("exp_ready")
        s_row = sem("rows_ready")
        s_store = [sem(f"rows_stored{q}") for q in range(NQ)]
        s_h = [sem(f"h_loaded{q}") for q in range(NQ)]
        n_const = 0

        with nc.Block() as block:
            @block.sync
            def _(sp):
                nonlocal n_const
                for q in range(NQ):
                    sp.dma_start(img[:, q], x[ds(q * P, P), :].rearrange("p (r c) -> p r c", r=8)).then_inc(s_img[q], 16)
                for n in range(3):
                    for b in range(4):
                        sp.dma_start(w_det[n][32 * b:32 * b + 32, :, :], wd[n].rearrange("g (j s) -> g j s", j=3)).then_inc(s_const, 16)
                for b in range(4):
                    sp.dma_start(w_avg[32 * b:32 * b + 32, :], wa).then_inc(s_const, 16)
                sp.dma_start(biases[:, :], bias.partition_broadcast(P)).then_inc(s_const, 16)
                sp.dma_start(scale_in[:, :], consts["scale_in"]).then_inc(s_const, 16)
                sp.dma_start(scale_out[:, :], consts["scale_out"]).then_inc(s_const, 16)
                sp.dma_start(group[:, :], consts["group"]).then_inc(s_const, 16)
                sp.dma_start(chip.ident[:, :], consts["ident"]).then_inc(s_const, 16)
                n_const = 16 * (12 + 4 + 5)
                sp.wait_ge(s_zero, 1)
                sp.dma_start(slot_x.rearrange("(n p r) d -> p n (r d)", p=P, r=BT), zeros[:, :].unsqueeze(1).to_broadcast([P, NRB, BT * D])).then_inc(s_zeroed, 16)
                for q in range(NQ):
                    sp.wait_ge(s_row, q + 1)
                    sp.dma_start(h_rows[ds(q * 4 * S, 4 * S), :].rearrange("(p r) c -> p r c", r=8), img[:, q]).then_inc(s_store[q], 16)
                for q in range(NQ):
                    sp.wait_ge(s_store[q], 16)
                    t = q * 4 * TI
                    sp.dma_start(chip.h[:, t:t + 4 * TI, :],
                                 h_rows[ds(q * 4 * S, 4 * S), :].rearrange("(t p) c -> p t c", p=P)).then_inc(s_h[q], 16)

                sp.wait_ge(s_zeroed, 16)

            @block.gpsimd
            def _(pool):
                pool.memset(zeros[:, :], 0.0).then_inc(s_zero, 1)

            @block.tensor
            def _(pe):
                pe.wait_ge(s_const, n_const)
                pe.wait_ge(s_parts, 1)
                pe.matmul(sums[:, :], group[:, :], parts[:].rearrange("p q w -> p (q w)"), start=True, stop=True).then_inc(s_sums, 1)

            @block.scalar
            def _(act):
                act.wait_ge(s_logit, 1)
                act.activation(wts[:, :, 0:9], logits[:, :, 0:9], ACT.Exp).then_inc(s_exp, 1)
                act.activation(wts[:, :, 9:10], logits[:, :, 9:10], ACT.Sigmoid).then_inc(s_exp, 1)

            @block.vector
            def _(dve):
                done = 0

                def step(ins):
                    nonlocal done
                    done += 1
                    ins.then_inc(s_dve, 1)

                def settled():
                    dve.wait_ge(s_dve, done)

                step(dve.memset(parts[:], 0.0))
                for q in range(NQ):
                    dve.wait_ge(s_img[q], 16)
                    for n in range(3):
                        src = img[:, q] if n == 0 else avg[n - 1][:, q]
                        R, C = ROWS[n], COLS[n]
                        rows = src.rearrange("p (r two) c -> p r two c", two=2)
                        lo_r, hi_r = lo_row[:, 0:R, 0:2 * C], hi_row[:, 0:R, 0:2 * C]
                        if n:
                            settled()
                        step(dve.tensor_tensor(lo_r, rows[:, :, 0], rows[:, :, 1], ALU.add))
                        step(dve.tensor_tensor(hi_r, rows[:, :, 0], rows[:, :, 1], ALU.subtract))
                        settled()
                        lo_c = lo_r.rearrange("p r (c two) -> p r c two", two=2)
                        hi_c = hi_r.rearrange("p r (c two) -> p r c two", two=2)
                        d = det[n][:, q].rearrange("p s (r c) -> p s r c", r=R)
                        step(dve.tensor_tensor(avg[n][:, q], lo_c[:, :, :, 0], lo_c[:, :, :, 1], ALU.add))
                        step(dve.tensor_tensor(d[:, 0], hi_c[:, :, :, 0], hi_c[:, :, :, 1], ALU.add))
                        step(dve.tensor_tensor(d[:, 1], lo_c[:, :, :, 0], lo_c[:, :, :, 1], ALU.subtract))
                        step(dve.tensor_tensor(d[:, 2], hi_c[:, :, :, 0], hi_c[:, :, :, 1], ALU.subtract))
                    settled()
                dve.wait_ge(s_const, n_const)
                k = 0
                for q in range(NQ):
                    for n in range(3):
                        for j in range(3):
                            m = 3 * ROWS[n] * COLS[n]
                            if k >= 2:
                                dve.wait_ge(s_dve, done - 1)
                            step(dve.tensor_tensor_reduce(prod[:, k % 2, 0:m], det[n][:, q].rearrange("p s c -> p (s c)"), w_det[n][:, j], 1.0, 0.0,
                                                          ALU.mult, ALU.add, parts[:, q, 3 * n + j:3 * n + j + 1]))
                            k += 1
                    dve.wait_ge(s_dve, done - 1)
                    step(dve.tensor_tensor_reduce(prod[:, k % 2, 0:COLS[2]], avg[2][:, q, 0], w_avg[:, :], 1.0, 0.0,
                                                  ALU.mult, ALU.add, parts[:, q, 9:10]))
                    k += 1
                settled()
                dve.engine_nop().then_inc(s_parts, 1)
                dve.wait_ge(s_sums, 1)

                def per_image(c):
                    return c[:, :].unsqueeze(1).to_broadcast([P, NQ, NW])

                step(dve.tensor_tensor(logits[:], sums[:, :].rearrange("p (q w) -> p q w", q=NQ), per_image(scale_in), ALU.mult))
                settled()
                step(dve.tensor_tensor(logits[:], logits[:], per_image(biases), ALU.add))
                settled()
                l3 = logits[:, :, 0:9].rearrange("p q (l j) -> p q l j", j=3)
                w3 = wts[:, :, 0:9].rearrange("p q (l j) -> p q l j", j=3)
                t3 = top[:].unsqueeze(3).to_broadcast([P, NQ, 3, 3])
                step(dve.tensor_reduce(top[:], l3, AX.X, ALU.max))
                settled()
                step(dve.tensor_tensor(l3, l3, t3, ALU.subtract))
                settled()
                dve.engine_nop().then_inc(s_logit, 1)
                dve.wait_ge(s_exp, 2)
                step(dve.tensor_reduce(top[:], w3, AX.X, ALU.add))
                settled()
                step(dve.reciprocal(top[:], top[:]))
                settled()
                step(dve.tensor_tensor(w3, w3, t3, ALU.mult))
                settled()
                step(dve.tensor_tensor(wts[:], wts[:], per_image(scale_out), ALU.mult))
                settled()
                step(dve.tensor_scalar(neg[:], wts[:], -1.0, None, ALU.mult))
                for q in range(NQ):
                    for n in (2, 1, 0):
                        R, C = ROWS[n], COLS[n]
                        d = det[n][:, q].rearrange("p s (r c) -> p s r c", r=R)
                        w = wts[:, q, 3 * n:3 * n + 3]
                        settled()
                        if n == 2:
                            step(dve.tensor_scalar(avg[2][:, q], avg[2][:, q], wts[:, q, 9:10], None, ALU.mult))
                            coarse = avg[2][:, q]
                        else:
                            coarse = up[n + 1][:, :, :]
                        t = tmp[:, 0:R * C].rearrange("p (r c) -> p r c", r=R)
                        step(dve.tensor_scalar(t, d[:, 2], w[:, 2:3], None, ALU.mult))
                        settled()
                        s_c = lo_row[:, 0:R, 0:2 * C].rearrange("p r (c two) -> p r c two", two=2)
                        d_c = hi_row[:, 0:R, 0:2 * C].rearrange("p r (c two) -> p r c two", two=2)
                        for e, wv, op in ((0, wts, ALU.add), (1, neg, ALU.subtract)):
                            step(dve.scalar_tensor_tensor(out=s_c[:, :, :, e], in0=d[:, 1], scalar=wv[:, q, 3 * n + 1:3 * n + 2],
                                                          in1=coarse, op0=ALU.mult, op1=ALU.add))
                            step(dve.scalar_tensor_tensor(out=d_c[:, :, :, e], in0=d[:, 0], scalar=w[:, 0:1],
                                                          in1=t, op0=ALU.mult, op1=op))
                        settled()
                        out = (img[:, q] if n == 0 else up[n][:, :, :]).rearrange("p (r two) c -> p r two c", two=2)
                        s_r, d_r = lo_row[:, 0:R, 0:2 * C], hi_row[:, 0:R, 0:2 * C]
                        step(dve.tensor_tensor(out[:, :, 0], s_r, d_r, ALU.add))
                        step(dve.tensor_tensor(out[:, :, 1], s_r, d_r, ALU.subtract))
                    settled()
                    dve.engine_nop().then_inc(s_row, 1)
                step(dve.memset(chip.x_hi[:, :, :, 0:1].bitcast(F32), 0.0))
                step(dve.memset(chip.x_lo[:, :, :, 0:1].bitcast(F32), 0.0))
                with dve.Fori(0, NB, 1) as i:
                    for q in range(NQ):
                        dve.wait_ge(s_h[q], 16)
                    stats.block(dve, chip.h, chip.mv, i)
                stats.finish(dve)
                settled()


def attention_stage(chip, a):
    nc = chip.nc
    EPS = 1e-8
    NF = D + 2
    Q, K, V = 0, 1, 2
    ORDER = (K, V, Q)
    with ExitStack() as ctx:
        def sb(name, shape, dt=F32):
            return ctx.enter_context(nc.sbuf_tensor(name, shape, dt))

        def ps(name, shape):
            return ctx.enter_context(nc.psum_tensor(name, shape, F32))

        sem = stage_semaphores(nc, ctx)

        w_raw = sb("w_raw", [P, 3, KT, D])
        fourier = sb("fourier", [P, KT, NF])
        inv_raw = sb("inv_raw", [P, 2, D])
        inv_hi = sb("inv_hi", [P, 2, D], F32R)
        inv_lo = sb("inv_lo", [P, 2, D], F32R)
        b_raw = sb("b_raw", [P, KT, 4])
        alt_cols = sb("alt_cols", [P, P])
        alt_row = sb("alt_row", [P, D])
        tri = sb("tri", [P, P])
        ones = sb("ones", [P, P])
        wf_hi = sb("wf_hi", [P, KT, 3, D], F32R)
        wf_lo = sb("wf_lo", [P, KT, 3, D], F32R)
        w_nyq = sb("w_nyq", [P, KT, 4])
        b_f = sb("b_f", [P, 3, 4])
        rstd = sb("rstd", [P, NT])
        xn = sb("xn", [P, BT, D])
        x_full = sb("x_full", [P, KT, BLK])
        sq = sb("sq", [P, 3, 2, BLK])
        mag = sb("mag", [P, 3, BLK])
        unit = sb("unit", [P, 3, 2, BLK])
        m = sb("m", [P, 4, BLK])
        cum = sb("cum", [P, 2, BLK])
        o = sb("o", [P, 4, BLK])
        o_hi = sb("o_hi", [P, 2, BLK], F32R)
        o_lo = sb("o_lo", [P, 2, BLK], F32R)
        nyq = sb("nyq", [P, BT, 3])
        nyq_r = sb("nyq_r", [P, BT, 3])
        nyq_p = sb("nyq_p", [P, BI, TI])
        nyq_z = sb("nyq_z", [P, BT])
        p_t = ps("p_t", [P, BLK])
        p_j = [[ps(f"p_j{n}{r}", [P, BLK]) for r in range(2)] for n in range(2)]
        p_o = ps("p_o", [P, BT, D])
        p_n = ps("p_n", [P, 512])
        BANK = {K: 0, V: 1, Q: 0}

        stats = TileStats("attn_stats", sb, sem)
        s_ld = sem("attn_loaded")
        s_wf = sem("fourier_weights")
        s_we = sem("fourier_weights_kept")
        s_prep = sem("prep_dve")
        s_var = sem("variance_ready")
        s_std = sem("std_ready")
        s_ready = sem("rstd_ready")
        s_xn = sem("xn_ready")
        s_tr = sem("transposed")
        s_hi = sem("x_hi_ready")
        s_xf = sem("x_full_ready")
        s_lo = sem("x_lo_ready")
        s_pj = sem("projected")
        s_nq = sem("nyquist_projected")
        s_nc = sem("nyquist_chain")
        s_np = sem("nyquist_product")
        s_z = sem("nyquist_unbound")
        s_cum = sem("nyquist_summed")
        s_sq = sem("squares_ready")
        s_sum = sem("power_ready")
        s_mag = sem("magnitude_ready")
        s_r = sem("reciprocal_chain")
        s_u = sem("units_ready")
        s_m = sem("products_dve")
        s_mp = sem("products_pool")
        s_c = sem("running_sums")
        s_ot = sem("unbound_dve")
        s_op = sem("unbound_pool")
        s_os = sem("unbound_ready")
        s_oh = sem("o_hi_ready")
        s_ol = sem("o_lo_ready")
        s_y = sem("y_ready")
        s_hz = sem("h_plus_nyquist")
        s_h = sem("h_updated")
        s_nu = sem("nyquist_units")

        with nc.Block() as block:
            @block.sync
            def _(sp):
                for dst, src in ((w_raw[:], a["w_qkv"].rearrange("(w k p) d -> p w k d", w=3, p=P)),
                                 (fourier[:], a["fourier"].rearrange("(k p) f -> p k f", p=P)),
                                 (inv_raw[:], a["inverse"].rearrange("(k p) d -> p k d", p=P)),
                                 (b_raw[:], a["b_qkv"].rearrange("(k p) w -> p k w", p=P)),
                                 (alt_cols[:], a["alt_cols"]), (alt_row[:], a["alt_row"]),
                                 (tri[:], a["tri"]), (ones[:], a["ones"])):
                    sp.dma_start(dst, src).then_inc(s_ld, 16)

            @block.tensor
            def _(pe):
                pe.wait_ge(s_ld, 16 * 8)
                for n in range(3 * KT):
                    w, mt = n // KT, n % KT
                    if n >= 4:
                        pe.wait_ge(s_we, n - 3)
                    out = p_j[n // 2 % 2][n % 2][:, 0:NF]
                    for k in range(KT):
                        mm = pe.matmul(out, w_raw[:, w, k, mt * P:(mt + 1) * P], fourier[:, k], start=(k == 0), stop=(k == KT - 1))
                    mm.then_inc(s_wf, 1)
                for part in range(3):
                    for k in range(KT):
                        lhs = alt_cols[:, :] if part == 2 else fourier[:, k, part * P:(part + 1) * P]
                        mm = pe.matmul(p_n[:, 4 * part:4 * part + 4], lhs, b_raw[:, k], start=(k == 0), stop=(k == KT - 1))
                mm.then_inc(s_wf, 1)

                def transposes(i):
                    pe.wait_ge(s_xn, BT * (i + 1))
                    for kt in range(KT):
                        pe.wait_ge(s_lo, KT * i + kt)
                        for t in range(BT):
                            mm = pe.transpose(p_t[:, t * P:(t + 1) * P], xn[:, t, kt * P:(kt + 1) * P], chip.ident[:, :])
                        mm.then_inc(s_tr, 1)

                def nyquist(i):
                    pe.wait_ge(s_xf, KT * (i + 1))
                    pe.wait_ge(s_z, i)
                    for t in range(BT):
                        for k in range(KT):
                            mm = pe.matmul(p_n[:, 4 * t:4 * t + 4], x_full[:, k, t * P:(t + 1) * P], w_nyq[:, k], start=(k == 0), stop=(k == KT - 1))
                    mm.then_inc(s_nq, 1)

                def back(i):
                    pe.wait_ge(s_lo, KT * (i + 1))
                    for n, w in enumerate(ORDER):
                        pe.wait_ge(s_u, 6 * i if n < 2 else 6 * i + 2)
                        for ri in range(2):
                            split_matmuls(pe, p_j[BANK[w]][ri][:, :],
                                          [(wf_hi[:, k, w, ri * P:(ri + 1) * P], wf_lo[:, k, w, ri * P:(ri + 1) * P]) for k in range(KT)],
                                          [(chip.x_block(chip.x_hi, k, i), chip.x_block(chip.x_lo, k, i)) for k in range(KT)]).then_inc(s_pj, 1)
                    pe.wait_ge(s_np, i + 1)
                    pe.matmul(p_n[:, 32:32 + BI], tri[:, :], nyq_p[:, :, 0], start=True, stop=True)
                    pe.matmul(p_n[:, 40:40 + BI], ones[:, :], nyq_p[:, :, 0], start=True, stop=False)
                    pe.matmul(p_n[:, 40:40 + BI], tri[:, :], nyq_p[:, :, 1], start=False, stop=True).then_inc(s_cum, 1)
                    pe.wait_ge(s_ol, 2 * (i + 1))
                    pe.wait_ge(s_h, BT * i)
                    for t in range(BT):
                        split_matmuls(pe, p_o[:, t], [(o_hi[:, r, t * P:(t + 1) * P], o_lo[:, r, t * P:(t + 1) * P]) for r in range(2)],
                                      [(inv_hi[:, r], inv_lo[:, r]) for r in range(2)]).then_inc(s_y, 1)

                pe.wait_ge(s_ready, 1)
                transposes(0)
                with pe.Fori(0, NB - 1, 1) as i:
                    nyquist(i)
                    transposes(i + 1)
                    back(i)
                nyquist(NB - 1)
                back(NB - 1)

            @block.scalar
            def _(act):
                act.wait_ge(s_var, 1)
                act.activation(rstd[:, :], rstd[:, :], ACT.Sqrt).then_inc(s_std, 1)

                def front(i):
                    for kt in range(KT):
                        act.wait_ge(s_tr, KT * i + kt + 1)
                        act.activation(chip.x_block(chip.x_hi, kt, i), p_t[:, :].rearrange("p (b s) -> p b s", b=BI), ACT.Copy).then_inc(s_hi, 1)
                        act.wait_ge(s_nq, i)
                        act.activation(x_full[:, kt], p_t[:, :], ACT.Copy).then_inc(s_xf, 1)

                def back(i):
                    def squares(n):
                        w = ORDER[n]
                        act.wait_ge(s_pj, 6 * i + 2 * n + 2)
                        for ri in range(2):
                            ins = act.activation(sq[:, w, ri], p_j[BANK[w]][ri][:, :], ACT.Square, bias=b_f[:, ri, w:w + 1])
                        ins.then_inc(s_sq, 1)

                    def root(n):
                        w = ORDER[n]
                        act.wait_ge(s_sum, 3 * i + n + 1)
                        act.activation(mag[:, w], mag[:, w], ACT.Sqrt).then_inc(s_mag, 1)

                    squares(0)
                    squares(1)
                    root(0)
                    root(1)
                    squares(2)
                    root(2)
                    for r in range(2):
                        act.wait_ge(s_os, 2 * i + r + 1)
                        act.wait_ge(s_y, BT * i)
                        act.activation(o_hi[:, r], o[:, 2 * r], ACT.Copy).then_inc(s_oh, 1)

                front(0)
                with act.Fori(0, NB - 1, 1) as i:
                    front(i + 1)
                    back(i)
                back(NB - 1)

            @block.gpsimd
            def _(pool):
                with pool.Fori(0, NB, 1) as i:
                    pool.wait_ge(s_u, 6 * i + 4)
                    pool.wait_ge(s_c, 4 * i)
                    pool.tensor_tensor(m[:, 1], unit[:, K, 1], unit[:, V, 1], ALU.mult).then_inc(s_mp, 1)
                    pool.tensor_tensor(m[:, 3], unit[:, K, 1], unit[:, V, 0], ALU.mult).then_inc(s_mp, 1)
                    pool.wait_ge(s_c, 4 * (i + 1))
                    pool.wait_ge(s_u, 6 * (i + 1))
                    pool.wait_ge(s_os, 2 * i)
                    pool.tensor_tensor(o[:, 3], cum[:, 0], unit[:, Q, 1], ALU.mult).then_inc(s_op, 1)

            @block.vector
            def _(dve):
                dve.tensor_scalar(rstd[:, :], chip.mv[:, :, 1], LN_EPS, None, ALU.add).then_inc(s_var, 1)
                dve.wait_ge(s_std, 1)
                dve.reciprocal(rstd[:, :], rstd[:, :]).then_inc(s_ready, 1)
                dve.wait_ge(s_ld, 16 * 8)
                dve.tensor_copy(inv_hi[:], inv_raw[:]).then_inc(s_prep, 1)
                dve.wait_ge(s_prep, 1)
                dve.tensor_tensor(inv_lo[:], inv_raw[:], inv_hi[:].bitcast(F32), ALU.subtract).then_inc(s_prep, 1)
                for n in range(3 * KT):
                    w, mt = n // KT, n % KT
                    src = p_j[n // 2 % 2][n % 2]
                    dve.wait_ge(s_wf, n + 1)
                    dve.tensor_copy(wf_hi[:, mt, w], src[:, 0:D]).then_inc(s_prep, 1)
                    dve.tensor_copy(w_nyq[:, mt, w:w + 1], src[:, D:D + 1]).then_inc(s_prep, 1)
                    dve.wait_ge(s_prep, 2 + 2 * n + 1)
                    dve.tensor_tensor(wf_lo[:, mt, w], src[:, 0:D], wf_hi[:, mt, w].bitcast(F32), ALU.subtract).then_inc(s_we, 1)
                dve.memset(w_nyq[:, :, 3:4], 0.0).then_inc(s_prep, 1)
                dve.wait_ge(s_wf, 3 * KT + 1)
                dve.tensor_copy(b_f[:], p_n[:, 0:12].rearrange("p (a w) -> p a w", a=3)).then_inc(s_prep, 1)
                dve.wait_ge(s_prep, 2 + 6 * KT + 2)

                def front(i):
                    dve.wait_ge(s_tr, KT * i)
                    for t in range(BT):
                        dve.tensor_scalar(xn[:, t:t + 1], chip.h[:, ds(BT * i + t, 1)], chip.mv[:, ds(BT * i + t, 1), 0], rstd[:, ds(BT * i + t, 1)],
                                          ALU.subtract, ALU.mult).then_inc(s_xn, 1)
                    for kt in range(KT):
                        dve.wait_ge(s_hi, KT * i + kt + 1)
                        dve.wait_ge(s_xf, KT * i + kt + 1)
                        dve.tensor_tensor(chip.x_block(chip.x_lo, kt, i), p_t[:, :].rearrange("p (b s) -> p b s", b=BI),
                                          chip.x_block(chip.x_hi, kt, i).bitcast(F32), ALU.subtract).then_inc(s_lo, 1)

                def back(i):
                    def power(n):
                        w = ORDER[n]
                        dve.wait_ge(s_sq, 3 * i + n + 1)
                        dve.tensor_tensor(mag[:, w], sq[:, w, 0], sq[:, w, 1], ALU.add).then_inc(s_sum, 1)

                    def units(n):
                        w = ORDER[n]
                        dve.wait_ge(s_mag, 3 * i + n + 1)
                        dve.tensor_scalar(mag[:, w], mag[:, w], EPS, None, ALU.add).then_inc(s_r, 1)
                        dve.wait_ge(s_r, 6 * i + 2 * n + 1)
                        dve.reciprocal(mag[:, w], mag[:, w]).then_inc(s_r, 1)
                        dve.wait_ge(s_r, 6 * i + 2 * n + 2)
                        if n == 2:
                            dve.wait_ge(s_op, i)
                        elif n == 0:
                            dve.wait_ge(s_mp, 2 * i)
                        for ri in range(2):
                            dve.scalar_tensor_tensor(out=unit[:, w, ri], in0=p_j[BANK[w]][ri][:, :], scalar=b_f[:, ri, w:w + 1],
                                                     in1=mag[:, w], op0=ALU.add, op1=ALU.mult).then_inc(s_u, 1)

                    power(0)
                    power(1)
                    units(0)
                    bias = b_f[:, 2, 0:3].unsqueeze(1).to_broadcast([P, BT, 3])
                    dve.wait_ge(s_nq, i + 1)
                    dve.tensor_tensor(nyq[:], p_n[:, 0:4 * BT].rearrange("p (t w) -> p t w", t=BT)[:, :, 0:3], bias, ALU.add).then_inc(s_nc, 1)
                    dve.wait_ge(s_nc, 5 * i + 1)
                    dve.tensor_scalar(nyq_r[:], nyq[:], -1.0, None, ALU.mult).then_inc(s_nc, 1)
                    dve.wait_ge(s_nc, 5 * i + 2)
                    dve.tensor_tensor(nyq_r[:], nyq_r[:], nyq[:], ALU.max).then_inc(s_nc, 1)
                    dve.wait_ge(s_nc, 5 * i + 3)
                    dve.tensor_scalar(nyq_r[:], nyq_r[:], EPS, None, ALU.add).then_inc(s_nc, 1)
                    dve.wait_ge(s_nc, 5 * i + 4)
                    dve.reciprocal(nyq_r[:], nyq_r[:]).then_inc(s_nc, 1)
                    dve.wait_ge(s_nc, 5 * i + 5)
                    dve.tensor_tensor(nyq[:], nyq[:], nyq_r[:], ALU.mult).then_inc(s_nu, 1)
                    dve.wait_ge(s_nu, i + 1)
                    dve.tensor_tensor(nyq_p[:], nyq[:, :, K].rearrange("p (b h) -> p b h", b=BI), nyq[:, :, V].rearrange("p (b h) -> p b h", b=BI),
                                      ALU.mult).then_inc(s_np, 1)
                    units(1)
                    power(2)
                    dve.wait_ge(s_u, 6 * i + 4)
                    dve.tensor_tensor(m[:, 0], unit[:, K, 0], unit[:, V, 0], ALU.mult).then_inc(s_m, 1)
                    dve.tensor_tensor(m[:, 2], unit[:, K, 0], unit[:, V, 1], ALU.mult).then_inc(s_m, 1)
                    units(2)
                    dve.wait_ge(s_cum, i + 1)
                    z = nyq_z[:, :].rearrange("p (b h) -> p h b", b=BI)
                    c = p_n[:, 32:48].rearrange("p (h b) -> p h b", h=2)[:, :, 0:BI]
                    dve.tensor_tensor(z, c, nyq[:, :, Q].rearrange("p (b h) -> p h b", b=BI), ALU.mult).then_inc(s_z, 1)
                    dve.wait_ge(s_m, 2 * (i + 1))
                    dve.wait_ge(s_mp, 2 * (i + 1))
                    for ri, op in ((0, ALU.subtract), (1, ALU.add)):
                        for b in range(BI):
                            dve.tensor_tensor_scan(cum[:, ri, b * S:(b + 1) * S], m[:, 2 * ri, b * S:(b + 1) * S], m[:, 2 * ri + 1, b * S:(b + 1) * S],
                                                   initial=0.0, op0=ALU.add, op1=op).then_inc(s_c, 1)
                    dve.wait_ge(s_c, 4 * (i + 1))
                    dve.wait_ge(s_u, 6 * (i + 1))
                    dve.wait_ge(s_oh, 2 * i)
                    dve.tensor_tensor(o[:, 0], cum[:, 0], unit[:, Q, 0], ALU.mult).then_inc(s_ot, 1)
                    dve.tensor_tensor(o[:, 1], cum[:, 1], unit[:, Q, 1], ALU.mult).then_inc(s_ot, 1)
                    dve.tensor_tensor(o[:, 2], cum[:, 1], unit[:, Q, 0], ALU.mult).then_inc(s_ot, 1)
                    dve.wait_ge(s_ot, 3 * i + 2)
                    dve.tensor_tensor(o[:, 0], o[:, 0], o[:, 1], ALU.add).then_inc(s_os, 1)
                    dve.wait_ge(s_ot, 3 * i + 3)
                    dve.wait_ge(s_op, i + 1)
                    dve.tensor_tensor(o[:, 2], o[:, 2], o[:, 3], ALU.subtract).then_inc(s_os, 1)
                    dve.wait_ge(s_y, BT * i)
                    for r in range(2):
                        dve.wait_ge(s_oh, 2 * i + r + 1)
                        dve.tensor_tensor(o_lo[:, r], o[:, 2 * r], o_hi[:, r].bitcast(F32), ALU.subtract).then_inc(s_ol, 1)
                    dve.wait_ge(s_z, i + 1)
                    for t in range(BT):
                        h = chip.h[:, ds(BT * i + t, 1)]
                        dve.scalar_tensor_tensor(out=h, in0=alt_row[:, :].unsqueeze(1), scalar=nyq_z[:, t:t + 1], in1=h, op0=ALU.mult, op1=ALU.add).then_inc(s_hz, 1)
                    for t in range(BT):
                        h = chip.h[:, ds(BT * i + t, 1)]
                        dve.wait_ge(s_hz, BT * i + t + 1)
                        dve.wait_ge(s_y, BT * i + t // 2 * 2 + 2)
                        dve.tensor_tensor(h, h, p_o[:, t:t + 1], ALU.add).then_inc(s_h, 1)
                    dve.wait_ge(s_h, BT * (i + 1))
                    stats.block(dve, chip.h, chip.mv, i)

                front(0)
                with dve.Fori(0, NB - 1, 1) as i:
                    front(i + 1)
                    back(i)
                back(NB - 1)
                stats.finish(dve)


class Routing:

    def __init__(self, nc, ctx):
        def sb(name, shape, dt=F32):
            return ctx.enter_context(nc.sbuf_tensor(name, shape, dt))

        self.weight = sb("choice_weight", [P, TOPK, NT])
        self.slot = sb("choice_slot", [P, TOPK, NT], U32)
        self.expert = sb("block_expert", [1, NRB], I32)


def gate_stage(chip, a, route, xn):
    nc = chip.nc
    with ExitStack() as ctx:
        def sb(name, shape, dt=F32):
            return ctx.enter_context(nc.sbuf_tensor(name, shape, dt))

        def ps(name, shape):
            return ctx.enter_context(nc.psum_tensor(name, shape, F32))

        sem = stage_semaphores(nc, ctx)
        rstd = sb("rstd_g", [P, NT])
        xn_blk = sb("xn_g", [P, BT, D])
        x_full = sb("x_full_g", [P, KT, BLK])
        w_gate = sb("w_gate", [P, KT, E])
        b_gate = sb("b_gate", [P, E])
        b_out = sb("b_out", [E + 1, D])
        before = sb("before", [P, E, E])
        tri = sb("tri_g", [P, P])
        ones = sb("ones_g", [P, P])
        counts = sb("counts", [P, NT // BT])
        numbers = sb("numbers", [P, NRB])
        later = sb("later", [P, E, NT])
        score = sb("score", [P, NT, E])
        biased = sb("biased", [P, NT, E])
        red = sb("red", [P, NT])
        wins = sb("wins", [P, NT, E, E])
        ties = sb("ties", [P, NT, E, E])
        rank = sb("rank", [P, NT, E])
        comb = sb("comb", [P, NT, E + 1])
        chosen = sb("chosen", [P, E, NT])
        total = sb("chosen_in_tile", [P, E, NT])
        upto = sb("chosen_upto", [P, E, NT])
        slots = sb("slots", [P, E, NT])
        fits = sb("fits", [P, E, NT // BT])
        blocks = sb("blocks", [P, E])
        last = sb("last_block", [P, E])
        base = sb("first_block", [P, E])
        pick = sb("pick", [P, NT, E])
        slot_f = sb("slot_f", [P, TOPK, NT])
        reached = sb("reached", [1, NRB, E])
        expert_f = sb("expert_f", [1, NRB])
        comb_blk = sb("comb_blk", [P, BT, E + 1])
        comb_t = sb("comb_t", [E + 1, BLK])
        p_t = [ps(f"p_t_g{k}", [P, BLK]) for k in range(KT)]
        p_g = ps("p_g", [P, BT, E])
        p_c = ps("p_c", [P, BLK])
        p_b = ps("p_b", [P, BT, D])
        p_n = ps("p_n_g", [P, 2, E * NT])

        s_ld = sem("gate_loaded")
        s_var = sem("g_variance_ready")
        s_std = sem("g_std_ready")
        s_ready = sem("g_rstd_ready")
        s_xn = sem("g_xn_ready")
        s_keep = sem("g_xn_kept")
        s_xa = sem("g_later_set")
        s_tr = sem("g_transposed")
        s_hi = sem("g_x_hi_ready")
        s_xf = sem("g_x_full_ready")
        s_lo = sem("g_x_lo_ready")
        s_gt = sem("gate_projected")
        s_sc = sem("scores_kept")
        s_ch = sem("gate_chain")
        s_mx = sem("gate_max_taken")
        s_ex = sem("gate_exp")
        s_sel = sem("chosen_ready")
        s_cnt = sem("chosen_counted")
        s_cb = sem("comb_ready")
        s_cc = sem("comb_block_ready")
        s_ct = sem("comb_transposed")
        s_ck = sem("comb_t_kept")
        s_bm = sem("biases_mixed")
        s_ba = sem("biases_added")
        LOADS = 8

        with nc.Block() as block:
            @block.sync
            def _(sp):
                for dst, src in ((w_gate[:], a["gate_w"].rearrange("(k p) e -> p k e", p=P)),
                                 (b_gate[:], a["gate_b"].partition_broadcast(P)),
                                 (b_out[:], a["b_out"]), (before[:], a["before"].rearrange("p (e f) -> p e f", e=E)),
                                 (tri[:], a["tri"]), (ones[:], a["ones"]), (counts[:], a["counts"]), (numbers[:], a["numbers"])):
                    sp.dma_start(dst, src).then_inc(s_ld, 16)

            @block.tensor
            def _(pe):
                pe.wait_ge(s_ld, 16 * LOADS)
                pe.wait_ge(s_ready, 1)
                with pe.Fori(0, NB, 1) as i:
                    pe.wait_ge(s_xn, BT * (i + 1))
                    pe.wait_ge(s_lo, KT * i)
                    for kt in range(KT):
                        for t in range(BT):
                            mm = pe.transpose(p_t[kt][:, t * P:(t + 1) * P], xn_blk[:, t, kt * P:(kt + 1) * P], chip.ident[:, :])
                        mm.then_inc(s_tr, 1)
                    pe.wait_ge(s_xf, KT * (i + 1))
                    pe.wait_ge(s_sc, i)
                    for t in range(BT):
                        for k in range(KT):
                            mm = pe.matmul(p_g[:, t], x_full[:, k, t * P:(t + 1) * P], w_gate[:, k], start=(k == 0), stop=(k == KT - 1))
                    mm.then_inc(s_gt, 1)
                pe.wait_ge(s_sel, 1)
                picked = chosen[:].rearrange("p e t -> p (e t)")
                pe.matmul(p_n[:, 0], tri[:, :], picked, start=True, stop=True)
                pe.matmul(p_n[:, 1], ones[:, :], picked, start=True, stop=True).then_inc(s_cnt, 1)
                pe.wait_ge(s_cb, 2)
                with pe.Fori(0, NB, 1) as i:
                    pe.wait_ge(s_cc, i + 1)
                    pe.wait_ge(s_ck, i)
                    for t in range(BT):
                        mm = pe.transpose(p_c[0:E + 1, t * P:(t + 1) * P], comb_blk[:, t], chip.ident[:, :])
                    mm.then_inc(s_ct, 1)
                    pe.wait_ge(s_ck, i + 1)
                    pe.wait_ge(s_ba, BT * i)
                    for t in range(BT):
                        pe.matmul(p_b[:, t], comb_t[:, t * P:(t + 1) * P], b_out[:, :], start=True, stop=True).then_inc(s_bm, 1)

            @block.scalar
            def _(act):
                act.wait_ge(s_var, 1)
                act.activation(rstd[:, :], rstd[:, :], ACT.Sqrt).then_inc(s_std, 1)
                with act.Fori(0, NB, 1) as i:
                    act.wait_ge(s_gt, i)
                    for kt in range(KT):
                        act.wait_ge(s_tr, KT * i + kt + 1)
                        act.activation(chip.x_block(chip.x_hi, kt, i), p_t[kt][:, :].rearrange("p (b s) -> p b s", b=BI), ACT.Copy).then_inc(s_hi, 1)
                        act.activation(x_full[:, kt], p_t[kt][:, :], ACT.Copy).then_inc(s_xf, 1)
                act.wait_ge(s_mx, 1)
                act.activation(score[:], score[:], ACT.Exp).then_inc(s_ex, 1)

            @block.gpsimd
            def _(pool):
                pool.memset(later[:], 1.0).then_inc(s_xa, 1)
                pool.wait_ge(s_xa, 1)
                pool.memset(later[:, :, 0:1], 0.0).then_inc(s_xa, 1)
                with pool.Fori(0, NB, 1) as i:
                    pool.wait_ge(s_xn, BT * (i + 1))
                    pool.tensor_copy(xn[:, ds(BT * i, BT)], xn_blk[:]).then_inc(s_keep, 1)

            @block.vector
            def _(dve):
                dve.tensor_scalar(rstd[:, :], chip.mv[:, :, 1], LN_EPS, None, ALU.add).then_inc(s_var, 1)
                dve.wait_ge(s_std, 1)
                dve.reciprocal(rstd[:, :], rstd[:, :]).then_inc(s_ready, 1)
                dve.wait_ge(s_ready, 1)
                with dve.Fori(0, NB, 1) as i:
                    dve.wait_ge(s_tr, KT * i)
                    dve.wait_ge(s_keep, i)
                    for t in range(BT):
                        dve.tensor_scalar(xn_blk[:, t:t + 1], chip.h[:, ds(BT * i + t, 1)], chip.mv[:, ds(BT * i + t, 1), 0], rstd[:, ds(BT * i + t, 1)],
                                          ALU.subtract, ALU.mult).then_inc(s_xn, 1)
                    for kt in range(KT):
                        dve.wait_ge(s_xf, KT * i + kt + 1)
                        dve.tensor_tensor(chip.x_block(chip.x_lo, kt, i), p_t[kt][:, :].rearrange("p (b s) -> p b s", b=BI),
                                          chip.x_block(chip.x_hi, kt, i).bitcast(F32), ALU.subtract).then_inc(s_lo, 1)
                    dve.wait_ge(s_gt, i + 1)
                    dve.tensor_copy(score[:, ds(BT * i, BT)], p_g[:]).then_inc(s_sc, 1)
                n = 0

                def chain(ins):
                    nonlocal n
                    n += 1
                    ins.then_inc(s_ch, 1)
                    dve.wait_ge(s_ch, n)

                per_token = red[:, :].unsqueeze(2).to_broadcast([P, NT, E])
                dve.wait_ge(s_sc, NB)
                chain(dve.tensor_reduce(red[:, :], score[:], AX.X, ALU.max))
                dve.tensor_tensor(score[:], score[:], per_token, ALU.subtract).then_inc(s_mx, 1)
                dve.wait_ge(s_ex, 1)
                chain(dve.tensor_reduce(red[:, :], score[:], AX.X, ALU.add))
                chain(dve.reciprocal(red[:, :], red[:, :]))
                chain(dve.tensor_tensor(score[:], score[:], per_token, ALU.mult))
                dve.wait_ge(s_ld, 16 * LOADS)
                chain(dve.tensor_tensor(biased[:], score[:], b_gate[:, :].unsqueeze(1).to_broadcast([P, NT, E]), ALU.add))
                mine = biased[:].unsqueeze(3).to_broadcast([P, NT, E, E])
                theirs = biased[:].unsqueeze(2).to_broadcast([P, NT, E, E])
                chain(dve.tensor_tensor(wins[:], theirs, mine, ALU.is_gt))
                chain(dve.tensor_tensor(ties[:], theirs, mine, ALU.is_equal))
                chain(dve.tensor_tensor(ties[:], ties[:], before[:].unsqueeze(1).to_broadcast([P, NT, E, E]), ALU.mult))
                chain(dve.tensor_tensor(wins[:], wins[:], ties[:], ALU.add))
                chain(dve.tensor_reduce(rank[:], wins[:], AX.X, ALU.add))
                dve.tensor_scalar(chosen[:].rearrange("p e t -> p t e"), rank[:], TOPK - 0.5, None, ALU.is_lt).then_inc(s_sel, 1)
                dve.scalar_tensor_tensor(out=comb[:, :, 0:E], in0=rank[:], scalar=TOPK - 0.5, in1=score[:], op0=ALU.is_lt, op1=ALU.mult).then_inc(s_cb, 1)
                dve.memset(comb[:, :, E:E + 1], 1.0).then_inc(s_cb, 1)
                with dve.Fori(0, NB, 1) as i:
                    dve.wait_ge(s_cb, 2)
                    dve.wait_ge(s_ct, i)
                    dve.tensor_copy(comb_blk[:], comb[:, ds(BT * i, BT)]).then_inc(s_cc, 1)
                    dve.wait_ge(s_ct, i + 1)
                    dve.wait_ge(s_bm, BT * i)
                    dve.tensor_copy(comb_t[:, :], p_c[0:E + 1, :]).then_inc(s_ck, 1)
                    for t in range(BT):
                        h = chip.h[:, ds(BT * i + t, 1)]
                        dve.wait_ge(s_bm, BT * i + t // 2 * 2 + 2)
                        dve.tensor_tensor(h, h, p_b[:, t:t + 1], ALU.add).then_inc(s_ba, 1)
                dve.wait_ge(s_cnt, 1)
                dve.wait_ge(s_xa, 2)
                chain(dve.tensor_copy(total[:], p_n[:, 1].rearrange("p (e t) -> p e t", e=E)))
                chain(dve.tensor_tensor_scan(upto[:].rearrange("p e t -> p (e t)"), later[:].rearrange("p e t -> p (e t)"),
                                             total[:].rearrange("p e t -> p (e t)"), initial=0.0, op0=ALU.mult, op1=ALU.add))
                chain(dve.tensor_tensor(fits[:], upto[:, :, NT - 1:NT].to_broadcast([P, E, NT // BT]),
                                        counts[:, :].unsqueeze(1).to_broadcast([P, E, NT // BT]), ALU.is_gt))
                chain(dve.tensor_reduce(blocks[:, :], fits[:], AX.X, ALU.add))
                chain(dve.tensor_tensor_scan(last[:, :], ones[:, 0:E], blocks[:, :], initial=0.0, op0=ALU.mult, op1=ALU.add))
                chain(dve.tensor_tensor(base[:, :], last[:, :], blocks[:, :], ALU.subtract))
                chain(dve.tensor_tensor(reached[:], base[0:1, :].unsqueeze(1).to_broadcast([1, NRB, E]),
                                        numbers[0:1, :].unsqueeze(2).to_broadcast([1, NRB, E]), ALU.is_le))
                chain(dve.tensor_reduce(expert_f[:, :], reached[:], AX.X, ALU.add))
                chain(dve.tensor_scalar(route.expert[:, :], expert_f[:, :], -1.0, None, ALU.add))
                chain(dve.tensor_scalar(last[:, :], base[:, :], float(BLK), -1.0, ALU.mult, ALU.add))
                chain(dve.tensor_tensor(upto[:], upto[:], total[:], ALU.subtract))
                chain(dve.tensor_tensor(slots[:], upto[:], p_n[:, 0].rearrange("p (e t) -> p e t", e=E), ALU.add))
                chain(dve.tensor_tensor(slots[:], slots[:], last[:, :].unsqueeze(2).to_broadcast([P, E, NT]), ALU.add))
                for c in range(TOPK):
                    chain(dve.scalar_tensor_tensor(out=pick[:], in0=rank[:], scalar=float(c), in1=score[:], op0=ALU.is_equal, op1=ALU.mult))
                    chain(dve.tensor_reduce(route.weight[:, c], pick[:], AX.X, ALU.add))
                    chain(dve.scalar_tensor_tensor(out=pick[:], in0=rank[:], scalar=float(c), in1=slots[:].rearrange("p e t -> p t e"),
                                                   op0=ALU.is_equal, op1=ALU.mult))
                    chain(dve.tensor_reduce(slot_f[:, c], pick[:], AX.X, ALU.add))
                chain(dve.tensor_copy(route.slot[:], slot_f[:]))


class ExpertBuffers:

    def __init__(self, nc, ctx, tag):
        def sb(name, shape, dt=F32):
            return ctx.enter_context(nc.sbuf_tensor(name + tag, shape, dt))

        def ps(name, shape):
            return ctx.enter_context(nc.psum_tensor(name + tag, shape, F32))

        self.w13_hi = sb("w13_hi", [P, NJ, KT, 4 * P], F32R)
        self.w13_lo = sb("w13_lo", [P, NJ, KT, 4 * P], F32R)
        self.w2_hi = sb("w2_hi", [P, NJ, D], F32R)
        self.w2_lo = sb("w2_lo", [P, NJ, D], F32R)
        self.lin = sb("lin", [P, 2, BLK])
        self.g = sb("g", [P, BLK])
        self.li = sb("li", [P, BLK])
        self.sg = sb("sg", [P, BLK])
        self.gl = sb("gl", [P, BLK])
        self.hid = sb("hid", [P, 2, BLK])
        self.hid_hi = sb("hid_hi", [P, NJ, BLK], F32R)
        self.hid_lo = sb("hid_lo", [P, NJ, BLK], F32R)
        self.p1 = [ps(f"p1_{h}", [P, BLK]) for h in range(2)]
        self.p3 = [ps(f"p3_{h}", [P, BLK]) for h in range(2)]
        self.p_y = ps("p_y", [P, BT, D])


class ExpertSems:
    def __init__(self, sem, tag):
        self.c13 = sem("w13_split" + tag)
        self.c2 = sem("w2_split" + tag)
        self.ph = sem("halves_projected" + tag)
        self.lin = sem("lin_ready" + tag)
        self.st = sem("halves_multiplied" + tag)
        self.gm = sem("g_limited" + tag)
        self.lc = sem("l_limited" + tag)
        self.gl = sem("gl_ready" + tag)
        self.sg = sem("sigmoid_ready" + tag)
        self.hm = sem("hidden_ready" + tag)
        self.hh = sem("hidden_hi_ready" + tag)
        self.hl = sem("hidden_lo_ready" + tag)
        self.w2 = [sem(f"w2_applied{j}" + tag) for j in range(NJ)]
        self.out = sem("y_taken" + tag)


def pe_half(pe, u, s, n, j, hf, weights, x, first=False):
    pe.wait_ge(s.c13, weights)
    if not first:
        pe.wait_ge(s.st, 2 * NJ * n + 2 * j + hf - 1)
    for q, out in ((2 * hf, u.p1[hf]), (2 * hf + 1, u.p3[hf])):
        mm = split_matmuls(pe, out[:, :], [(u.w13_hi[:, j, k, q * P:(q + 1) * P], u.w13_lo[:, j, k, q * P:(q + 1) * P]) for k in range(KT)], x)
    mm.then_inc(s.ph, 1)


def pe_down(pe, u, s, n, j, weights):
    pe.wait_ge(s.hl, NJ * n + j + 1)
    if j == 0:
        pe.wait_ge(s.out, BT * n)
        pe.wait_ge(s.c2, weights)
    for t in range(BT):
        hi, lo = u.hid_hi[:, j, t * P:(t + 1) * P], u.hid_lo[:, j, t * P:(t + 1) * P]
        pe.matmul(u.p_y[:, t], hi, u.w2_hi[:, j], start=(j == 0 and t % 2 == 0), stop=False, skip_group_check=True)
        pe.matmul(u.p_y[:, t], hi, u.w2_lo[:, j], start=False, stop=False, skip_group_check=True)
        mm = pe.matmul(u.p_y[:, t], lo, u.w2_hi[:, j], start=False, stop=(j == NJ - 1), skip_group_check=True)
    mm.then_inc(s.w2[j], 1)


def act_inner(act, u, s, n, j, bias):
    for hf in range(2):
        act.wait_ge(s.ph, 2 * NJ * n + 2 * j + hf + 1)
        act.wait_ge(s.st, 2 * NJ * n if j == 0 else 2 * NJ * n + 2 * j + hf - 1)
        act.activation(u.lin[:, hf], u.p1[hf][:, :], ACT.Identity, bias=bias(j, 2 * hf)).then_inc(s.lin, 1)
        if hf == 0:
            act.wait_ge(s.gm, NJ * n + j + 1)
            act.wait_ge(s.hm, NJ * n + j)
            act.activation(u.sg[:, :], u.g[:, :], ACT.Sigmoid, scale=SWIGLU_ALPHA).then_inc(s.sg, 1)
    act.wait_ge(s.hm, NJ * n + j + 1)
    act.wait_ge(s.w2[j], n)
    act.activation(u.hid_hi[:, j], u.hid[:, j % 2], ACT.Copy).then_inc(s.hh, 1)


def dve_inner(dve, u, s, n, j, bias):
    def low(m):
        dve.wait_ge(s.hh, NJ * n + m + 1)
        dve.tensor_tensor(u.hid_lo[:, m], u.hid[:, m % 2], u.hid_hi[:, m].bitcast(F32), ALU.subtract).then_inc(s.hl, 1)

    k = NJ * n + j
    if j:
        low(j - 1)
    dve.wait_ge(s.lin, 2 * k + 1)
    dve.wait_ge(s.gl, k)
    dve.scalar_tensor_tensor(out=u.g[:, :], in0=u.p3[0][:, :], scalar=bias(j, 1), in1=u.lin[:, 0], op0=ALU.add, op1=ALU.mult).then_inc(s.st, 1)
    dve.wait_ge(s.st, 2 * k + 1)
    dve.tensor_scalar(u.g[:, :], u.g[:, :], SWIGLU_LIMIT, None, ALU.min).then_inc(s.gm, 1)
    dve.wait_ge(s.lin, 2 * k + 2)
    dve.scalar_tensor_tensor(out=u.li[:, :], in0=u.p3[1][:, :], scalar=bias(j, 3), in1=u.lin[:, 1], op0=ALU.add, op1=ALU.mult).then_inc(s.st, 1)
    dve.wait_ge(s.st, 2 * k + 2)
    dve.tensor_scalar(u.li[:, :], u.li[:, :], SWIGLU_LIMIT, -SWIGLU_LIMIT, ALU.min, ALU.max).then_inc(s.lc, 1)
    dve.wait_ge(s.lc, k + 1)
    dve.wait_ge(s.gm, k + 1)
    dve.scalar_tensor_tensor(out=u.gl[:, :], in0=u.li[:, :], scalar=1.0, in1=u.g[:, :], op0=ALU.add, op1=ALU.mult).then_inc(s.gl, 1)
    dve.wait_ge(s.gl, k + 1)
    dve.wait_ge(s.sg, k + 1)
    dve.tensor_tensor(u.hid[:, j % 2], u.gl[:, :], u.sg[:, :], ALU.mult).then_inc(s.hm, 1)
    if j == NJ - 1:
        dve.wait_ge(s.hm, k + 1)
        low(j)


def shared_expert_stage(chip, a, route, xn, slot_x):
    nc = chip.nc
    with ExitStack() as ctx:
        sem = stage_semaphores(nc, ctx)
        u = ExpertBuffers(nc, ctx, "_s")
        s = ExpertSems(sem, "_s")
        b13 = ctx.enter_context(nc.sbuf_tensor("b13_s", [P, 4 * NJ], F32))
        s_ld = sem("shared_loaded")
        s_hi = sem("shared_hi_ready")
        s_sent = sem("rows_sent")
        with nc.sbuf_tensor("raw_s", [P, KT * 4 * P], F32) as raw, nc.Block() as block:
            chunks = [(u.w13_hi[:, j].rearrange("p k c -> p (k c)"), u.w13_lo[:, j].rearrange("p k c -> p (k c)"),
                       a["w13"][(E * NJ + j) * P:(E * NJ + j + 1) * P, :]) for j in range(NJ)]
            chunks.append((u.w2_hi[:].rearrange("p j d -> p (j d)"), u.w2_lo[:].rearrange("p j d -> p (j d)"), a["w2"][E * P:(E + 1) * P, :]))

            @block.sync
            def _(sp):
                sp.dma_start(b13[:, :], a["b13"][E * P:(E + 1) * P, :]).then_inc(s_ld, 16)
                for j, (_, _, src) in enumerate(chunks):
                    if j:
                        sp.wait_ge(s.c13, j)
                    sp.wait_ge(s_ld, 16 * (j + 1))
                    sp.dma_start(raw[:, :], src).then_inc(s_ld, 16)

            @block.scalar
            def _(act):
                for j, (hi, _, _) in enumerate(chunks):
                    act.wait_ge(s_ld, 32 + 16 * j)
                    act.activation(hi, raw[:, :], ACT.Copy).then_inc(s_hi, 1)

            @block.vector
            def _(dve):
                for j, (hi, lo, _) in enumerate(chunks):
                    dve.wait_ge(s_hi, j + 1)
                    dve.tensor_tensor(lo, raw[:, :], hi.bitcast(F32), ALU.subtract).then_inc(s.c13 if j < NJ else s.c2, 1)

        def bias(j, q):
            return b13[:, 4 * j + q:4 * j + q + 1]

        with nc.Block() as block:
            @block.gpsimd
            def _(pool):
                for t in range(NT):
                    for c in range(TOPK):
                        pool.indirect_dma_start(slot_x, bass.IndirectOffsetOnAxis(ap=route.slot[:, c, t:t + 1], axis=0), xn[:, t], None).then_inc(s_sent, 16)
                pool.wait_ge(s_sent, 16 * TOPK * NT)

            @block.tensor
            def _(pe):
                def x(i):
                    return [(chip.x_block(chip.x_hi, k, i), chip.x_block(chip.x_lo, k, i)) for k in range(KT)]

                def body(i, more):
                    for j in range(1, NJ):
                        pe_half(pe, u, s, i, j, 0, NJ, x(i))
                        pe_half(pe, u, s, i, j, 1, NJ, x(i))
                        pe_down(pe, u, s, i, j - 1, 1)
                    if more:
                        pe_half(pe, u, s, i + 1, 0, 0, NJ, x(i + 1))
                    pe_down(pe, u, s, i, NJ - 1, 1)
                    if more:
                        pe_half(pe, u, s, i + 1, 0, 1, NJ, x(i + 1))

                for hf in range(2):
                    pe_half(pe, u, s, 0, 0, hf, NJ, x(0), first=True)
                with pe.Fori(0, NB - 1, 1) as i:
                    body(i, True)
                body(NB - 1, False)

            @block.scalar
            def _(act):
                with act.Fori(0, NB, 1) as i:
                    for j in range(NJ):
                        act_inner(act, u, s, i, j, bias)

            @block.vector
            def _(dve):
                with dve.Fori(0, NB, 1) as i:
                    for j in range(NJ):
                        dve_inner(dve, u, s, i, j, bias)
                    dve.wait_ge(s.w2[NJ - 1], i + 1)
                    for t in range(BT):
                        h = chip.h[:, ds(BT * i + t, 1)]
                        dve.tensor_tensor(h, h, u.p_y[:, t:t + 1], ALU.add).then_inc(s.out, 1)


def routed_experts_stage(chip, a, route, slot_x, slot_y):
    nc = chip.nc
    with ExitStack() as ctx:
        def sb(name, shape, dt=F32):
            return ctx.enter_context(nc.sbuf_tensor(name, shape, dt))

        sem = stage_semaphores(nc, ctx)
        u = ExpertBuffers(nc, ctx, "_r")
        s = ExpertSems(sem, "_r")
        w13_raw = sb("w13_raw", [P, NJ, KT, 4 * P])
        w2_raw = sb("w2_raw", [P, NJ, D])
        b13 = sb("b13", [P, 2, 4 * NJ])
        x_in = sb("x_in", [P, BT, D])
        x_hi = sb("xs_hi", [P, KT, 2, BLK], F32R)
        x_lo = sb("xs_lo", [P, KT, 2, BLK], F32R)
        y_out = sb("y_out", [P, 2, BT, D])
        p_t = [ctx.enter_context(nc.psum_tensor(f"p_t_r{k}", [P, BLK], F32)) for k in range(KT)]
        s_x = sem("slot_rows_loaded")
        s_b = sem("slot_biases_loaded")
        s_r13 = [sem(f"w13_loaded{j}") for j in range(NJ)]
        s_r2 = sem("w2_loaded")
        s_h13 = sem("w13_hi_ready")
        s_h2 = sem("w2_hi_ready")
        s_tr = sem("slots_transposed")
        s_xh = sem("slots_hi_ready")
        s_xl = sem("slots_lo_ready")
        s_y = [sem(f"y_stored{r}") for r in range(2)]

        with nc.Block() as block:
            @block.sync
            def _(sp):
                def expert_of(n):
                    return sp.value_load(route.expert[0:1, ds(n, 1)], min_val=0, max_val=E - 1)

                def load_rows(n, first=False):
                    e = expert_of(n)
                    if not first:
                        sp.wait_ge(s_tr, KT * n)
                    sp.dma_start(x_in[:], slot_x[ds(n * BLK, BLK), :].rearrange("(t p) d -> p t d", p=P)).then_inc(s_x, 16)
                    for j in range(NJ):
                        if not first:
                            sp.wait_ge(s.c13, NJ * (n - 1) + j + 1)
                        sp.dma_start(w13_raw[:, j], a["w13"][ds((e * NJ + j) * P, P), :].rearrange("p (k c) -> p k c", k=KT)).then_inc(s_r13[j], 16)

                def load_w2(n, first=False):
                    e = expert_of(n)
                    if not first:
                        sp.wait_ge(s.c2, n)
                        sp.wait_ge(s.st, 2 * NJ * (n - 1) + 1)
                    sp.dma_start(w2_raw[:], a["w2"][ds(e * P, P), :].rearrange("p (j d) -> p j d", j=NJ)).then_inc(s_r2, 16)
                    sp.dma_start(b13[:, ds(n % 2, 1)], a["b13"][ds(e * P, P), :].unsqueeze(1)).then_inc(s_b, 16)

                def store(n, parity):
                    sp.wait_ge(s.out, BT * (n + 1))
                    sp.dma_start(slot_y[ds(n * BLK, BLK), :].rearrange("(t p) d -> p t d", p=P), y_out[:, parity]).then_inc(s_y[parity], 16)

                load_rows(0, first=True)
                load_w2(0, first=True)
                load_rows(1)
                load_w2(1)
                with sp.Fori(0, NRB // 2 - 1, 1) as m:
                    for parity in range(2):
                        load_rows(2 * m + 2 + parity)
                        store(2 * m + parity, parity)
                        load_w2(2 * m + 2 + parity)
                for parity in range(2):
                    store(NRB - 2 + parity, parity)
                for parity in range(2):
                    sp.wait_ge(s_y[parity], 16 * (NRB // 2))

            @block.gpsimd
            def _(pool):
                def split(n):
                    for j in range(NJ):
                        pool.wait_ge(s_h13, NJ * n + j + 1)
                        pool.tensor_tensor(u.w13_lo[:, j], w13_raw[:, j], u.w13_hi[:, j].bitcast(F32), ALU.subtract).then_inc(s.c13, 1)
                    pool.wait_ge(s_h2, n + 1)
                    pool.tensor_tensor(u.w2_lo[:], w2_raw[:], u.w2_hi[:].bitcast(F32), ALU.subtract).then_inc(s.c2, 1)

                with pool.Fori(0, NRB, 1) as n:
                    split(n)

            @block.tensor
            def _(pe):
                def x(n):
                    return [(x_hi[:, k, ds(n % 2, 1)], x_lo[:, k, ds(n % 2, 1)]) for k in range(KT)]

                def transposes(n):
                    pe.wait_ge(s_x, 16 * (n + 1))
                    pe.wait_ge(s_xl, KT * n)
                    for kt in range(KT):
                        for t in range(BT):
                            mm = pe.transpose(p_t[kt][:, t * P:(t + 1) * P], x_in[:, t, kt * P:(kt + 1) * P], chip.ident[:, :])
                        mm.then_inc(s_tr, 1)

                def half(n, j, hf, first=False):
                    pe_half(pe, u, s, n, j, hf, NJ * n + j + 1, x(n), first)

                def body(n, more):
                    for j in range(1, NJ):
                        half(n, j, 0)
                        half(n, j, 1)
                        pe_down(pe, u, s, n, j - 1, n + 1)
                        if more and j == 1:
                            transposes(n + 1)
                    if more:
                        pe.wait_ge(s_xl, KT * (n + 2))
                        half(n + 1, 0, 0)
                    pe_down(pe, u, s, n, NJ - 1, n + 1)
                    if more:
                        half(n + 1, 0, 1)

                transposes(0)
                pe.wait_ge(s_xl, KT)
                half(0, 0, 0, first=True)
                half(0, 0, 1, first=True)
                with pe.Fori(0, NRB - 1, 1) as n:
                    body(n, True)
                body(NRB - 1, False)

            @block.scalar
            def _(act):
                def high13(n, j):
                    act.wait_ge(s_r13[j], 16 * (n + 1))
                    act.wait_ge(s.c13, NJ * n)
                    act.activation(u.w13_hi[:, j], w13_raw[:, j], ACT.Copy).then_inc(s_h13, 1)

                def high2(n):
                    act.wait_ge(s_r2, 16 * (n + 1))
                    act.activation(u.w2_hi[:], w2_raw[:], ACT.Copy).then_inc(s_h2, 1)

                def rows(n):
                    for kt in range(KT):
                        act.wait_ge(s_tr, KT * n + kt + 1)
                        act.activation(x_hi[:, kt, ds(n % 2, 1)], p_t[kt][:, :].unsqueeze(1), ACT.Copy).then_inc(s_xh, 1)

                def body(n, more):
                    def bias(j, q):
                        return b13[:, ds(n % 2, 1), 4 * j + q]

                    act.wait_ge(s_b, 16 * (n + 1))
                    for j in range(NJ):
                        act_inner(act, u, s, n, j, bias)
                        if more:
                            high13(n + 1, j)
                            if j == 1:
                                rows(n + 1)
                    act.wait_ge(s.w2[NJ - 1], n + 1)
                    if more:
                        high2(n + 1)

                rows(0)
                for j in range(NJ):
                    high13(0, j)
                high2(0)
                with act.Fori(0, NRB - 1, 1) as n:
                    body(n, True)
                body(NRB - 1, False)

            @block.vector
            def _(dve):
                def rows(n):
                    for kt in range(KT):
                        dve.wait_ge(s_xh, KT * n + kt + 1)
                        dve.tensor_tensor(x_lo[:, kt, ds(n % 2, 1)], p_t[kt][:, :].unsqueeze(1), x_hi[:, kt, ds(n % 2, 1)].bitcast(F32),
                                          ALU.subtract).then_inc(s_xl, 1)

                def body(n, parity, more):
                    def bias(j, q):
                        return b13[:, ds(n % 2, 1), 4 * j + q]

                    dve.wait_ge(s_b, 16 * (n + 1))
                    for j in range(NJ):
                        dve_inner(dve, u, s, n, j, bias)
                        if more and j == 1:
                            rows(n + 1)
                    dve.wait_ge(s.w2[NJ - 1], n + 1)
                    dve.wait_ge(s_y[parity], 16 * (n // 2) if isinstance(n, int) else 8 * (n - parity))
                    for t in range(BT):
                        dve.tensor_copy(y_out[:, parity, t], u.p_y[:, t]).then_inc(s.out, 1)

                rows(0)
                with dve.Fori(0, NRB // 2 - 1, 1) as m:
                    body(2 * m, 0, True)
                    body(2 * m + 1, 1, True)
                body(NRB - 2, 0, True)
                body(NRB - 1, 1, False)


def combine_stage(chip, route, slot_y):
    nc = chip.nc
    RING = 8
    with ExitStack() as ctx:
        sem = stage_semaphores(nc, ctx)
        rows = ctx.enter_context(nc.sbuf_tensor("expert_rows", [P, RING, TOPK, D], F32))
        s_got = [sem(f"rows_gathered{r}") for r in range(RING)]
        s_add = sem("rows_added")
        with nc.Block() as block:
            @block.gpsimd
            def _(pool):
                for t in range(NT):
                    if t >= RING:
                        pool.wait_ge(s_add, TOPK * (t - RING + 1))
                    for c in range(TOPK):
                        pool.indirect_dma_start(rows[:, t % RING, c], None, slot_y, bass.IndirectOffsetOnAxis(ap=route.slot[:, c, t:t + 1], axis=0)).then_inc(s_got[t % RING], 16)

            @block.vector
            def _(dve):
                for t in range(NT):
                    dve.wait_ge(s_got[t % RING], 16 * TOPK * (t // RING + 1))
                    for c in range(TOPK):
                        if c:
                            dve.wait_ge(s_add, TOPK * t + c)
                        dve.scalar_tensor_tensor(out=chip.h[:, t], in0=rows[:, t % RING, c], scalar=route.weight[:, c, t:t + 1], in1=chip.h[:, t],
                                                 op0=ALU.mult, op1=ALU.add).then_inc(s_add, 1)
                dve.wait_ge(s_add, TOPK * NT)


def ring_block(part, kt, i, first=1):
    return part[:, kt, ds(BI * (i % 2), BI), first:first + S]


def by_image(tile):
    return tile.rearrange("p (b s) -> p b s", b=BI)


def time_mix_stage(chip, a, x1, mv1):
    nc = chip.nc
    KV = 3
    NO_STATE = -1e38
    with ExitStack() as ctx:
        def sb(name, shape, dt=F32):
            return ctx.enter_context(nc.sbuf_tensor(name, shape, dt))

        def ps(name, shape):
            return ctx.enter_context(nc.psum_tensor(name, shape, F32))

        sem = stage_semaphores(nc, ctx)

        x_hi = sb("xa_hi", [P, KT, 2 * BI, XS], F32R)
        x_lo = sb("xa_lo", [P, KT, 2 * BI, XS], F32R)
        wm_hi = sb("wm_hi", [P, KT, 2, KV, D], F32R)
        wm_lo = sb("wm_lo", [P, KT, 2, KV, D], F32R)
        wo_hi = sb("wo_hi", [P, KT, D], F32R)
        wo_lo = sb("wo_lo", [P, KT, D], F32R)
        vecs = sb("vecs", [P, KT, 8])
        one_m = sb("one_m", [P, KT, KV])
        decay = sb("decay", [P, KT])
        rstd = sb("rstd1", [P, 2, NT])
        s_vec = sem("vectors_loaded")
        s_pd = sem("mix_prep_dve")
        s_pa = sem("mix_prep_act")
        s_bs = sem("variance_ready1")
        h_stats = TileStats("h_stats", sb, sem)
        x1_stats = TileStats("x1_stats", sb, sem)

        with nc.sbuf_tensor("wm_raw", [P, KT, KV, D], F32) as w_raw, nc.sbuf_tensor("wo_raw", [P, KT, D], F32) as wo_raw, \
                nc.sbuf_tensor("wm_f", [P, KT, 2, KV, D], F32) as w_f, nc.Block() as block:
            @block.sync
            def _(sp):
                for dst, src in ((vecs[:], a["mix_vecs"].rearrange("(k p) v -> p k v", p=P)),
                                 (w_raw[:], a["w_kvr"].rearrange("(k p) (v o) -> p k v o", p=P, v=KV)),
                                 (wo_raw[:], a["w_o"].rearrange("(k p) o -> p k o", p=P))):
                    sp.dma_start(dst, src).then_inc(s_vec, 16)

            @block.scalar
            def _(act):
                act.wait_ge(s_vec, 48)
                act.activation(decay[:, :], vecs[:, :, 5], ACT.Exp).then_inc(s_pa, 1)
                act.wait_ge(s_pd, 1)
                act.activation(rstd[:], rstd[:], ACT.Sqrt).then_inc(s_pa, 1)

            @block.vector
            def _(dve):
                with dve.Fori(0, NB, 1) as i:
                    h_stats.block(dve, chip.h, chip.mv, i)
                h_stats.finish(dve)
                dve.tensor_scalar(rstd[:, 0], chip.mv[:, :, 1], LN_EPS, None, ALU.add).then_inc(s_bs, 1)
                dve.wait_ge(s_bs, 1)
                dve.scalar_tensor_tensor(out=rstd[:, 1], in0=rstd[:, 0], scalar=LN_EPS, in1=chip.mv[:, :, 1], op0=ALU.mult, op1=ALU.add).then_inc(s_pd, 1)
                dve.wait_ge(s_pa, 2)
                dve.reciprocal(rstd[:], rstd[:]).then_inc(s_pd, 1)
                dve.tensor_scalar(decay[:, :], decay[:, :], -1.0, None, ALU.mult).then_inc(s_pd, 1)
                dve.tensor_scalar(one_m[:], vecs[:, :, 0:KV], -1.0, 1.0, ALU.mult, ALU.add).then_inc(s_pd, 1)
                dve.memset(x_hi[:, :, :, 0:1].bitcast(F32), 0.0).then_inc(s_pd, 1)
                dve.memset(x_lo[:, :, :, 0:1].bitcast(F32), 0.0).then_inc(s_pd, 1)
                dve.wait_ge(s_pd, 4)
                for k in range(KT):
                    for v in range(KV):
                        dve.tensor_scalar(w_f[:, k, 0, v], w_raw[:, k, v], vecs[:, k, v:v + 1], None, ALU.mult).then_inc(s_pd, 1)
                        dve.tensor_scalar(w_f[:, k, 1, v], w_raw[:, k, v], one_m[:, k, v:v + 1], None, ALU.mult).then_inc(s_pd, 1)
                dve.wait_ge(s_pd, 6 + 2 * KT * KV)
                dve.tensor_copy(wm_hi[:].rearrange("p k m v d -> p (k m v d)"), w_f[:].rearrange("p k m v d -> p (k m v d)")).then_inc(s_pd, 1)
                dve.tensor_copy(wo_hi[:], wo_raw[:]).then_inc(s_pd, 1)
                dve.wait_ge(s_pd, 6 + 2 * KT * KV + 2)
                dve.tensor_tensor(wm_lo[:].rearrange("p k m v d -> p (k m v d)"), w_f[:].rearrange("p k m v d -> p (k m v d)"),
                                  wm_hi[:].bitcast(F32).rearrange("p k m v d -> p (k m v d)"), ALU.subtract).then_inc(s_pd, 1)
                dve.tensor_tensor(wo_lo[:], wo_raw[:], wo_hi[:].bitcast(F32), ALU.subtract).then_inc(s_pd, 1)

        def pair(name, shape):
            return [sb(f"{name}{m}", shape) for m in range(KT)]

        xn = sb("xn1", [P, BT, D])
        xa = sb("xa", [P, KT, BLK])
        key, val, gate = pair("key", [P, BLK]), pair("val", [P, BLK]), pair("gate", [P, BLK])
        top = pair("top_state", [P, BI, S + 1])
        keep, add = pair("keep", [P, BLK]), pair("add", [P, BLK])
        mix = pair("mix", [P, 2, BLK])
        addv = pair("addv", [P, BLK])
        num_s, den_s = pair("num_state", [P, BI, S + 1]), pair("den_state", [P, BI, S + 1])
        rw_hi = sb("rw_hi", [P, KT, BLK], F32R)
        rw_lo = sb("rw_lo", [P, KT, BLK], F32R)
        p_t = [ps(f"p_t1_{k}", [P, BLK]) for k in range(KT)]
        p_j = [ps(f"p_j1_{k}", [P, BLK]) for k in range(4)]
        p_y = ps("p_y1", [P, BT, D])
        BANK = [0, 1, 2, 3, 0, 1]

        s_x1 = sem("x1_ready")
        s_xn = sem("xn1_ready")
        s_tr = sem("transposed1")
        s_xa = sem("xa_ready")
        s_xh = sem("xa_hi_ready")
        s_xl = sem("xa_lo_ready")
        s_pj = sem("kvr_projected")
        s_kv = sem("kvr_kept")
        s_top = sem("top_scanned")
        s_kd = sem("keep_exponent")
        s_ad = sem("add_exponent")
        s_md = sem("mix_exponents")
        s_ch = sem("mix_chain")
        s_ke = sem("keep_ready")
        s_ae = sem("add_ready")
        s_me = sem("mix_ready")
        s_av = sem("addv_ready")
        s_sc = sem("states_scanned")
        s_n2 = sem("token_part_ready")
        s_nd = sem("num_den_chain")
        s_dn = sem("den_ready")
        s_ln = sem("log_den_ready")
        s_y0 = sem("first_guess_ready")
        s_q = sem("gated_num_ready")
        s_nw = sem("newton_chain")
        s_rw = sem("rwkv_ready")
        s_rh = sem("rwkv_hi_ready")
        s_rl = sem("rwkv_lo_ready")
        s_y = sem("wo_applied")
        s_xu = sem("x1_updated")
        s_zero = sem("initial_states")

        with nc.Block() as block:
            @block.tensor
            def _(pe):
                def transposes(i):
                    pe.wait_ge(s_xn, BT * (i + 1))
                    pe.wait_ge(s_xa, KT * i)
                    for kt in range(KT):
                        for t in range(BT):
                            mm = pe.transpose(p_t[kt][:, t * P:(t + 1) * P], xn[:, t, kt * P:(kt + 1) * P], chip.ident[:, :])
                        mm.then_inc(s_tr, 1)

                def back(i):
                    pe.wait_ge(s_xl, KT * (i + 1))
                    for n in range(2 * KV):
                        m, v = n // KV, n % KV
                        pe.wait_ge(s_kv, 6 * i + max(n - 3, 0))
                        w, x = [], []
                        for k in range(KT):
                            for shifted in range(2):
                                w.append((wm_hi[:, k, shifted, v, m * P:(m + 1) * P], wm_lo[:, k, shifted, v, m * P:(m + 1) * P]))
                                x.append((ring_block(x_hi, k, i, 1 - shifted), ring_block(x_lo, k, i, 1 - shifted)))
                        split_matmuls(pe, p_j[BANK[n]][:, :], w, x).then_inc(s_pj, 1)
                    pe.wait_ge(s_rl, KT * (i + 1))
                    pe.wait_ge(s_xu, BT * i)
                    for t in range(BT):
                        split_matmuls(pe, p_y[:, t], [(rw_hi[:, k, t * P:(t + 1) * P], rw_lo[:, k, t * P:(t + 1) * P]) for k in range(KT)],
                                      [(wo_hi[:, k], wo_lo[:, k]) for k in range(KT)]).then_inc(s_y, 1)

                transposes(0)
                with pe.Fori(0, NB - 1, 1) as i:
                    transposes(i + 1)
                    back(i)
                back(NB - 1)

            @block.scalar
            def _(act):
                def front(i):
                    act.wait_ge(s_xl, KT * i)
                    for kt in range(KT):
                        act.wait_ge(s_tr, KT * i + kt + 1)
                        act.activation(xa[:, kt], p_t[kt][:, :], ACT.Identity, bias=vecs[:, kt, 4:5], scale=vecs[:, kt, 3:4]).then_inc(s_xa, 1)
                    for kt in range(KT):
                        act.wait_ge(s_xa, KT * i + kt + 1)
                        act.activation(ring_block(x_hi, kt, i), by_image(xa[:, kt]), ACT.Copy).then_inc(s_xh, 1)

                def back(i):
                    act.wait_ge(s_rw, KT * i)
                    for m in range(KT):
                        for v, dst in enumerate((key[m], val[m])):
                            act.wait_ge(s_pj, 6 * i + KV * m + v + 1)
                            act.activation(dst[:, :], p_j[BANK[KV * m + v]][:, :], ACT.Copy).then_inc(s_kv, 1)
                        act.wait_ge(s_pj, 6 * i + KV * m + 3)
                        act.activation(gate[m][:, :], p_j[BANK[KV * m + 2]][:, :], ACT.Sigmoid).then_inc(s_kv, 1)
                    for m in range(KT):
                        act.wait_ge(s_kd, KT * i + m + 1)
                        act.activation(keep[m][:, :], keep[m][:, :], ACT.Exp).then_inc(s_ke, 1)
                        act.wait_ge(s_ad, KT * i + m + 1)
                        act.activation(add[m][:, :], add[m][:, :], ACT.Exp).then_inc(s_ae, 1)
                        act.wait_ge(s_md, KT * i + m + 1)
                        act.activation(mix[m][:], mix[m][:], ACT.Exp).then_inc(s_me, 1)
                    for m in range(KT):
                        act.wait_ge(s_dn, KT * i + m + 1)
                        act.activation(key[m][:, :], mix[m][:, 0], ACT.Ln).then_inc(s_ln, 1)
                        act.wait_ge(s_ln, KT * i + m + 1)
                        act.activation(key[m][:, :], key[m][:, :], ACT.Exp, scale=-1.0).then_inc(s_y0, 1)
                    for m in range(KT):
                        act.wait_ge(s_rw, KT * i + m + 1)
                        act.wait_ge(s_y, BT * i)
                        act.activation(rw_hi[:, m], addv[m][:, :], ACT.Copy).then_inc(s_rh, 1)

                front(0)
                with act.Fori(0, NB - 1, 1) as i:
                    front(i + 1)
                    back(i)
                back(NB - 1)

            @block.gpsimd
            def _(pool):
                def front(i):
                    for kt in range(KT):
                        pool.wait_ge(s_xh, KT * i + kt + 1)
                        pool.tensor_tensor(ring_block(x_lo, kt, i), by_image(xa[:, kt]), ring_block(x_hi, kt, i).bitcast(F32), ALU.subtract).then_inc(s_xl, 1)

                def back(i):
                    for m in range(KT):
                        pool.wait_ge(s_top, BI * (KT * i + m + 1))
                        pool.tensor_tensor(by_image(add[m][:, :]), by_image(key[m][:, :]), top[m][:, :, 1:], ALU.subtract).then_inc(s_ad, 1)
                    for m in range(KT):
                        pool.wait_ge(s_ae, KT * i + m + 1)
                        pool.tensor_tensor(addv[m][:, :], add[m][:, :], val[m][:, :], ALU.mult).then_inc(s_av, 1)
                    for m in range(KT):
                        pool.wait_ge(s_me, KT * i + m + 1)
                        pool.wait_ge(s_av, KT * i + m + 1)
                        pool.tensor_tensor(val[m][:, :], mix[m][:, 1], val[m][:, :], ALU.mult).then_inc(s_n2, 1)
                    for m in range(KT):
                        pool.wait_ge(s_rh, KT * i + m + 1)
                        pool.tensor_tensor(rw_lo[:, m], addv[m][:, :], rw_hi[:, m].bitcast(F32), ALU.subtract).then_inc(s_rl, 1)

                front(0)
                with pool.Fori(0, NB - 1, 1) as i:
                    front(i + 1)
                    back(i)
                back(NB - 1)

            @block.vector
            def _(dve):
                for m in range(KT):
                    dve.memset(top[m][:, :, 0:1], NO_STATE).then_inc(s_zero, 1)
                    dve.memset(num_s[m][:, :, 0:1], 0.0).then_inc(s_zero, 1)
                    dve.memset(den_s[m][:, :, 0:1], 0.0).then_inc(s_zero, 1)
                dve.wait_ge(s_zero, 3 * KT)

                def front(i):
                    dve.wait_ge(s_tr, KT * i)
                    for t in range(BT):
                        tile = ds(BT * i + t, 1)
                        dve.tensor_scalar(xn[:, t:t + 1], chip.h[:, tile], chip.mv[:, tile, 0], rstd[:, 1, tile], ALU.subtract, ALU.mult).then_inc(s_xn, 1)
                    for t in range(BT):
                        tile = ds(BT * i + t, 1)
                        dve.tensor_scalar(x1[:, tile], chip.h[:, tile], chip.mv[:, tile, 0], rstd[:, 0, tile], ALU.subtract, ALU.mult).then_inc(s_x1, 1)

                def back(i):
                    two = KT * i
                    for m in range(KT):
                        u = vecs[:, m, 6:7]
                        before, after = top[m][:, :, 0:S], top[m][:, :, 1:]
                        dve.wait_ge(s_kv, 6 * i + KV * m + 1)
                        for b in range(BI):
                            dve.tensor_tensor_scan(top[m][:, b, 1:], decay[:, m:m + 1].to_broadcast([P, S]), key[m][:, b * S:(b + 1) * S],
                                                   initial=NO_STATE, op0=ALU.add, op1=ALU.max).then_inc(s_top, 1)
                        dve.wait_ge(s_top, BI * (two + m + 1))
                        dve.scalar_tensor_tensor(out=by_image(keep[m][:, :]), in0=before, scalar=decay[:, m:m + 1], in1=after,
                                                 op0=ALU.add, op1=ALU.subtract).then_inc(s_kd, 1)
                        dve.scalar_tensor_tensor(out=by_image(mix[m][:, 1]), in0=by_image(key[m][:, :]), scalar=u, in1=before,
                                                 op0=ALU.add, op1=ALU.subtract).then_inc(s_ch, 1)
                        dve.wait_ge(s_ch, 2 * (two + m) + 1)
                        dve.tensor_scalar(mix[m][:, 0], mix[m][:, 1], 0.0, -1.0, ALU.max, ALU.mult).then_inc(s_ch, 1)
                        dve.wait_ge(s_ch, 2 * (two + m) + 2)
                        dve.tensor_scalar(mix[m][:, 1], mix[m][:, 1], 0.0, None, ALU.min).then_inc(s_md, 1)
                    for m in range(KT):
                        dve.wait_ge(s_ke, two + m + 1)
                        dve.wait_ge(s_ae, two + m + 1)
                        for b in range(BI):
                            dve.tensor_tensor_scan(den_s[m][:, b, 1:], keep[m][:, b * S:(b + 1) * S], add[m][:, b * S:(b + 1) * S],
                                                   initial=0.0, op0=ALU.mult, op1=ALU.add).then_inc(s_sc, 1)
                        dve.wait_ge(s_av, two + m + 1)
                        for b in range(BI):
                            dve.tensor_tensor_scan(num_s[m][:, b, 1:], keep[m][:, b * S:(b + 1) * S], addv[m][:, b * S:(b + 1) * S],
                                                   initial=0.0, op0=ALU.mult, op1=ALU.add).then_inc(s_sc, 1)
                    for m in range(KT):
                        base = 3 * (two + m)
                        dve.wait_ge(s_me, two + m + 1)
                        dve.wait_ge(s_sc, 2 * BI * (two + m + 1))
                        dve.tensor_tensor(by_image(addv[m][:, :]), by_image(mix[m][:, 0]), num_s[m][:, :, 0:S], ALU.mult).then_inc(s_nd, 1)
                        dve.tensor_tensor(by_image(mix[m][:, 0]), by_image(mix[m][:, 0]), den_s[m][:, :, 0:S], ALU.mult).then_inc(s_nd, 1)
                        dve.wait_ge(s_nd, base + 2)
                        dve.tensor_tensor(mix[m][:, 0], mix[m][:, 0], mix[m][:, 1], ALU.add).then_inc(s_dn, 1)
                        dve.wait_ge(s_n2, two + m + 1)
                        dve.tensor_tensor(addv[m][:, :], addv[m][:, :], val[m][:, :], ALU.add).then_inc(s_nd, 1)
                        dve.wait_ge(s_nd, base + 3)
                        dve.wait_ge(s_kv, 6 * i + KV * m + 3)
                        dve.tensor_tensor(addv[m][:, :], addv[m][:, :], gate[m][:, :], ALU.mult).then_inc(s_q, 1)
                    for m in range(KT):
                        base = 2 * (two + m)
                        dve.wait_ge(s_y0, two + m + 1)
                        dve.wait_ge(s_dn, two + m + 1)
                        dve.tensor_tensor(mix[m][:, 0], mix[m][:, 0], key[m][:, :], ALU.mult).then_inc(s_nw, 1)
                        dve.wait_ge(s_nw, base + 1)
                        dve.scalar_tensor_tensor(out=mix[m][:, 0], in0=mix[m][:, 0], scalar=2.0, in1=key[m][:, :], op0=ALU.subtract, op1=ALU.mult).then_inc(s_nw, 1)
                        dve.wait_ge(s_nw, base + 2)
                        dve.wait_ge(s_q, two + m + 1)
                        dve.scalar_tensor_tensor(out=addv[m][:, :], in0=addv[m][:, :], scalar=-1.0, in1=mix[m][:, 0], op0=ALU.mult, op1=ALU.mult).then_inc(s_rw, 1)
                    for t in range(BT):
                        tile = ds(BT * i + t, 1)
                        dve.wait_ge(s_y, BT * i + t // 2 * 2 + 2)
                        dve.tensor_tensor(x1[:, tile], x1[:, tile], p_y[:, t:t + 1], ALU.add).then_inc(s_xu, 1)
                    dve.wait_ge(s_xu, BT * (i + 1))
                    x1_stats.block(dve, x1, mv1, i)

                front(0)
                with dve.Fori(0, NB - 1, 1) as i:
                    front(i + 1)
                    back(i)
                back(NB - 1)
                x1_stats.finish(dve)


def channel_mix_stage(chip, a, x1, mv1):
    nc = chip.nc
    NH = 4 * D // P
    with ExitStack() as ctx:
        def sb(name, shape, dt=F32):
            return ctx.enter_context(nc.sbuf_tensor(name, shape, dt))

        def ps(name, shape):
            return ctx.enter_context(nc.psum_tensor(name, shape, F32))

        sem = stage_semaphores(nc, ctx)

        wk_hi = sb("wk_hi", [P, KT, NH * P], F32R)
        wk_lo = sb("wk_lo", [P, KT, NH * P], F32R)
        wv_hi = sb("wv_hi", [P, NH, D], F32R)
        wv_lo = sb("wv_lo", [P, NH, D], F32R)
        wr_hi = sb("wr_hi", [P, KT, D], F32R)
        wr_lo = sb("wr_lo", [P, KT, D], F32R)
        vecs = sb("vecs2", [P, KT, 4])
        one_m = sb("one_m2", [P, KT, 2])
        rstd = sb("rstd2", [P, NT])
        xc = sb("xc", [P, KT, BI, XS])
        s_vec = sem("vectors2_loaded")
        s_pd = sem("cm_prep_dve")
        s_pa = sem("cm_prep_act")

        with nc.sbuf_tensor("wk_raw", [P, KT, NH * P], F32) as wk_raw, nc.sbuf_tensor("wv_raw", [P, NH, D], F32) as wv_raw, \
                nc.sbuf_tensor("wr_raw", [P, KT, D], F32) as wr_raw, nc.Block() as block:
            @block.sync
            def _(sp):
                for dst, src in ((vecs[:], a["cm_vecs"].rearrange("(k p) v -> p k v", p=P)),
                                 (wr_raw[:], a["w_r2"].rearrange("(k p) o -> p k o", p=P)),
                                 (wk_raw[:], a["w_k2"].rearrange("(k p) o -> p k o", p=P)),
                                 (wv_raw[:], a["w_v2"].rearrange("(k p) o -> p k o", p=P))):
                    sp.dma_start(dst, src).then_inc(s_vec, 16)

            @block.scalar
            def _(act):
                act.wait_ge(s_pd, 1)
                act.activation(rstd[:, :], rstd[:, :], ACT.Sqrt).then_inc(s_pa, 1)
                act.wait_ge(s_vec, 64)
                act.activation(wk_hi[:], wk_raw[:], ACT.Copy).then_inc(s_pa, 1)
                act.activation(wv_hi[:], wv_raw[:], ACT.Copy).then_inc(s_pa, 1)
                act.activation(wr_hi[:], wr_raw[:], ACT.Copy).then_inc(s_pa, 1)

            @block.vector
            def _(dve):
                dve.tensor_scalar(rstd[:, :], mv1[:, :, 1], LN_EPS, None, ALU.add).then_inc(s_pd, 1)
                dve.memset(xc[:, :, :, 0:1], 0.0).then_inc(s_pd, 1)
                dve.wait_ge(s_pa, 1)
                dve.reciprocal(rstd[:, :], rstd[:, :]).then_inc(s_pd, 1)
                dve.wait_ge(s_vec, 64)
                dve.tensor_scalar(one_m[:], vecs[:, :, 0:2], -1.0, 1.0, ALU.mult, ALU.add).then_inc(s_pd, 1)
                for n, (lo, raw, hi) in enumerate(((wk_lo, wk_raw, wk_hi), (wv_lo, wv_raw, wv_hi), (wr_lo, wr_raw, wr_hi))):
                    dve.wait_ge(s_pa, n + 2)
                    dve.tensor_tensor(lo[:], raw[:], hi[:].bitcast(F32), ALU.subtract).then_inc(s_pd, 1)

        xn = sb("xn2", [P, BT, D])
        old = sb("old", [P, 2, KT, BLK])
        mixed = sb("mixed", [P, 2, KT, BLK])
        xk_hi = sb("xk_hi", [P, KT, 2, BLK], F32R)
        xk_lo = sb("xk_lo", [P, KT, 2, BLK], F32R)
        xr_hi = sb("xr_hi", [P, KT, BLK], F32R)
        xr_lo = sb("xr_lo", [P, KT, BLK], F32R)
        pos = sb("pos", [P, 2, BLK])
        sqr = sb("sqr", [P, 2, BLK])
        hid_hi = sb("hid2_hi", [P, NH, BLK], F32R)
        hid_lo = sb("hid2_lo", [P, NH, BLK], F32R)
        gate = sb("gate2", [P, BT, D])
        stats = TileStats("h_stats2", sb, sem)
        p_t = [ps(f"p_t2_{k}", [P, BLK]) for k in range(KT)]
        p_u = [ps(f"p_u2_{k}", [P, BLK]) for k in range(2)]
        p_y = ps("p_y2", [P, BT, D])
        p_r = ps("p_r2", [P, BT, D])

        s_xn = sem("xn2_ready")
        s_tr = sem("transposed2")
        s_xc = sem("xc_ready")
        s_old = sem("old_ready")
        s_mx = sem("mixed_ready")
        s_xh = sem("x2_hi_ready")
        s_xl = sem("x2_lo_ready")
        s_r = sem("r_projected")
        s_g = sem("gate2_ready")
        s_up = sem("up_projected")
        s_po = sem("relu_ready")
        s_sq = sem("square_ready")
        s_hh = sem("hid2_hi_ready")
        s_hl = sem("hid2_lo_ready")
        s_dn = [sem(f"down_applied{j}") for j in range(NH)]
        s_hx = sem("h_plus_x1")
        s_ry = sem("gated")
        s_h = sem("h_updated2")

        with nc.Block() as block:
            @block.tensor
            def _(pe):
                def transposes(i):
                    pe.wait_ge(s_xn, BT * (i + 1))
                    pe.wait_ge(s_xc, KT * i)
                    for kt in range(KT):
                        for t in range(BT):
                            mm = pe.transpose(p_t[kt][:, t * P:(t + 1) * P], xn[:, t, kt * P:(kt + 1) * P], chip.ident[:, :])
                        mm.then_inc(s_tr, 1)

                def up(i, j):
                    if j >= 2:
                        pe.wait_ge(s_po, NH * i + j - 1)
                    else:
                        pe.wait_ge(s_po, NH * i)
                    split_matmuls(pe, p_u[j % 2][:, :], [(wk_hi[:, k, j * P:(j + 1) * P], wk_lo[:, k, j * P:(j + 1) * P]) for k in range(KT)],
                                  [(xk_hi[:, k, ds(i % 2, 1)], xk_lo[:, k, ds(i % 2, 1)]) for k in range(KT)]).then_inc(s_up, 1)

                def down(i, j):
                    pe.wait_ge(s_hl, NH * i + j + 1)
                    if j == 0:
                        pe.wait_ge(s_ry, BT * i)
                    for t in range(BT):
                        hi, lo = hid_hi[:, j, t * P:(t + 1) * P], hid_lo[:, j, t * P:(t + 1) * P]
                        pe.matmul(p_y[:, t], hi, wv_hi[:, j], start=(j == 0 and t % 2 == 0), stop=False, skip_group_check=True)
                        pe.matmul(p_y[:, t], hi, wv_lo[:, j], start=False, stop=False, skip_group_check=True)
                        mm = pe.matmul(p_y[:, t], lo, wv_hi[:, j], start=False, stop=(j == NH - 1), skip_group_check=True)
                    mm.then_inc(s_dn[j], 1)

                def back(i):
                    pe.wait_ge(s_xl, 2 * KT * (i + 1))
                    pe.wait_ge(s_g, 2 * i)
                    for t in range(BT):
                        mm = split_matmuls(pe, p_r[:, t], [(xr_hi[:, k, t * P:(t + 1) * P], xr_lo[:, k, t * P:(t + 1) * P]) for k in range(KT)],
                                           [(wr_hi[:, k], wr_lo[:, k]) for k in range(KT)])
                        if t % 2:
                            mm.then_inc(s_r, 1)
                    up(i, 0)
                    for j in range(1, NH):
                        up(i, j)
                        down(i, j - 1)
                    down(i, NH - 1)

                transposes(0)
                with pe.Fori(0, NB - 1, 1) as i:
                    transposes(i + 1)
                    back(i)
                back(NB - 1)

            @block.scalar
            def _(act):
                def front(i):
                    act.wait_ge(s_mx, 2 * KT * i)
                    for kt in range(KT):
                        act.wait_ge(s_tr, KT * i + kt + 1)
                        act.activation(xc[:, kt, :, 1:1 + S], by_image(p_t[kt][:, :]), ACT.Identity, bias=vecs[:, kt, 3:4], scale=vecs[:, kt, 2:3]).then_inc(s_xc, 1)
                    act.wait_ge(s_xc, KT * (i + 1))
                    for kt in range(KT):
                        for v in range(2):
                            act.activation(by_image(old[:, v, kt]), xc[:, kt, :, 0:S], ACT.Copy, scale=one_m[:, kt, v:v + 1]).then_inc(s_old, 1)
                    act.wait_ge(s_r, 2 * i)
                    for kt in range(KT):
                        for v in range(2):
                            act.wait_ge(s_mx, 2 * KT * i + 2 * kt + v + 1)
                            dst = xk_hi[:, kt, ds(i % 2, 1)] if v == 0 else xr_hi[:, kt:kt + 1]
                            act.activation(dst, mixed[:, v, kt:kt + 1], ACT.Copy).then_inc(s_xh, 1)

                def back(i):
                    act.wait_ge(s_h, BT * i)
                    for n in range(2):
                        act.wait_ge(s_r, 2 * i + n + 1)
                        act.activation(gate[:, 2 * n:2 * n + 2], p_r[:, 2 * n:2 * n + 2], ACT.Sigmoid).then_inc(s_g, 1)
                    for j in range(NH):
                        act.wait_ge(s_up, NH * i + j + 1)
                        act.wait_ge(s_sq, NH * i + max(j - 1, 0))
                        act.activation(pos[:, j % 2], p_u[j % 2][:, :], ACT.Relu).then_inc(s_po, 1)
                        if j:
                            act.wait_ge(s_sq, NH * i + j)
                            act.wait_ge(s_dn[j - 1], i)
                            act.activation(hid_hi[:, j - 1], sqr[:, (j - 1) % 2], ACT.Copy).then_inc(s_hh, 1)
                    act.wait_ge(s_sq, NH * i + NH)
                    act.wait_ge(s_dn[NH - 1], i)
                    act.activation(hid_hi[:, NH - 1], sqr[:, (NH - 1) % 2], ACT.Copy).then_inc(s_hh, 1)

                front(0)
                with act.Fori(0, NB - 1, 1) as i:
                    front(i + 1)
                    back(i)
                back(NB - 1)

            @block.gpsimd
            def _(pool):
                def front(i):
                    for kt in range(KT):
                        for v in range(2):
                            pool.wait_ge(s_xh, 2 * KT * i + 2 * kt + v + 1)
                            hi = xk_hi[:, kt, ds(i % 2, 1)] if v == 0 else xr_hi[:, kt:kt + 1]
                            dst = xk_lo[:, kt, ds(i % 2, 1)] if v == 0 else xr_lo[:, kt:kt + 1]
                            pool.tensor_tensor(dst, mixed[:, v, kt:kt + 1], hi.bitcast(F32), ALU.subtract).then_inc(s_xl, 1)
                    for t in range(BT):
                        tile = ds(BT * i + t, 1)
                        pool.tensor_tensor(chip.h[:, tile], chip.h[:, tile], x1[:, tile], ALU.add).then_inc(s_hx, 1)

                with pool.Fori(0, NB, 1) as i:
                    front(i)

            @block.vector
            def _(dve):
                def front(i):
                    dve.wait_ge(s_tr, KT * i)
                    for t in range(BT):
                        tile = ds(BT * i + t, 1)
                        dve.tensor_scalar(xn[:, t:t + 1], x1[:, tile], mv1[:, tile, 0], rstd[:, tile], ALU.subtract, ALU.mult).then_inc(s_xn, 1)
                    dve.wait_ge(s_xl, 2 * KT * i)
                    for kt in range(KT):
                        for v in range(2):
                            dve.wait_ge(s_old, 2 * KT * i + 2 * kt + v + 1)
                            dve.scalar_tensor_tensor(out=by_image(mixed[:, v, kt]), in0=xc[:, kt, :, 1:1 + S], scalar=vecs[:, kt, v:v + 1],
                                                     in1=by_image(old[:, v, kt]), op0=ALU.mult, op1=ALU.add).then_inc(s_mx, 1)

                def back(i):
                    def low(j):
                        dve.wait_ge(s_hh, NH * i + j + 1)
                        dve.tensor_tensor(hid_lo[:, j], sqr[:, j % 2], hid_hi[:, j].bitcast(F32), ALU.subtract).then_inc(s_hl, 1)

                    for j in range(NH):
                        dve.wait_ge(s_po, NH * i + j + 1)
                        dve.wait_ge(s_hl, NH * i + max(j - 1, 0))
                        dve.tensor_tensor(sqr[:, j % 2], pos[:, j % 2], pos[:, j % 2], ALU.mult).then_inc(s_sq, 1)
                        if j:
                            low(j - 1)
                    low(NH - 1)
                    dve.wait_ge(s_g, 2 * (i + 1))
                    dve.wait_ge(s_dn[NH - 1], i + 1)
                    for t in range(BT):
                        dve.tensor_tensor(gate[:, t], gate[:, t], p_y[:, t], ALU.mult).then_inc(s_ry, 1)
                    dve.wait_ge(s_hx, BT * (i + 1))
                    for t in range(BT):
                        h = chip.h[:, ds(BT * i + t, 1)]
                        dve.wait_ge(s_ry, BT * i + t + 1)
                        dve.tensor_tensor(h, h, gate[:, t:t + 1], ALU.add).then_inc(s_h, 1)
                    dve.wait_ge(s_h, BT * (i + 1))
                    stats.block(dve, chip.h, chip.mv, i)

                front(0)
                with dve.Fori(0, NB - 1, 1) as i:
                    front(i + 1)
                    back(i)
                back(NB - 1)
                stats.finish(dve)


def ternary_stage(chip, a, out):
    nc = chip.nc
    EPS = 1e-8
    NH = 4 * D // P
    with ExitStack() as ctx:
        def sb(name, shape, dt=F32):
            return ctx.enter_context(nc.sbuf_tensor(name, shape, dt))

        def ps(name, shape):
            return ctx.enter_context(nc.psum_tensor(name, shape, F32))

        sem = stage_semaphores(nc, ctx)

        x_hi = sb("xt_hi", [P, KT, 2 * BI, XS], F32R)
        x_lo = sb("xt_lo", [P, KT, 2 * BI, XS], F32R)
        w_up = sb("w_up", [P, KT, NH * P], F32R)
        w_down = sb("w_down", [P, NH, D], F32R)
        ones = sb("ones3", [P, P])
        root = sb("root", [P, 2, NT])
        scale = sb("scale3", [P, NT])
        s_ld = sem("ternary_loaded")
        s_pd = sem("ternary_prep_dve")
        s_tot = sem("weight_sums")
        s_pa = sem("ternary_prep_act")

        with nc.sbuf_tensor("up_raw", [P, KT, NH * P], F32) as up_raw, nc.sbuf_tensor("down_raw", [P, NH, D], F32) as down_raw, \
                nc.sbuf_tensor("above", [P, KT * NH * P], F32) as above, nc.sbuf_tensor("below", [P, KT * NH * P], F32) as below, \
                nc.sbuf_tensor("abs_sum", [P, 2], F32) as abs_sum, nc.sbuf_tensor("limits", [P, 2, 2], F32) as limits, \
                nc.psum_tensor("total", [P, 2], F32) as total, nc.Block() as block:
            @block.sync
            def _(sp):
                for dst, src in ((up_raw[:], a["w_up"].rearrange("(k p) o -> p k o", p=P)),
                                 (down_raw[:], a["w_down"].rearrange("(k p) o -> p k o", p=P)), (ones[:], a["ones"])):
                    sp.dma_start(dst, src).then_inc(s_ld, 16)

            @block.tensor
            def _(pe):
                pe.wait_ge(s_pd, 2)
                pe.matmul(total[:, :], ones[:, :], abs_sum[:, :], start=True, stop=True).then_inc(s_tot, 1)

            @block.scalar
            def _(act):
                act.wait_ge(s_pa, 1)
                act.activation(root[:], root[:], ACT.Sqrt).then_inc(s_pa, 1)

            @block.vector
            def _(dve):
                dve.wait_ge(s_ld, 48)
                for n, raw in enumerate((up_raw, down_raw)):
                    dve.tensor_reduce(abs_sum[:, n:n + 1], raw[:], AX.XY, ALU.add, apply_absolute_value=True).then_inc(s_pd, 1)
                dve.tensor_copy(root[:, 0], chip.mv[:, :, 1]).then_inc(s_pd, 1)
                dve.wait_ge(s_pd, 3)
                dve.tensor_scalar(root[:, 1], chip.mv[:, :, 1], LN_EPS, None, ALU.add).then_inc(s_pa, 1)
                dve.wait_ge(s_pa, 2)
                dve.scalar_tensor_tensor(out=scale[:, :], in0=root[:, 1], scalar=EPS, in1=root[:, 0], op0=ALU.mult, op1=ALU.add).then_inc(s_pd, 1)
                dve.wait_ge(s_pd, 4)
                dve.reciprocal(scale[:, :], scale[:, :]).then_inc(s_pd, 1)
                dve.wait_ge(s_tot, 1)
                half_mean = 0.5 / (D * NH * P)
                dve.tensor_scalar(limits[:, 0], total[:, :], half_mean, None, ALU.mult).then_inc(s_pd, 1)
                dve.tensor_scalar(limits[:, 1], total[:, :], -half_mean, None, ALU.mult).then_inc(s_pd, 1)
                n = 7
                for k, (raw, dst) in enumerate(((up_raw, w_up), (down_raw, w_down))):
                    flat = raw[:].rearrange("p a b -> p (a b)")
                    dve.wait_ge(s_pd, n)
                    dve.tensor_scalar(above[:, :], flat, limits[:, 0, k:k + 1], None, ALU.is_gt).then_inc(s_pd, 1)
                    dve.tensor_scalar(below[:, :], flat, limits[:, 1, k:k + 1], None, ALU.is_lt).then_inc(s_pd, 1)
                    dve.wait_ge(s_pd, n + 2)
                    dve.tensor_tensor(dst[:].rearrange("p a b -> p (a b)"), above[:, :], below[:, :], ALU.subtract).then_inc(s_pd, 1)
                    n += 3

        xn = sb("xn3", [P, BT, D])
        act_out = sb("act_out", [P, 2, BLK])
        squares = sb("squares", [P, 2, BLK])
        hid_hi = sb("hid3_hi", [P, NH, BLK], F32R)
        hid_lo = sb("hid3_lo", [P, NH, BLK], F32R)
        rms = sb("rms", [P, BT])
        p_t = [ps(f"p_t3_{k}", [P, BLK]) for k in range(KT)]
        p_u = [ps(f"p_u3_{k}", [P, BLK]) for k in range(2)]
        p_y = ps("p_y3", [P, BT, D])
        p_s = ps("p_s3", [P, BT])

        s_xn = sem("xn3_ready")
        s_tr = sem("transposed3")
        s_xh = sem("x3_hi_ready")
        s_xl = sem("x3_lo_ready")
        s_up = sem("up3_projected")
        s_ge = sem("gelu_ready")
        s_sq = sem("gelu_squared")
        s_hh = sem("hid3_hi_ready")
        s_hl = sem("hid3_lo_ready")
        s_ss = sem("squares_summed")
        s_dn = [sem(f"down3_applied{j}") for j in range(NH)]
        s_rt = sem("rms_ready")
        s_rc = sem("rms_chain")
        s_h = sem("h_updated3")
        s_o = sem("out_stored")

        with nc.Block() as block:
            @block.sync
            def _(sp):
                with sp.Fori(0, NB, 1) as i:
                    sp.wait_ge(s_h, BT * (i + 1))
                    sp.dma_start(out[ds(i * BLK, BLK), :].rearrange("(t p) c -> p t c", p=P), chip.h[:, ds(BT * i, BT)]).then_inc(s_o, 16)
                sp.wait_ge(s_o, 16 * NB)

            @block.tensor
            def _(pe):
                def transposes(i):
                    pe.wait_ge(s_xn, BT * (i + 1))
                    pe.wait_ge(s_xl, KT * i)
                    for kt in range(KT):
                        for t in range(BT):
                            mm = pe.transpose(p_t[kt][:, t * P:(t + 1) * P], xn[:, t, kt * P:(kt + 1) * P], chip.ident[:, :])
                        mm.then_inc(s_tr, 1)

                def up(i, j):
                    pe.wait_ge(s_ge, NH * i + max(j - 1, 0))
                    for k in range(KT):
                        w = w_up[:, k, j * P:(j + 1) * P]
                        pe.matmul(p_u[j % 2][:, :], w, ring_block(x_hi, k, i), start=(k == 0), stop=False)
                        mm = pe.matmul(p_u[j % 2][:, :], w, ring_block(x_lo, k, i), start=False, stop=(k == KT - 1))
                    mm.then_inc(s_up, 1)

                def down(i, j):
                    if j == 0:
                        pe.wait_ge(s_rt, i)
                        pe.wait_ge(s_rc, 3 * i)
                        pe.wait_ge(s_h, BT * i)
                    pe.wait_ge(s_sq, NH * i + j + 1)
                    for t in range(BT):
                        mm = pe.matmul(p_s[:, t:t + 1], squares[:, j % 2, t * P:(t + 1) * P], ones[:, 0:1],
                                       start=(j == 0 and t == 0), stop=(j == NH - 1), skip_group_check=True)
                    mm.then_inc(s_ss, 1)
                    pe.wait_ge(s_hl, NH * i + j + 1)
                    for t in range(BT):
                        pe.matmul(p_y[:, t], hid_hi[:, j, t * P:(t + 1) * P], w_down[:, j], start=(j == 0 and t % 2 == 0), stop=False, skip_group_check=True)
                        mm = pe.matmul(p_y[:, t], hid_lo[:, j, t * P:(t + 1) * P], w_down[:, j], start=False, stop=(j == NH - 1), skip_group_check=True)
                    mm.then_inc(s_dn[j], 1)

                def back(i):
                    pe.wait_ge(s_xl, KT * (i + 1))
                    up(i, 0)
                    for j in range(1, NH):
                        up(i, j)
                        down(i, j - 1)
                    down(i, NH - 1)

                transposes(0)
                with pe.Fori(0, NB - 1, 1) as i:
                    transposes(i + 1)
                    back(i)
                back(NB - 1)

            @block.scalar
            def _(act):
                def front(i):
                    for kt in range(KT):
                        act.wait_ge(s_tr, KT * i + kt + 1)
                        act.activation(ring_block(x_hi, kt, i), by_image(p_t[kt][:, :]), ACT.Copy).then_inc(s_xh, 1)

                def back(i):
                    def high(j):
                        act.wait_ge(s_ge, NH * i + j + 1)
                        act.wait_ge(s_dn[j], i)
                        act.activation(hid_hi[:, j], act_out[:, j % 2], ACT.Copy).then_inc(s_hh, 1)

                    for j in range(NH):
                        act.wait_ge(s_up, NH * i + j + 1)
                        act.wait_ge(s_hl, NH * i + max(j - 1, 0))
                        act.wait_ge(s_sq, NH * i + max(j - 1, 0))
                        act.activation(act_out[:, j % 2], p_u[j % 2][:, :], ACT.Gelu).then_inc(s_ge, 1)
                        high(j)
                    act.wait_ge(s_ss, NH * (i + 1))
                    act.wait_ge(s_h, BT * i)
                    act.activation(rms[:, :], p_s[:, :], ACT.Sqrt, scale=1.0 / (NH * P)).then_inc(s_rt, 1)

                front(0)
                with act.Fori(0, NB - 1, 1) as i:
                    front(i + 1)
                    back(i)
                back(NB - 1)

            @block.gpsimd
            def _(pool):
                with pool.Fori(0, NB, 1) as i:
                    for j in range(NH):
                        pool.wait_ge(s_ge, NH * i + j + 1)
                        pool.wait_ge(s_ss, NH * i + max(j - 1, 0))
                        pool.tensor_tensor(squares[:, j % 2], act_out[:, j % 2], act_out[:, j % 2], ALU.mult).then_inc(s_sq, 1)

            @block.vector
            def _(dve):
                def front(i):
                    dve.wait_ge(s_tr, KT * i)
                    for t in range(BT):
                        tile = ds(BT * i + t, 1)
                        dve.tensor_scalar(xn[:, t:t + 1], chip.h[:, tile], chip.mv[:, tile, 0], scale[:, tile], ALU.subtract, ALU.mult).then_inc(s_xn, 1)
                    for kt in range(KT):
                        dve.wait_ge(s_xh, KT * i + kt + 1)
                        dve.tensor_tensor(ring_block(x_lo, kt, i), by_image(p_t[kt][:, :]), ring_block(x_hi, kt, i).bitcast(F32), ALU.subtract).then_inc(s_xl, 1)

                def back(i):
                    for j in range(NH):
                        dve.wait_ge(s_hh, NH * i + j + 1)
                        dve.tensor_tensor(hid_lo[:, j], act_out[:, j % 2], hid_hi[:, j].bitcast(F32), ALU.subtract).then_inc(s_hl, 1)
                    dve.wait_ge(s_rt, i + 1)
                    dve.tensor_scalar(rms[:, :], rms[:, :], EPS, None, ALU.add).then_inc(s_rc, 1)
                    dve.wait_ge(s_rc, 3 * i + 1)
                    dve.reciprocal(rms[:, :], rms[:, :]).then_inc(s_rc, 1)
                    dve.wait_ge(s_rc, 3 * i + 2)
                    dve.wait_ge(s_dn[NH - 1], i + 1)
                    for t in range(BT):
                        h = chip.h[:, ds(BT * i + t, 1)]
                        dve.scalar_tensor_tensor(out=h, in0=p_y[:, t:t + 1], scalar=rms[:, t:t + 1], in1=h, op0=ALU.mult, op1=ALU.add).then_inc(s_h, 1)
                    dve.engine_nop().then_inc(s_rc, 1)

                front(0)
                with dve.Fori(0, NB - 1, 1) as i:
                    front(i + 1)
                    back(i)
                back(NB - 1)


def build_program(nc, a, out, scratch, stop=9, start=0):
    with ExitStack() as ctx:
        chip = Chip(nc, ctx)
        route = Routing(nc, ctx)
        with nc.sbuf_tensor("x_hi", [P, KT, B, XS], F32R) as chip.x_hi, nc.sbuf_tensor("x_lo", [P, KT, B, XS], F32R) as chip.x_lo:
            wavelet_stage(chip, a["x"], [a["wd_fine"], a["wd_mid"], a["wd_coarse"]], a["wa"], a["wave_bias"], scratch["h_rows"], scratch["slot_x"], a)
            if stop > 0:
                attention_stage(chip, a)
            if stop > 1:
                with nc.sbuf_tensor("xn_rows", [P, NT, D], F32) as xn:
                    gate_stage(chip, a, route, xn)
                    shared_expert_stage(chip, a, route, xn, scratch["slot_x"])
        if stop > 1:
            routed_experts_stage(chip, a, route, scratch["slot_x"], scratch["slot_y"])
            combine_stage(chip, route, scratch["slot_y"])
        if stop > 2:
            with nc.sbuf_tensor("x1", [P, NT, D], F32) as x1, nc.sbuf_tensor("mv1", [P, NT, 2], F32) as mv1:
                time_mix_stage(chip, a, x1, mv1)
                channel_mix_stage(chip, a, x1, mv1)
        if stop <= 3:
            return store_h(chip, out)
        ternary_stage(chip, a, out)


def store_h(chip, out):
    nc = chip.nc
    with nc.semaphore("out_stored") as s_out, nc.Block() as block:
        @block.sync
        def _(sp):
            sp.dma_start(out.rearrange("(t p) c -> p t c", p=P), chip.h[:]).then_inc(s_out, 16)
            sp.wait_ge(s_out, 16)


def layout(inputs):
    import numpy as np

    f = {k: np.asarray(v) for k, v in inputs.items()}
    a = {"x": f["x"].reshape(B * S // 8, 8 * 256)}
    for name, w, rows, cols in (("wd_fine", f["L0_tok_Wd3"], 4, 128), ("wd_mid", f["L0_tok_Wd2"], 2, 64), ("wd_coarse", f["L0_tok_Wd1"], 1, 32)):
        a[name] = w.reshape(3, 32, rows, cols, 3).transpose(1, 4, 0, 2, 3).reshape(32, -1)
    a["wa"] = f["L0_tok_Wa"].reshape(32, 32)
    a["wave_bias"] = np.concatenate([f["L0_tok_bd3"], f["L0_tok_bd2"], f["L0_tok_bd1"], f["L0_tok_ba"]])
    level = np.array([1, 1, 1, 2, 2, 2, 3, 3, 3, 3])
    a["scale_in"] = np.broadcast_to(0.5 ** level, (P, 10)).astype(np.float32)
    a["scale_out"] = np.broadcast_to(0.25 ** level, (P, 10)).astype(np.float32)
    a["group"] = np.kron(np.eye(4), np.ones((32, 32))).astype(np.float32)
    a["ident"] = np.eye(P, dtype=np.float32)
    a["w_qkv"] = np.concatenate([f["L0_attn_Wq"], f["L0_attn_Wk"], f["L0_attn_Wv"]])
    a["b_qkv"] = np.stack([f["L0_attn_bq"], f["L0_attn_bk"], f["L0_attn_bv"], np.zeros(D, np.float32)], axis=1)
    e, n = np.arange(D)[:, None], np.arange(P)[None, :]
    turn = 2 * np.pi * (e * n % D) / D
    sign = np.where(np.arange(D) % 2, -1.0, 1.0)
    a["fourier"] = np.concatenate([np.cos(turn), -np.sin(turn), sign[:, None], np.zeros((D, 1))], axis=1).astype(np.float32)
    twice = np.where(np.arange(P) == 0, 1.0, 2.0)[:, None] / D
    a["inverse"] = np.concatenate([twice * np.cos(turn).T, -twice * np.sin(turn).T]).astype(np.float32)
    a["alt_cols"] = np.broadcast_to(sign[:P, None], (P, P)).astype(np.float32)
    a["alt_row"] = np.broadcast_to(sign[None, :] / D, (P, D)).astype(np.float32)
    a["tri"] = np.triu(np.ones((P, P), np.float32))
    a["ones"] = np.ones((P, P), np.float32)
    a["gate_w"] = f["L0_ffn_gate_w"].T
    a["gate_b"] = f["L0_ffn_gate_b"]
    a["b_out"] = np.concatenate([f["L0_ffn_b2"], f["L0_ffn_sb2"][None]])
    a["before"] = np.broadcast_to(np.tril(np.ones((E, E), np.float32), -1).reshape(1, -1), (P, E * E))
    w1 = np.concatenate([f["L0_ffn_w1"], f["L0_ffn_sw1"][None]]).reshape(E + 1, KT, P, I // P, P, 2)
    w3 = np.concatenate([f["L0_ffn_w3"], f["L0_ffn_sw3"][None]]).reshape(E + 1, KT, P, I // P, P, 2)
    a["w13"] = np.stack([w1, w3], axis=-1).transpose(0, 3, 2, 1, 5, 6, 4).reshape((E + 1) * NJ * P, -1)
    b1 = np.concatenate([f["L0_ffn_b1"], f["L0_ffn_sb1"][None]]).reshape(E + 1, I // P, P, 2)
    b3 = np.concatenate([f["L0_ffn_b3"], f["L0_ffn_sb3"][None]]).reshape(E + 1, I // P, P, 2)
    a["b13"] = np.stack([b1, b3], axis=-1).transpose(0, 2, 1, 3, 4).reshape((E + 1) * P, -1)
    a["counts"] = np.broadcast_to(np.arange(NT // BT, dtype=np.float32) * BLK, (P, NT // BT))
    a["numbers"] = np.broadcast_to(np.arange(NRB, dtype=np.float32), (P, NRB))
    w2 = np.concatenate([f["L0_ffn_w2"], f["L0_ffn_sw2"][None]]).reshape(E + 1, I // P, P, D)
    a["w2"] = w2.transpose(0, 2, 1, 3).reshape((E + 1) * P, -1)
    g = {k[8:]: v for k, v in f.items() if k.startswith("L1_attn_")}
    zero = np.zeros(D, np.float32)
    a["mix_vecs"] = np.stack([g["time_mix_k"], g["time_mix_v"], g["time_mix_r"], g["ln1_g"], g["ln1_b"], g["time_decay"], g["time_first"], zero], axis=1)
    a["w_kvr"] = np.concatenate([g["att_Wk"].T, g["att_Wv"].T, g["att_Wr"].T], axis=1)
    a["w_o"] = g["att_Wo"].T
    a["cm_vecs"] = np.stack([g["cm_k"], g["cm_r"], g["ln2_g"], g["ln2_b"]], axis=1)
    a["w_r2"] = g["ffn_Wr"].T
    a["w_k2"] = g["ffn_Wk"].T
    a["w_v2"] = g["ffn_Wv"].T
    a["w_up"] = f["L1_ffn_w_up"].T
    a["w_down"] = f["L1_ffn_w_down"].T
    return {k: np.ascontiguousarray(v) for k, v in a.items()}


def kernel(stop=9, runner=None, **inputs):
    import numpy as np
    import concourse.bacc as bacc
    from concourse.bass_utils import run_bass_kernel_spmd

    arrays = layout(inputs)
    nc = bacc.Bacc("TRN2", target_bir_lowering=False, num_devices=1)
    args = {k: nc.dram_tensor(f"in_{k}", v.shape, mybir.dt.from_np(v.dtype), kind="ExternalInput").ap() for k, v in arrays.items()}
    out = nc.dram_tensor("out_h", (B * S, D), F32, kind="ExternalOutput").ap()
    scratch = {"h_rows": nc.dram_tensor("h_rows", (B * S, D), F32, kind="Internal").ap(),
               "slot_x": nc.dram_tensor("slot_x", (NRB * BLK, D), F32, kind="Internal").ap(),
               "slot_y": nc.dram_tensor("slot_y", (NRB * BLK, D), F32, kind="Internal").ap()}
    build_program(nc, args, out, scratch, stop)
    feed = {f"in_{k}": v for k, v in arrays.items()}
    if runner:
        return runner(nc, feed, ["out_h"])
    r = run_bass_kernel_spmd(nc, [feed], core_ids=[0])
    return r.results[0]["out_h"].reshape(B, S, D)
```

```python
from contextlib import ExitStack

import concourse.bass as bass
from concourse import mybir

F32 = mybir.dt.float32
F32R = mybir.dt.float32r
ALU = mybir.AluOpType
ACT = mybir.ActivationFunctionType
AX = mybir.AxisListType

P = 128
B, S, D = 16, 256, 256
KT = D // P
NT = B * S // P
BT = 4
NB = NT // BT
BLK = BT * P
BI = BLK // S
TI = S // P
XS = S + 2
LN_EPS = 1e-5
E, TOPK, I = 8, 2, 512
NJ = I // P
LAG = 2
NRB = TOPK * NT // BT + E - 1
SWIGLU_ALPHA, SWIGLU_LIMIT = 1.702, 7.0
U32, I32 = mybir.dt.uint32, mybir.dt.int32


def ds(start, size):
    return bass.ds(start, size)


class Chip:

    def __init__(self, nc, ctx):
        self.nc, self.ctx = nc, ctx
        self.h = ctx.enter_context(nc.sbuf_tensor("h", [P, NT, D], F32))
        self.mv = ctx.enter_context(nc.sbuf_tensor("mean_var", [P, NT, 2], F32))
        self.ident = ctx.enter_context(nc.sbuf_tensor("ident", [P, P], F32))

    def x_block(self, part, kt, i):
        return part[:, kt, ds(BI * i, BI), 1:1 + S]

    def x_shifted(self, part, kt, i):
        return part[:, kt, ds(BI * i, BI), 0:S]


class TileStats:
    PER = 2 * BT + 3

    def __init__(self, name, sb, sem):
        self.stats = sb(name + "_parts", [P, BT, 6])
        self.mean_var = sb(name + "_mean_var", [P, BT, 2])
        self.tick = sb(name + "_tick", [P, 2])
        self.done = sem(name + "_done")

    def block(self, dve, rows, mv, i):
        base = self.PER * i
        dve.wait_ge(self.done, base)
        dve.memset(self.tick[:, 0:1], 0.0).then_inc(self.done, 1)
        for t in range(BT):
            dve.bn_stats(self.stats[:, t], rows[:, ds(BT * i + t, 1)]).then_inc(self.done, 1)
        dve.wait_ge(self.done, base + BT + 1)
        dve.memset(self.tick[:, 1:2], 0.0).then_inc(self.done, 1)
        for t in range(BT):
            dve.bn_aggr(self.mean_var[:, t], self.stats[:, t]).then_inc(self.done, 1)
        dve.wait_ge(self.done, base + 2 * BT + 2)
        dve.tensor_scalar(mv[:, ds(BT * i, BT)], self.mean_var[:], 1.0, None, ALU.mult).then_inc(self.done, 1)

    def finish(self, dve):
        dve.wait_ge(self.done, self.PER * NB)


def split_matmuls(pe, out, weights, moving, first=True, last=True):
    n = len(weights)
    for k in range(n):
        (w_hi, w_lo), (m_hi, m_lo) = weights[k], moving[k]
        pe.matmul(out, w_hi, m_hi, start=(first and k == 0), stop=False)
        pe.matmul(out, w_hi, m_lo, start=False, stop=False)
        mm = pe.matmul(out, w_lo, m_hi, start=False, stop=(last and k == n - 1))
    return mm


def stage_semaphores(nc, ctx):
    taken = []
    ctx.callback(nc.all_engine_barrier)
    ctx.callback(lambda: nc.clear_and_free_semaphores(taken))

    def sem(name):
        taken.append(nc.alloc_semaphore(name))
        return taken[-1]

    return sem


def wavelet_stage(chip, x, wd, wa, bias, h_rows, slot_x, consts):
    nc = chip.nc
    NQ = 4
    ROWS, COLS = [4, 2, 1], [128, 64, 32]
    NW = 10
    with ExitStack() as ctx:
        def sb(name, shape, dt=F32):
            return ctx.enter_context(nc.sbuf_tensor(name, shape, dt))

        sem = stage_semaphores(nc, ctx)

        img = chip.h[:].rearrange("p (q r) c -> p q r c", q=NQ)
        lo_row = sb("lo_row", [P, 4, 256])
        hi_row = sb("hi_row", [P, 4, 256])
        avg = [sb(f"avg{n}", [P, NQ, ROWS[n], COLS[n]]) for n in range(3)]
        det = [sb(f"det{n}", [P, NQ, 3, ROWS[n] * COLS[n]]) for n in range(3)]
        w_det = [sb(f"w_det{n}", [P, 3, 3 * ROWS[n] * COLS[n]]) for n in range(3)]
        w_avg = sb("w_avg", [P, COLS[2]])
        prod = sb("prod", [P, 2, 3 * ROWS[0] * COLS[0]])
        parts = sb("parts", [P, NQ, NW])
        group = sb("group", [P, P])
        scale_in = sb("scale_in", [P, NW])
        scale_out = sb("scale_out", [P, NW])
        biases = sb("biases", [P, NW])
        logits = sb("logits", [P, NQ, NW])
        top = sb("top", [P, NQ, 3])
        wts = sb("wts", [P, NQ, NW])
        neg = sb("neg", [P, NQ, NW])
        tmp = sb("tmp", [P, 512])
        up = [sb(f"up{n}", [P, ROWS[n] * 2, COLS[n] * 2]) for n in range(3)]
        sums = ctx.enter_context(nc.psum_tensor("sums", [P, NQ * NW], F32))

        stats = TileStats("wave_stats", sb, sem)
        s_img = [sem(f"img_loaded{q}") for q in range(NQ)]
        zeros = sb("zeros", [P, BT * D])
        s_zero = sem("zeros_ready")
        s_zeroed = sem("slots_zeroed")
        s_const = sem("wavelet_consts_loaded")
        s_dve = sem("wavelet_dve")
        s_parts = sem("parts_ready")
        s_sums = sem("sums_ready")
        s_logit = sem("logits_ready")
        s_exp = sem("exp_ready")
        s_row = sem("rows_ready")
        s_store = [sem(f"rows_stored{q}") for q in range(NQ)]
        s_h = [sem(f"h_loaded{q}") for q in range(NQ)]
        n_const = 0

        with nc.Block() as block:
            @block.sync
            def _(sp):
                nonlocal n_const
                for q in range(NQ):
                    sp.dma_start(img[:, q], x[ds(q * P, P), :].rearrange("p (r c) -> p r c", r=8)).then_inc(s_img[q], 16)
                for n in range(3):
                    for b in range(4):
                        sp.dma_start(w_det[n][32 * b:32 * b + 32, :, :], wd[n].rearrange("g (j s) -> g j s", j=3)).then_inc(s_const, 16)
                for b in range(4):
                    sp.dma_start(w_avg[32 * b:32 * b + 32, :], wa).then_inc(s_const, 16)
                sp.dma_start(biases[:, :], bias.partition_broadcast(P)).then_inc(s_const, 16)
                sp.dma_start(scale_in[:, :], consts["scale_in"]).then_inc(s_const, 16)
                sp.dma_start(scale_out[:, :], consts["scale_out"]).then_inc(s_const, 16)
                sp.dma_start(group[:, :], consts["group"]).then_inc(s_const, 16)
                sp.dma_start(chip.ident[:, :], consts["ident"]).then_inc(s_const, 16)
                n_const = 16 * (12 + 4 + 5)
                sp.wait_ge(s_zero, 1)
                sp.dma_start(slot_x.rearrange("(n p r) d -> p n (r d)", p=P, r=BT), zeros[:, :].unsqueeze(1).to_broadcast([P, NRB, BT * D])).then_inc(s_zeroed, 16)
                for q in range(NQ):
                    sp.wait_ge(s_row, q + 1)
                    sp.dma_start(h_rows[ds(q * 4 * S, 4 * S), :].rearrange("(p r) c -> p r c", r=8), img[:, q]).then_inc(s_store[q], 16)
                for q in range(NQ):
                    sp.wait_ge(s_store[q], 16)
                    t = q * 4 * TI
                    sp.dma_start(chip.h[:, t:t + 4 * TI, :],
                                 h_rows[ds(q * 4 * S, 4 * S), :].rearrange("(t p) c -> p t c", p=P)).then_inc(s_h[q], 16)

                sp.wait_ge(s_zeroed, 16)

            @block.gpsimd
            def _(pool):
                pool.memset(zeros[:, :], 0.0).then_inc(s_zero, 1)

            @block.tensor
            def _(pe):
                pe.wait_ge(s_const, n_const)
                pe.wait_ge(s_parts, 1)
                pe.matmul(sums[:, :], group[:, :], parts[:].rearrange("p q w -> p (q w)"), start=True, stop=True).then_inc(s_sums, 1)

            @block.scalar
            def _(act):
                act.wait_ge(s_logit, 1)
                act.activation(wts[:, :, 0:9], logits[:, :, 0:9], ACT.Exp).then_inc(s_exp, 1)
                act.activation(wts[:, :, 9:10], logits[:, :, 9:10], ACT.Sigmoid).then_inc(s_exp, 1)

            @block.vector
            def _(dve):
                done = 0

                def step(ins):
                    nonlocal done
                    done += 1
                    ins.then_inc(s_dve, 1)

                def settled():
                    dve.wait_ge(s_dve, done)

                step(dve.memset(parts[:], 0.0))
                for q in range(NQ):
                    dve.wait_ge(s_img[q], 16)
                    for n in range(3):
                        src = img[:, q] if n == 0 else avg[n - 1][:, q]
                        R, C = ROWS[n], COLS[n]
                        rows = src.rearrange("p (r two) c -> p r two c", two=2)
                        lo_r, hi_r = lo_row[:, 0:R, 0:2 * C], hi_row[:, 0:R, 0:2 * C]
                        if n:
                            settled()
                        step(dve.tensor_tensor(lo_r, rows[:, :, 0], rows[:, :, 1], ALU.add))
                        step(dve.tensor_tensor(hi_r, rows[:, :, 0], rows[:, :, 1], ALU.subtract))
                        settled()
                        lo_c = lo_r.rearrange("p r (c two) -> p r c two", two=2)
                        hi_c = hi_r.rearrange("p r (c two) -> p r c two", two=2)
                        d = det[n][:, q].rearrange("p s (r c) -> p s r c", r=R)
                        step(dve.tensor_tensor(avg[n][:, q], lo_c[:, :, :, 0], lo_c[:, :, :, 1], ALU.add))
                        step(dve.tensor_tensor(d[:, 0], hi_c[:, :, :, 0], hi_c[:, :, :, 1], ALU.add))
                        step(dve.tensor_tensor(d[:, 1], lo_c[:, :, :, 0], lo_c[:, :, :, 1], ALU.subtract))
                        step(dve.tensor_tensor(d[:, 2], hi_c[:, :, :, 0], hi_c[:, :, :, 1], ALU.subtract))
                    settled()
                dve.wait_ge(s_const, n_const)
                k = 0
                for q in range(NQ):
                    for n in range(3):
                        for j in range(3):
                            m = 3 * ROWS[n] * COLS[n]
                            if k >= 2:
                                dve.wait_ge(s_dve, done - 1)
                            step(dve.tensor_tensor_reduce(prod[:, k % 2, 0:m], det[n][:, q].rearrange("p s c -> p (s c)"), w_det[n][:, j], 1.0, 0.0,
                                                          ALU.mult, ALU.add, parts[:, q, 3 * n + j:3 * n + j + 1]))
                            k += 1
                    dve.wait_ge(s_dve, done - 1)
                    step(dve.tensor_tensor_reduce(prod[:, k % 2, 0:COLS[2]], avg[2][:, q, 0], w_avg[:, :], 1.0, 0.0,
                                                  ALU.mult, ALU.add, parts[:, q, 9:10]))
                    k += 1
                settled()
                dve.engine_nop().then_inc(s_parts, 1)
                dve.wait_ge(s_sums, 1)

                def per_image(c):
                    return c[:, :].unsqueeze(1).to_broadcast([P, NQ, NW])

                step(dve.tensor_tensor(logits[:], sums[:, :].rearrange("p (q w) -> p q w", q=NQ), per_image(scale_in), ALU.mult))
                settled()
                step(dve.tensor_tensor(logits[:], logits[:], per_image(biases), ALU.add))
                settled()
                l3 = logits[:, :, 0:9].rearrange("p q (l j) -> p q l j", j=3)
                w3 = wts[:, :, 0:9].rearrange("p q (l j) -> p q l j", j=3)
                t3 = top[:].unsqueeze(3).to_broadcast([P, NQ, 3, 3])
                step(dve.tensor_reduce(top[:], l3, AX.X, ALU.max))
                settled()
                step(dve.tensor_tensor(l3, l3, t3, ALU.subtract))
                settled()
                dve.engine_nop().then_inc(s_logit, 1)
                dve.wait_ge(s_exp, 2)
                step(dve.tensor_reduce(top[:], w3, AX.X, ALU.add))
                settled()
                step(dve.reciprocal(top[:], top[:]))
                settled()
                step(dve.tensor_tensor(w3, w3, t3, ALU.mult))
                settled()
                step(dve.tensor_tensor(wts[:], wts[:], per_image(scale_out), ALU.mult))
                settled()
                step(dve.tensor_scalar(neg[:], wts[:], -1.0, None, ALU.mult))
                for q in range(NQ):
                    for n in (2, 1, 0):
                        R, C = ROWS[n], COLS[n]
                        d = det[n][:, q].rearrange("p s (r c) -> p s r c", r=R)
                        w = wts[:, q, 3 * n:3 * n + 3]
                        settled()
                        if n == 2:
                            step(dve.tensor_scalar(avg[2][:, q], avg[2][:, q], wts[:, q, 9:10], None, ALU.mult))
                            coarse = avg[2][:, q]
                        else:
                            coarse = up[n + 1][:, :, :]
                        t = tmp[:, 0:R * C].rearrange("p (r c) -> p r c", r=R)
                        step(dve.tensor_scalar(t, d[:, 2], w[:, 2:3], None, ALU.mult))
                        settled()
                        s_c = lo_row[:, 0:R, 0:2 * C].rearrange("p r (c two) -> p r c two", two=2)
                        d_c = hi_row[:, 0:R, 0:2 * C].rearrange("p r (c two) -> p r c two", two=2)
                        for e, wv, op in ((0, wts, ALU.add), (1, neg, ALU.subtract)):
                            step(dve.scalar_tensor_tensor(out=s_c[:, :, :, e], in0=d[:, 1], scalar=wv[:, q, 3 * n + 1:3 * n + 2],
                                                          in1=coarse, op0=ALU.mult, op1=ALU.add))
                            step(dve.scalar_tensor_tensor(out=d_c[:, :, :, e], in0=d[:, 0], scalar=w[:, 0:1],
                                                          in1=t, op0=ALU.mult, op1=op))
                        settled()
                        out = (img[:, q] if n == 0 else up[n][:, :, :]).rearrange("p (r two) c -> p r two c", two=2)
                        s_r, d_r = lo_row[:, 0:R, 0:2 * C], hi_row[:, 0:R, 0:2 * C]
                        step(dve.tensor_tensor(out[:, :, 0], s_r, d_r, ALU.add))
                        step(dve.tensor_tensor(out[:, :, 1], s_r, d_r, ALU.subtract))
                    settled()
                    dve.engine_nop().then_inc(s_row, 1)
                step(dve.memset(chip.x_hi[:, :, :, 0:1].bitcast(F32), 0.0))
                step(dve.memset(chip.x_lo[:, :, :, 0:1].bitcast(F32), 0.0))
                with dve.Fori(0, NB, 1) as i:
                    for q in range(NQ):
                        dve.wait_ge(s_h[q], 16)
                    stats.block(dve, chip.h, chip.mv, i)
                stats.finish(dve)
                settled()


def attention_stage(chip, a):
    nc = chip.nc
    EPS = 1e-8
    NF = D + 2
    Q, K, V = 0, 1, 2
    ORDER = (K, V, Q)
    with ExitStack() as ctx:
        def sb(name, shape, dt=F32):
            return ctx.enter_context(nc.sbuf_tensor(name, shape, dt))

        def ps(name, shape):
            return ctx.enter_context(nc.psum_tensor(name, shape, F32))

        sem = stage_semaphores(nc, ctx)

        inv_hi = sb("inv_hi", [P, 2, D], F32R)
        inv_lo = sb("inv_lo", [P, 2, D], F32R)
        alt_row = sb("alt_row", [P, D])
        tri = sb("tri", [P, P])
        ones = sb("ones", [P, P])
        wf_hi = sb("wf_hi", [P, KT, 3, D], F32R)
        wf_lo = sb("wf_lo", [P, KT, 3, D], F32R)
        w_nyq = sb("w_nyq", [P, KT, 4])
        b_f = sb("b_f", [P, 3, 4])
        rstd = sb("rstd", [P, NT])
        eps = sb("eps", [P, 1])
        p_t = ps("p_t", [P, BLK])
        p_j = [ps(f"p_j{n}", [P, BLK]) for n in range(4)]
        p_o = ps("p_o", [P, BT, D])
        p_n = ps("p_n", [P, 512])

        stats = TileStats("attn_stats", sb, sem)
        s_ld = sem("attn_loaded")
        s_wf = sem("fourier_weights")
        s_we = sem("fourier_weights_kept")
        s_prep = sem("prep_dve")
        s_var = sem("variance_ready")
        s_std = sem("std_ready")
        s_ready = sem("rstd_ready")
        s_xn = sem("xn_ready")
        s_tr = sem("transposed")
        s_hi = sem("x_hi_ready")
        s_xf = sem("x_full_ready")
        s_lo = sem("x_lo_ready")
        s_pj = sem("projected")
        s_nq = sem("nyquist_projected")
        s_nc = sem("nyquist_chain")
        s_np = sem("nyquist_product")
        s_z = sem("nyquist_unbound")
        s_cum = sem("nyquist_summed")
        s_sq = sem("squares_ready")
        s_sum = sem("power_ready")
        s_mag = sem("magnitude_ready")
        s_fk = sem("spectra_kept")
        s_ln = sem("log_magnitude_ready")
        s_y0 = sem("reciprocal_guess_ready")
        s_r = sem("reciprocal_chain")
        s_u = sem("units_ready")
        s_m = sem("products_dve")
        s_mp = sem("products_pool")
        s_c = sem("running_sums")
        s_ot = sem("unbound_dve")
        s_op = sem("unbound_pool")
        s_os = sem("unbound_ready")
        s_oh = sem("o_hi_ready")
        s_ol = sem("o_lo_ready")
        s_y = sem("y_ready")
        s_hz = sem("h_plus_nyquist")
        s_h = sem("h_updated")
        s_nu = sem("nyquist_units")

        with nc.sbuf_tensor("w_raw", [P, 3, KT, D], F32) as w_raw, nc.sbuf_tensor("fourier", [P, KT, NF], F32) as fourier, \
                nc.sbuf_tensor("inv_raw", [P, 2, D], F32) as inv_raw, nc.sbuf_tensor("b_raw", [P, KT, 4], F32) as b_raw, \
                nc.sbuf_tensor("alt_cols", [P, P], F32) as alt_cols, nc.Block() as block:
            @block.sync
            def _(sp):
                for dst, src in ((w_raw[:], a["w_qkv"].rearrange("(w k p) d -> p w k d", w=3, p=P)),
                                 (fourier[:], a["fourier"].rearrange("(k p) f -> p k f", p=P)),
                                 (inv_raw[:], a["inverse"].rearrange("(k p) d -> p k d", p=P)),
                                 (b_raw[:], a["b_qkv"].rearrange("(k p) w -> p k w", p=P)),
                                 (alt_cols[:], a["alt_cols"]), (alt_row[:], a["alt_row"]),
                                 (tri[:], a["tri"]), (ones[:], a["ones"])):
                    sp.dma_start(dst, src).then_inc(s_ld, 16)

            @block.tensor
            def _(pe):
                pe.wait_ge(s_ld, 16 * 8)
                for n in range(3 * KT):
                    w, mt = n // KT, n % KT
                    if n >= 4:
                        pe.wait_ge(s_we, n - 3)
                    out = p_j[n % 4][:, 0:NF]
                    for k in range(KT):
                        mm = pe.matmul(out, w_raw[:, w, k, mt * P:(mt + 1) * P], fourier[:, k], start=(k == 0), stop=(k == KT - 1))
                    mm.then_inc(s_wf, 1)
                for part in range(3):
                    for k in range(KT):
                        lhs = alt_cols[:, :] if part == 2 else fourier[:, k, part * P:(part + 1) * P]
                        mm = pe.matmul(p_n[:, 4 * part:4 * part + 4], lhs, b_raw[:, k], start=(k == 0), stop=(k == KT - 1))
                mm.then_inc(s_wf, 1)

            @block.scalar
            def _(act):
                act.wait_ge(s_var, 1)
                act.activation(rstd[:, :], rstd[:, :], ACT.Sqrt).then_inc(s_std, 1)

            @block.vector
            def _(dve):
                dve.tensor_scalar(rstd[:, :], chip.mv[:, :, 1], LN_EPS, None, ALU.add).then_inc(s_var, 1)
                dve.wait_ge(s_std, 1)
                dve.reciprocal(rstd[:, :], rstd[:, :]).then_inc(s_ready, 1)
                dve.wait_ge(s_ld, 16 * 8)
                dve.tensor_copy(inv_hi[:], inv_raw[:]).then_inc(s_prep, 1)
                dve.wait_ge(s_prep, 1)
                dve.tensor_tensor(inv_lo[:], inv_raw[:], inv_hi[:].bitcast(F32), ALU.subtract).then_inc(s_prep, 1)
                for n in range(3 * KT):
                    w, mt = n // KT, n % KT
                    src = p_j[n % 4]
                    dve.wait_ge(s_wf, n + 1)
                    dve.tensor_copy(wf_hi[:, mt, w], src[:, 0:D]).then_inc(s_prep, 1)
                    dve.tensor_copy(w_nyq[:, mt, w:w + 1], src[:, D:D + 1]).then_inc(s_prep, 1)
                    dve.wait_ge(s_prep, 2 + 2 * n + 1)
                    dve.tensor_tensor(wf_lo[:, mt, w], src[:, 0:D], wf_hi[:, mt, w].bitcast(F32), ALU.subtract).then_inc(s_we, 1)
                dve.memset(w_nyq[:, :, 3:4], 0.0).then_inc(s_prep, 1)
                dve.wait_ge(s_wf, 3 * KT + 1)
                dve.tensor_copy(b_f[:], p_n[:, 0:12].rearrange("p (a w) -> p a w", a=3)).then_inc(s_prep, 1)
                dve.memset(eps[:, :], EPS).then_inc(s_prep, 1)

        xn = sb("xn", [P, BT, D])
        x_full = sb("x_full", [P, KT, BLK])
        sq = sb("sq", [P, 2, 2, BLK])
        unit = sb("unit", [P, 3, 2, 2, BLK])
        mag = sb("mag", [P, 3, BLK])
        rec = sb("rec", [P, 3, BLK])
        m = sb("m", [P, 4, BLK])
        cum = sb("cum", [P, 2, BLK])
        o_hi = sb("o_hi", [P, 2, BLK], F32R)
        o_lo = sb("o_lo", [P, 2, BLK], F32R)
        nyq = sb("nyq", [P, BT, 3])
        nyq_r = sb("nyq_r", [P, BT, 3])
        nyq_p = sb("nyq_p", [P, BI, TI])
        nyq_z = sb("nyq_z", [P, BT])

        with nc.Block() as block:
            @block.tensor
            def _(pe):
                def transposes(i, kt, first=False):
                    if kt == 0:
                        pe.wait_ge(s_xn, BT * (i + 1))
                    if kt or not first:
                        pe.wait_ge(s_lo, KT * i + kt)
                    for t in range(BT):
                        mm = pe.transpose(p_t[:, t * P:(t + 1) * P], xn[:, t, kt * P:(kt + 1) * P], chip.ident[:, :])
                    mm.then_inc(s_tr, 1)

                def nyquist(i, first=False):
                    pe.wait_ge(s_xf, KT * (i + 1))
                    if not first:
                        pe.wait_ge(s_z, i)
                    for t in range(BT):
                        for k in range(KT):
                            mm = pe.matmul(p_n[:, 4 * t:4 * t + 4], x_full[:, k, t * P:(t + 1) * P], w_nyq[:, k], start=(k == 0), stop=(k == KT - 1))
                    mm.then_inc(s_nq, 1)

                def projections(i, ns, first=False):
                    pe.wait_ge(s_lo, KT * (i + 1))
                    for n in ns:
                        w, ri = ORDER[n // 2], n % 2
                        if n >= 4:
                            pe.wait_ge(s_fk, 6 * i + n - 3)
                        elif not first:
                            pe.wait_ge(s_fk, 6 * i + min(n - 1, 0))
                        split_matmuls(pe, p_j[n % 4][:, :],
                                      [(wf_hi[:, k, w, ri * P:(ri + 1) * P], wf_lo[:, k, w, ri * P:(ri + 1) * P]) for k in range(KT)],
                                      [(chip.x_block(chip.x_hi, k, i), chip.x_block(chip.x_lo, k, i)) for k in range(KT)]).then_inc(s_pj, 1)

                def nyquist_sums(i):
                    pe.wait_ge(s_np, i + 1)
                    pe.matmul(p_n[:, 32:32 + BI], tri[:, :], nyq_p[:, :, 0], start=True, stop=True)
                    pe.matmul(p_n[:, 40:40 + BI], ones[:, :], nyq_p[:, :, 0], start=True, stop=False)
                    pe.matmul(p_n[:, 40:40 + BI], tri[:, :], nyq_p[:, :, 1], start=False, stop=True).then_inc(s_cum, 1)

                def outputs(i, first=False):
                    pe.wait_ge(s_ol, 2 * (i + 1))
                    if not first:
                        pe.wait_ge(s_h, BT * i)
                    for t in range(BT):
                        split_matmuls(pe, p_o[:, t], [(o_hi[:, r, t * P:(t + 1) * P], o_lo[:, r, t * P:(t + 1) * P]) for r in range(2)],
                                      [(inv_hi[:, r], inv_lo[:, r]) for r in range(2)]).then_inc(s_y, 1)

                def body(i, first=False, second=False, ahead=2):
                    if ahead >= 1:
                        projections(i + 1, (0, 1))
                    nyquist_sums(i)
                    if ahead >= 1:
                        projections(i + 1, (2, 3, 4, 5))
                        nyquist(i + 1)
                    if ahead >= 2:
                        transposes(i + 2, 0)
                    if not first:
                        outputs(i - 1, second)
                    if ahead >= 2:
                        transposes(i + 2, 1)

                for kt in range(KT):
                    transposes(0, kt, first=True)
                nyquist(0, first=True)
                for kt in range(KT):
                    transposes(1, kt)
                projections(0, range(6), first=True)
                body(0, first=True)
                body(1, second=True)
                with pe.Fori(2, NB - 2, 1) as i:
                    body(i)
                body(NB - 2, ahead=1)
                body(NB - 1, ahead=0)
                outputs(NB - 1)

            @block.scalar
            def _(act):
                def rows(i, kt, first=False):
                    act.wait_ge(s_tr, KT * i + kt + 1)
                    act.activation(chip.x_block(chip.x_hi, kt, i), p_t[:, :].rearrange("p (b s) -> p b s", b=BI), ACT.Copy).then_inc(s_hi, 1)
                    if not first:
                        act.wait_ge(s_nq, i)
                    act.activation(x_full[:, kt], p_t[:, :], ACT.Copy).then_inc(s_xf, 1)

                def spectra(i):
                    if not isinstance(i, int) or i > 1:
                        act.wait_ge(s_os, 2 * (i - 1))
                        act.wait_ge(s_op, 2 * (i - 1))
                    for n, w in enumerate(ORDER):
                        if n == 2:
                            act.wait_ge(s_sum, 3 * i + 1)
                        elif not isinstance(i, int) or i > 0:
                            act.wait_ge(s_sum, 3 * i - n)
                        for ri in range(2):
                            bank = p_j[(2 * n + ri) % 4]
                            act.wait_ge(s_pj, 6 * i + 2 * n + ri + 1)
                            act.activation(sq[:, n % 2, ri], bank[:, :], ACT.Square, bias=b_f[:, ri, w:w + 1]).then_inc(s_sq, 1)
                            act.activation(unit[:, w, ri, ds(i % 2, 1)], bank[:, :].unsqueeze(1), ACT.Identity, bias=b_f[:, ri, w:w + 1]).then_inc(s_fk, 1)

                def magnitudes(i):
                    for n, w in enumerate(ORDER):
                        act.wait_ge(s_sum, 3 * i + n + 1)
                        act.activation(mag[:, w:w + 1], mag[:, w:w + 1], ACT.Sqrt).then_inc(s_mag, 1)

                def reciprocals(i):
                    for n, w in enumerate(ORDER):
                        act.wait_ge(s_mag, 3 * i + n + 1)
                        act.activation(rec[:, w:w + 1], mag[:, w:w + 1], ACT.Ln, bias=eps[:, :]).then_inc(s_ln, 1)
                    for n, w in enumerate(ORDER):
                        act.wait_ge(s_ln, 3 * i + n + 1)
                        act.activation(rec[:, w:w + 1], rec[:, w:w + 1], ACT.Exp, scale=-1.0).then_inc(s_y0, 1)

                def body(i, first=False, ahead=2):
                    if ahead >= 1:
                        spectra(i + 1)
                    if ahead >= 2:
                        rows(i + 2, 0)
                    if ahead >= 1:
                        magnitudes(i + 1)
                    if ahead >= 2:
                        rows(i + 2, 1)
                    if ahead >= 1:
                        reciprocals(i + 1)
                    if not first:
                        act.wait_ge(s_y, BT * i)
                    for r in range(2):
                        act.wait_ge(s_os, 2 * i + r + 1)
                        act.activation(o_hi[:, r], m[:, 2 * r], ACT.Copy).then_inc(s_oh, 1)

                for kt in range(KT):
                    rows(0, kt, first=True)
                for kt in range(KT):
                    rows(1, kt)
                spectra(0)
                magnitudes(0)
                reciprocals(0)
                body(0, first=True)
                with act.Fori(1, NB - 2, 1) as i:
                    body(i)
                body(NB - 2, ahead=1)
                body(NB - 1, ahead=0)

            @block.gpsimd
            def _(pool):
                def power(i, n):
                    w = ORDER[n]
                    pool.wait_ge(s_sq, 6 * i + 2 * n + 2)
                    if not isinstance(i, int) or i > 0:
                        pool.wait_ge(s_u, 6 * (i - 1) + 2 * n + 2)
                    pool.tensor_tensor(mag[:, w:w + 1], sq[:, n % 2, 0:1], sq[:, n % 2, 1:2], ALU.add).then_inc(s_sum, 1)

                def u(i, w, ri):
                    return unit[:, w, ri, ds(i % 2, 1)]

                def body(i, first=False, ahead=True):
                    if ahead:
                        power(i + 1, 0)
                    pool.wait_ge(s_u, 6 * i + 4)
                    if not first:
                        pool.wait_ge(s_ol, 2 * i)
                    for n, rv in ((1, 1), (3, 0)):
                        pool.tensor_tensor(m[:, n:n + 1], u(i, K, 1), u(i, V, rv), ALU.mult).then_inc(s_mp, 1)
                    for n in (1, 2):
                        if ahead:
                            power(i + 1, n)
                    pool.wait_ge(s_c, 4 * (i + 1))
                    pool.wait_ge(s_u, 6 * (i + 1))
                    pool.tensor_tensor(m[:, 1:2], cum[:, 1:2], u(i, Q, 1), ALU.mult).then_inc(s_op, 1)
                    pool.tensor_tensor(m[:, 3:4], cum[:, 0:1], u(i, Q, 1), ALU.mult).then_inc(s_op, 1)
                    for r in range(2):
                        pool.wait_ge(s_oh, 2 * i + r + 1)
                        pool.tensor_tensor(o_lo[:, r], m[:, 2 * r], o_hi[:, r].bitcast(F32), ALU.subtract).then_inc(s_ol, 1)

                for n in range(3):
                    power(0, n)
                body(0, first=True)
                with pool.Fori(1, NB - 1, 1) as i:
                    body(i)
                body(NB - 1, ahead=False)

            @block.vector
            def _(dve):
                def rows(i, first=False):
                    if not first:
                        dve.wait_ge(s_tr, KT * i)
                    for t in range(BT):
                        tile = ds(BT * i + t, 1)
                        dve.tensor_scalar(xn[:, t:t + 1], chip.h[:, tile], chip.mv[:, tile, 0], rstd[:, tile], ALU.subtract, ALU.mult).then_inc(s_xn, 1)

                def rows_low(i, kt):
                    dve.wait_ge(s_xf, KT * i + kt + 1)
                    dve.tensor_tensor(chip.x_block(chip.x_lo, kt, i), p_t[:, :].rearrange("p (b s) -> p b s", b=BI),
                                      chip.x_block(chip.x_hi, kt, i).bitcast(F32), ALU.subtract).then_inc(s_lo, 1)

                def units(i, n):
                    w = ORDER[n]
                    mg, y = mag[:, w:w + 1], rec[:, w:w + 1]
                    dve.wait_ge(s_y0, 3 * i + n + 1)
                    dve.scalar_tensor_tensor(out=mg, in0=mg, scalar=EPS, in1=y, op0=ALU.add, op1=ALU.mult).then_inc(s_r, 1)
                    dve.wait_ge(s_r, 6 * i + 2 * n + 1)
                    dve.scalar_tensor_tensor(out=mg, in0=mg, scalar=2.0, in1=y, op0=ALU.subtract, op1=ALU.mult).then_inc(s_r, 1)
                    dve.wait_ge(s_r, 6 * i + 2 * n + 2)
                    for ri in range(2):
                        f = unit[:, w, ri, ds(i % 2, 1)]
                        dve.tensor_tensor(f, f, mg, ALU.mult).then_inc(s_u, 1)

                def nyquist(i):
                    bias = b_f[:, 2, 0:3].unsqueeze(1).to_broadcast([P, BT, 3])
                    dve.wait_ge(s_nq, i + 1)
                    dve.tensor_tensor(nyq[:], p_n[:, 0:4 * BT].rearrange("p (t w) -> p t w", t=BT)[:, :, 0:3], bias, ALU.add).then_inc(s_nc, 1)
                    dve.wait_ge(s_nc, 5 * i + 1)
                    dve.tensor_scalar(nyq_r[:], nyq[:], -1.0, None, ALU.mult).then_inc(s_nc, 1)
                    dve.wait_ge(s_nc, 5 * i + 2)
                    dve.tensor_tensor(nyq_r[:], nyq_r[:], nyq[:], ALU.max).then_inc(s_nc, 1)
                    dve.wait_ge(s_nc, 5 * i + 3)
                    dve.tensor_scalar(nyq_r[:], nyq_r[:], EPS, None, ALU.add).then_inc(s_nc, 1)
                    dve.wait_ge(s_nc, 5 * i + 4)
                    dve.reciprocal(nyq_r[:], nyq_r[:]).then_inc(s_nc, 1)
                    dve.wait_ge(s_nc, 5 * i + 5)
                    dve.tensor_tensor(nyq[:], nyq[:], nyq_r[:], ALU.mult).then_inc(s_nu, 1)
                    dve.wait_ge(s_nu, i + 1)
                    dve.tensor_tensor(nyq_p[:], nyq[:, :, K].rearrange("p (b h) -> p b h", b=BI), nyq[:, :, V].rearrange("p (b h) -> p b h", b=BI),
                                      ALU.mult).then_inc(s_np, 1)

                def nyquist_unbind(i):
                    dve.wait_ge(s_cum, i + 1)
                    z = nyq_z[:, :].rearrange("p (b h) -> p h b", b=BI)
                    c = p_n[:, 32:48].rearrange("p (h b) -> p h b", h=2)[:, :, 0:BI]
                    dve.tensor_tensor(z, c, nyq[:, :, Q].rearrange("p (b h) -> p h b", b=BI), ALU.mult).then_inc(s_z, 1)

                def results(i):
                    for t in range(BT):
                        h = chip.h[:, ds(BT * i + t, 1)]
                        dve.wait_ge(s_hz, BT * i + t + 1)
                        dve.wait_ge(s_y, BT * i + t // 2 * 2 + 2)
                        dve.tensor_tensor(h, h, p_o[:, t:t + 1], ALU.add).then_inc(s_h, 1)
                    dve.wait_ge(s_h, BT * (i + 1))
                    stats.block(dve, chip.h, chip.mv, i)

                def body(i, first=False, ahead=2):
                    if ahead >= 2:
                        rows(i + 2)
                    nyquist(i)
                    units(i, 0)
                    units(i, 1)
                    dve.wait_ge(s_u, 6 * i + 4)
                    if not first:
                        dve.wait_ge(s_ol, 2 * i)
                    for n, rv in ((0, 0), (2, 1)):
                        dve.tensor_tensor(m[:, n:n + 1], unit[:, K, 0, ds(i % 2, 1)], unit[:, V, rv, ds(i % 2, 1)], ALU.mult).then_inc(s_m, 1)
                    nyquist_unbind(i)
                    units(i, 2)
                    if ahead >= 2:
                        rows_low(i + 2, 0)
                    if not first:
                        dve.wait_ge(s_op, 2 * i)
                    for ri, op in ((0, ALU.subtract), (1, ALU.add)):
                        dve.wait_ge(s_m, 2 * i + ri + 1)
                        dve.wait_ge(s_mp, 2 * i + ri + 1)
                        for b in range(BI):
                            dve.tensor_tensor_scan(cum[:, ri, b * S:(b + 1) * S], m[:, 2 * ri, b * S:(b + 1) * S], m[:, 2 * ri + 1, b * S:(b + 1) * S],
                                                   initial=0.0, op0=ALU.add, op1=op).then_inc(s_c, 1)
                    dve.wait_ge(s_z, i + 1)
                    for t in range(BT):
                        h = chip.h[:, ds(BT * i + t, 1)]
                        dve.scalar_tensor_tensor(out=h, in0=alt_row[:, :].unsqueeze(1), scalar=nyq_z[:, t:t + 1], in1=h, op0=ALU.mult, op1=ALU.add).then_inc(s_hz, 1)
                    dve.wait_ge(s_c, 4 * (i + 1))
                    dve.wait_ge(s_u, 6 * (i + 1))
                    for r in range(2):
                        dve.tensor_tensor(m[:, 2 * r:2 * r + 1], cum[:, r:r + 1], unit[:, Q, 0, ds(i % 2, 1)], ALU.mult).then_inc(s_ot, 1)
                    if ahead >= 2:
                        rows_low(i + 2, 1)
                    for r, op in ((0, ALU.add), (1, ALU.subtract)):
                        dve.wait_ge(s_ot, 2 * i + r + 1)
                        dve.wait_ge(s_op, 2 * i + r + 1)
                        dve.tensor_tensor(m[:, 2 * r], m[:, 2 * r], m[:, 2 * r + 1], op).then_inc(s_os, 1)
                    if not first:
                        results(i - 1)

                rows(0, first=True)
                rows_low(0, 0)
                rows_low(0, 1)
                rows(1)
                rows_low(1, 0)
                rows_low(1, 1)
                body(0, first=True)
                with dve.Fori(1, NB - 2, 1) as i:
                    body(i)
                body(NB - 2, ahead=1)
                body(NB - 1, ahead=0)
                results(NB - 1)
                stats.finish(dve)


class Routing:

    def __init__(self, nc, ctx):
        def sb(name, shape, dt=F32):
            return ctx.enter_context(nc.sbuf_tensor(name, shape, dt))

        self.weight = sb("choice_weight", [P, TOPK, NT])
        self.slot = sb("choice_slot", [P, TOPK, NT], U32)
        self.expert = sb("block_expert", [1, NRB], I32)


def gate_stage(chip, a, route, xn):
    nc = chip.nc
    with ExitStack() as ctx:
        def sb(name, shape, dt=F32):
            return ctx.enter_context(nc.sbuf_tensor(name, shape, dt))

        def ps(name, shape):
            return ctx.enter_context(nc.psum_tensor(name, shape, F32))

        sem = stage_semaphores(nc, ctx)
        rstd = sb("rstd_g", [P, NT])
        xn_blk = sb("xn_g", [P, BT, D])
        x_full = sb("x_full_g", [P, 2, KT, BLK])
        w_gate = sb("w_gate", [P, KT, E])
        b_gate = sb("b_gate", [P, E])
        before = sb("before", [P, E, E])
        tri = sb("tri_g", [P, P])
        ones = sb("ones_g", [P, P])
        counts = sb("counts", [P, NT // BT])
        numbers = sb("numbers", [P, NRB])
        later = sb("later", [P, E, NT])
        score = sb("score", [P, NT, E])
        biased = sb("biased", [P, NT, E])
        red = sb("red", [P, NT])
        wins = sb("wins", [P, NT, E, E])
        ties = sb("ties", [P, NT, E, E])
        rank = sb("rank", [P, NT, E])
        chosen = sb("chosen", [P, E, NT])
        total = sb("chosen_in_tile", [P, E, NT])
        upto = sb("chosen_upto", [P, E, NT])
        slots = sb("slots", [P, E, NT])
        fits = sb("fits", [P, E, NT // BT])
        blocks = sb("blocks", [P, E])
        last = sb("last_block", [P, E])
        base = sb("first_block", [P, E])
        pick = sb("pick", [P, NT, E])
        slot_f = sb("slot_f", [P, TOPK, NT])
        reached = sb("reached", [1, NRB, E])
        expert_f = sb("expert_f", [1, NRB])
        p_t = [ps(f"p_t_g{k}", [P, BLK]) for k in range(KT)]
        p_g = ps("p_g", [P, BT, E])
        p_n = ps("p_n_g", [P, 2, E * NT])

        s_ld = sem("gate_loaded")
        s_var = sem("g_variance_ready")
        s_std = sem("g_std_ready")
        s_ready = sem("g_rstd_ready")
        s_xn = sem("g_xn_ready")
        s_keep = sem("g_xn_kept")
        s_xa = sem("g_later_set")
        s_tr = sem("g_transposed")
        s_hi = sem("g_x_hi_ready")
        s_xf = sem("g_x_full_ready")
        s_lo = sem("g_x_lo_ready")
        s_gt = sem("gate_projected")
        s_sc = sem("scores_kept")
        s_ch = sem("gate_chain")
        s_mx = sem("gate_max_taken")
        s_ex = sem("gate_exp")
        s_sel = sem("chosen_ready")
        s_cnt = sem("chosen_counted")
        LOADS = 7

        with nc.Block() as block:
            @block.sync
            def _(sp):
                for dst, src in ((w_gate[:], a["gate_w"].rearrange("(k p) e -> p k e", p=P)),
                                 (b_gate[:], a["gate_b"].partition_broadcast(P)),
                                 (before[:], a["before"].rearrange("p (e f) -> p e f", e=E)),
                                 (tri[:], a["tri"]), (ones[:], a["ones"]), (counts[:], a["counts"]), (numbers[:], a["numbers"])):
                    sp.dma_start(dst, src).then_inc(s_ld, 16)

            @block.tensor
            def _(pe):
                pe.wait_ge(s_ld, 16 * LOADS)
                pe.wait_ge(s_ready, 1)

                def transposes(i, first=False):
                    pe.wait_ge(s_xn, BT * (i + 1))
                    if not first:
                        pe.wait_ge(s_lo, KT * i)
                    for kt in range(KT):
                        for t in range(BT):
                            mm = pe.transpose(p_t[kt][:, t * P:(t + 1) * P], xn_blk[:, t, kt * P:(kt + 1) * P], chip.ident[:, :])
                        mm.then_inc(s_tr, 1)

                def gates(i, parity, first=False):
                    pe.wait_ge(s_xf, KT * (i + 1))
                    if not first:
                        pe.wait_ge(s_sc, i)
                    for t in range(BT):
                        for k in range(KT):
                            mm = pe.matmul(p_g[:, t], x_full[:, parity, k, t * P:(t + 1) * P], w_gate[:, k], start=(k == 0), stop=(k == KT - 1))
                    mm.then_inc(s_gt, 1)

                transposes(0, first=True)
                transposes(1)
                gates(0, 0, first=True)
                with pe.Fori(0, NB // 2 - 1, 1) as n:
                    transposes(2 * n + 2)
                    gates(2 * n + 1, 1)
                    transposes(2 * n + 3)
                    gates(2 * n + 2, 0)
                gates(NB - 1, 1)
                pe.wait_ge(s_sel, 1)
                picked = chosen[:].rearrange("p e t -> p (e t)")
                pe.matmul(p_n[:, 0], tri[:, :], picked, start=True, stop=True)
                pe.matmul(p_n[:, 1], ones[:, :], picked, start=True, stop=True).then_inc(s_cnt, 1)

            @block.scalar
            def _(act):
                act.wait_ge(s_var, 1)
                act.activation(rstd[:, :], rstd[:, :], ACT.Sqrt).then_inc(s_std, 1)

                def rows(i, parity, first=False):
                    if not first:
                        act.wait_ge(s_gt, i - 1)
                    for kt in range(KT):
                        act.wait_ge(s_tr, KT * i + kt + 1)
                        act.activation(chip.x_block(chip.x_hi, kt, i), p_t[kt][:, :].rearrange("p (b s) -> p b s", b=BI), ACT.Copy).then_inc(s_hi, 1)
                        act.activation(x_full[:, parity, kt], p_t[kt][:, :], ACT.Copy).then_inc(s_xf, 1)

                rows(0, 0, first=True)
                rows(1, 1, first=True)
                with act.Fori(1, NB // 2, 1) as n:
                    rows(2 * n, 0)
                    rows(2 * n + 1, 1)
                act.wait_ge(s_mx, 1)
                act.activation(score[:], score[:], ACT.Exp).then_inc(s_ex, 1)

            @block.gpsimd
            def _(pool):
                pool.memset(later[:], 1.0).then_inc(s_xa, 1)
                pool.wait_ge(s_xa, 1)
                pool.memset(later[:, :, 0:1], 0.0).then_inc(s_xa, 1)
                with pool.Fori(0, NB, 1) as i:
                    pool.wait_ge(s_xn, BT * (i + 1))
                    pool.tensor_copy(xn[:, ds(BT * i, BT)], xn_blk[:]).then_inc(s_keep, 1)

            @block.vector
            def _(dve):
                dve.tensor_scalar(rstd[:, :], chip.mv[:, :, 1], LN_EPS, None, ALU.add).then_inc(s_var, 1)
                dve.wait_ge(s_std, 1)
                dve.reciprocal(rstd[:, :], rstd[:, :]).then_inc(s_ready, 1)
                dve.wait_ge(s_ready, 1)

                def rows(i, first=False):
                    if not first:
                        dve.wait_ge(s_tr, KT * i)
                        dve.wait_ge(s_keep, i)
                    for t in range(BT):
                        dve.tensor_scalar(xn_blk[:, t:t + 1], chip.h[:, ds(BT * i + t, 1)], chip.mv[:, ds(BT * i + t, 1), 0], rstd[:, ds(BT * i + t, 1)],
                                          ALU.subtract, ALU.mult).then_inc(s_xn, 1)

                def rows_low(i):
                    for kt in range(KT):
                        dve.wait_ge(s_xf, KT * i + kt + 1)
                        dve.tensor_tensor(chip.x_block(chip.x_lo, kt, i), p_t[kt][:, :].rearrange("p (b s) -> p b s", b=BI),
                                          chip.x_block(chip.x_hi, kt, i).bitcast(F32), ALU.subtract).then_inc(s_lo, 1)

                def scores(i):
                    dve.wait_ge(s_gt, i + 1)
                    dve.tensor_copy(score[:, ds(BT * i, BT)], p_g[:]).then_inc(s_sc, 1)

                rows(0, first=True)
                rows_low(0)
                rows(1)
                with dve.Fori(0, NB - 2, 1) as i:
                    rows_low(i + 1)
                    rows(i + 2)
                    scores(i)
                rows_low(NB - 1)
                scores(NB - 2)
                scores(NB - 1)
                n = 0

                def chain(ins):
                    nonlocal n
                    n += 1
                    ins.then_inc(s_ch, 1)
                    dve.wait_ge(s_ch, n)

                per_token = red[:, :].unsqueeze(2).to_broadcast([P, NT, E])
                dve.wait_ge(s_sc, NB)
                chain(dve.tensor_reduce(red[:, :], score[:], AX.X, ALU.max))
                dve.tensor_tensor(score[:], score[:], per_token, ALU.subtract).then_inc(s_mx, 1)
                dve.wait_ge(s_ex, 1)
                chain(dve.tensor_reduce(red[:, :], score[:], AX.X, ALU.add))
                chain(dve.reciprocal(red[:, :], red[:, :]))
                chain(dve.tensor_tensor(score[:], score[:], per_token, ALU.mult))
                dve.wait_ge(s_ld, 16 * LOADS)
                chain(dve.tensor_tensor(biased[:], score[:], b_gate[:, :].unsqueeze(1).to_broadcast([P, NT, E]), ALU.add))
                mine = biased[:].unsqueeze(3).to_broadcast([P, NT, E, E])
                theirs = biased[:].unsqueeze(2).to_broadcast([P, NT, E, E])
                chain(dve.tensor_tensor(wins[:], theirs, mine, ALU.is_gt))
                chain(dve.tensor_tensor(ties[:], theirs, mine, ALU.is_equal))
                chain(dve.tensor_tensor(ties[:], ties[:], before[:].unsqueeze(1).to_broadcast([P, NT, E, E]), ALU.mult))
                chain(dve.tensor_tensor(wins[:], wins[:], ties[:], ALU.add))
                chain(dve.tensor_reduce(rank[:], wins[:], AX.X, ALU.add))
                dve.tensor_scalar(chosen[:].rearrange("p e t -> p t e"), rank[:], TOPK - 0.5, None, ALU.is_lt).then_inc(s_sel, 1)
                dve.wait_ge(s_cnt, 1)
                dve.wait_ge(s_xa, 2)
                chain(dve.tensor_copy(total[:], p_n[:, 1].rearrange("p (e t) -> p e t", e=E)))
                chain(dve.tensor_tensor_scan(upto[:].rearrange("p e t -> p (e t)"), later[:].rearrange("p e t -> p (e t)"),
                                             total[:].rearrange("p e t -> p (e t)"), initial=0.0, op0=ALU.mult, op1=ALU.add))
                chain(dve.tensor_tensor(fits[:], upto[:, :, NT - 1:NT].to_broadcast([P, E, NT // BT]),
                                        counts[:, :].unsqueeze(1).to_broadcast([P, E, NT // BT]), ALU.is_gt))
                chain(dve.tensor_reduce(blocks[:, :], fits[:], AX.X, ALU.add))
                chain(dve.tensor_tensor_scan(last[:, :], ones[:, 0:E], blocks[:, :], initial=0.0, op0=ALU.mult, op1=ALU.add))
                chain(dve.tensor_tensor(base[:, :], last[:, :], blocks[:, :], ALU.subtract))
                chain(dve.tensor_tensor(reached[:], base[0:1, :].unsqueeze(1).to_broadcast([1, NRB, E]),
                                        numbers[0:1, :].unsqueeze(2).to_broadcast([1, NRB, E]), ALU.is_le))
                chain(dve.tensor_reduce(expert_f[:, :], reached[:], AX.X, ALU.add))
                chain(dve.tensor_scalar(route.expert[:, :], expert_f[:, :], -1.0, None, ALU.add))
                chain(dve.tensor_scalar(last[:, :], base[:, :], float(BLK), -1.0, ALU.mult, ALU.add))
                chain(dve.tensor_tensor(upto[:], upto[:], total[:], ALU.subtract))
                chain(dve.tensor_tensor(slots[:], upto[:], p_n[:, 0].rearrange("p (e t) -> p e t", e=E), ALU.add))
                chain(dve.tensor_tensor(slots[:], slots[:], last[:, :].unsqueeze(2).to_broadcast([P, E, NT]), ALU.add))
                for c in range(TOPK):
                    chain(dve.scalar_tensor_tensor(out=pick[:], in0=rank[:], scalar=float(c), in1=score[:], op0=ALU.is_equal, op1=ALU.mult))
                    chain(dve.tensor_reduce(route.weight[:, c], pick[:], AX.X, ALU.add))
                    chain(dve.scalar_tensor_tensor(out=pick[:], in0=rank[:], scalar=float(c), in1=slots[:].rearrange("p e t -> p t e"),
                                                   op0=ALU.is_equal, op1=ALU.mult))
                    chain(dve.tensor_reduce(slot_f[:, c], pick[:], AX.X, ALU.add))
                chain(dve.tensor_copy(route.slot[:], slot_f[:]))


class ExpertBuffers:

    def __init__(self, nc, ctx, tag):
        def sb(name, shape, dt=F32):
            return ctx.enter_context(nc.sbuf_tensor(name + tag, shape, dt))

        def ps(name, shape):
            return ctx.enter_context(nc.psum_tensor(name + tag, shape, F32))

        self.w13_hi = sb("w13_hi", [P, NJ, KT, 4 * P], F32R)
        self.w13_lo = sb("w13_lo", [P, NJ, KT, 4 * P], F32R)
        self.w2_hi = sb("w2_hi", [P, NJ, D], F32R)
        self.w2_lo = sb("w2_lo", [P, NJ, D], F32R)
        self.lin = sb("lin", [P, 2, BLK])
        self.g = sb("g", [P, BLK])
        self.li = sb("li", [P, BLK])
        self.sg = sb("sg", [P, BLK])
        self.gl = sb("gl", [P, BLK])
        self.hid = sb("hid", [P, 2, BLK])
        self.hid_hi = sb("hid_hi", [P, NJ, BLK], F32R)
        self.hid_lo = sb("hid_lo", [P, NJ, BLK], F32R)
        self.p1 = [ps(f"p1_{h}", [P, BLK]) for h in range(2)]
        self.p3 = [ps(f"p3_{h}", [P, BLK]) for h in range(2)]
        self.p_y = ps("p_y", [P, BT, D])


class ExpertSems:
    def __init__(self, sem, tag):
        self.c13 = sem("w13_split" + tag)
        self.c2 = sem("w2_split" + tag)
        self.ph = sem("halves_projected" + tag)
        self.lin = sem("lin_ready" + tag)
        self.st = sem("halves_multiplied" + tag)
        self.gm = sem("g_limited" + tag)
        self.lc = sem("l_limited" + tag)
        self.gl = sem("gl_ready" + tag)
        self.sg = sem("sigmoid_ready" + tag)
        self.hm = sem("hidden_ready" + tag)
        self.hh = sem("hidden_hi_ready" + tag)
        self.hl = sem("hidden_lo_ready" + tag)
        self.w2 = [sem(f"w2_applied{j}" + tag) for j in range(NJ)]
        self.out = sem("y_taken" + tag)


def pe_half(pe, u, s, n, j, hf, x, first):
    if not (first and j == 0):
        pe.wait_ge(s.st, 2 * NJ * n + 2 * j + hf - 1)
    for q, out in ((2 * hf, u.p1[hf]), (2 * hf + 1, u.p3[hf])):
        mm = split_matmuls(pe, out[:, :], [(u.w13_hi[:, j, k, q * P:(q + 1) * P], u.w13_lo[:, j, k, q * P:(q + 1) * P]) for k in range(KT)], x)
    mm.then_inc(s.ph, 1)


def pe_down(pe, u, s, n, j, first=False, splits=None):
    pe.wait_ge(s.hl, NJ * n + j + 1)
    if j == 0 and not first:
        pe.wait_ge(s.out, BT * n)
    if j == 0 and splits is not None:
        pe.wait_ge(s.c2, splits)
    for t in range(BT):
        hi, lo = u.hid_hi[:, j, t * P:(t + 1) * P], u.hid_lo[:, j, t * P:(t + 1) * P]
        pe.matmul(u.p_y[:, t], hi, u.w2_hi[:, j], start=(j == 0 and t % 2 == 0), stop=False, skip_group_check=True)
        pe.matmul(u.p_y[:, t], hi, u.w2_lo[:, j], start=False, stop=False, skip_group_check=True)
        mm = pe.matmul(u.p_y[:, t], lo, u.w2_hi[:, j], start=False, stop=(j == NJ - 1), skip_group_check=True)
    mm.then_inc(s.w2[j], 1)


def pe_tile(pe, u, s, n, j, x, first=False, splits=None):
    for hf in range(2):
        pe_half(pe, u, s, n, j, hf, x, first)
    if j >= LAG:
        pe_down(pe, u, s, n, j - LAG, first, splits)
    elif not first:
        pe_down(pe, u, s, n - 1, NJ + j - LAG)


def act_high(act, u, s, n, j, first=False):
    act.wait_ge(s.hm, NJ * n + j + 1)
    if not first:
        act.wait_ge(s.w2[j], n)
    act.activation(u.hid_hi[:, j], u.hid[:, j % 2], ACT.Copy).then_inc(s.hh, 1)


def act_tile(act, u, s, n, j, bias, first=False, second=False):
    for hf in range(2):
        act.wait_ge(s.ph, 2 * NJ * n + 2 * j + hf + 1)
        if not (first and j == 0):
            act.wait_ge(s.st, 2 * NJ * n + 2 * j + hf - 1)
        act.activation(u.lin[:, hf], u.p1[hf][:, :], ACT.Identity, bias=bias(j, 2 * hf)).then_inc(s.lin, 1)
        if hf == 0:
            if j:
                act_high(act, u, s, n, j - 1, first)
            elif not first:
                act_high(act, u, s, n - 1, NJ - 1, second)
            act.wait_ge(s.gm, NJ * n + j + 1)
            if not (first and j == 0):
                act.wait_ge(s.hm, NJ * n + j)
            act.activation(u.sg[:, :], u.g[:, :], ACT.Sigmoid, scale=SWIGLU_ALPHA).then_inc(s.sg, 1)


def dve_low(dve, u, s, n, j):
    dve.wait_ge(s.hh, NJ * n + j + 1)
    dve.tensor_tensor(u.hid_lo[:, j], u.hid[:, j % 2], u.hid_hi[:, j].bitcast(F32), ALU.subtract).then_inc(s.hl, 1)


def dve_tile(dve, u, s, n, j, bias, first=False):
    k = NJ * n + j
    dve.wait_ge(s.lin, 2 * k + 1)
    if not (first and j == 0):
        dve.wait_ge(s.gl, k)
    dve.scalar_tensor_tensor(out=u.g[:, :], in0=u.p3[0][:, :], scalar=bias(j, 1), in1=u.lin[:, 0], op0=ALU.add, op1=ALU.mult).then_inc(s.st, 1)
    dve.wait_ge(s.st, 2 * k + 1)
    dve.tensor_scalar(u.g[:, :], u.g[:, :], SWIGLU_LIMIT, None, ALU.min).then_inc(s.gm, 1)
    if j:
        dve_low(dve, u, s, n, j - 1)
    elif not first:
        dve_low(dve, u, s, n - 1, NJ - 1)
    dve.wait_ge(s.lin, 2 * k + 2)
    dve.scalar_tensor_tensor(out=u.li[:, :], in0=u.p3[1][:, :], scalar=bias(j, 3), in1=u.lin[:, 1], op0=ALU.add, op1=ALU.mult).then_inc(s.st, 1)
    dve.wait_ge(s.st, 2 * k + 2)
    dve.tensor_scalar(u.li[:, :], u.li[:, :], SWIGLU_LIMIT, -SWIGLU_LIMIT, ALU.min, ALU.max).then_inc(s.lc, 1)
    dve.wait_ge(s.lc, k + 1)
    dve.wait_ge(s.gm, k + 1)
    dve.scalar_tensor_tensor(out=u.gl[:, :], in0=u.li[:, :], scalar=1.0, in1=u.g[:, :], op0=ALU.add, op1=ALU.mult).then_inc(s.gl, 1)
    dve.wait_ge(s.gl, k + 1)
    dve.wait_ge(s.sg, k + 1)
    dve.tensor_tensor(u.hid[:, j % 2], u.gl[:, :], u.sg[:, :], ALU.mult).then_inc(s.hm, 1)


def shared_expert_stage(chip, a, route, xn, slot_x):
    nc = chip.nc
    with ExitStack() as ctx:
        sem = stage_semaphores(nc, ctx)
        u = ExpertBuffers(nc, ctx, "_s")
        s = ExpertSems(sem, "_s")
        b13 = ctx.enter_context(nc.sbuf_tensor("b13_s", [P, 4 * NJ], F32))
        b2 = ctx.enter_context(nc.sbuf_tensor("b2_s", [P, 1, D], F32))
        s_b2 = sem("shared_bias_added")
        s_ld = sem("shared_loaded")
        s_hi = sem("shared_hi_ready")
        s_sent = sem("rows_sent")
        with nc.sbuf_tensor("raw_s", [P, KT * 4 * P], F32) as raw, nc.Block() as block:
            chunks = [(u.w13_hi[:, j].rearrange("p k c -> p (k c)"), u.w13_lo[:, j].rearrange("p k c -> p (k c)"),
                       a["w13"][(E * NJ + j) * P:(E * NJ + j + 1) * P, :]) for j in range(NJ)]
            chunks.append((u.w2_hi[:].rearrange("p j d -> p (j d)"), u.w2_lo[:].rearrange("p j d -> p (j d)"), a["w2"][E * P:(E + 1) * P, :]))

            @block.sync
            def _(sp):
                sp.dma_start(b13[:, :], a["b13"][E * P:(E + 1) * P, :]).then_inc(s_ld, 16)
                sp.dma_start(b2[:, 0], a["b_out"][E * P:(E + 1) * P, :]).then_inc(s_ld, 16)
                for j, (_, _, src) in enumerate(chunks):
                    if j:
                        sp.wait_ge(s.c13, j)
                    sp.wait_ge(s_ld, 16 * (j + 2))
                    sp.dma_start(raw[:, :], src).then_inc(s_ld, 16)

            @block.scalar
            def _(act):
                for j, (hi, _, _) in enumerate(chunks):
                    act.wait_ge(s_ld, 48 + 16 * j)
                    act.activation(hi, raw[:, :], ACT.Copy).then_inc(s_hi, 1)

            @block.vector
            def _(dve):
                for j, (hi, lo, _) in enumerate(chunks):
                    dve.wait_ge(s_hi, j + 1)
                    dve.tensor_tensor(lo, raw[:, :], hi.bitcast(F32), ALU.subtract).then_inc(s.c13 if j < NJ else s.c2, 1)

        def bias(j, q):
            return b13[:, 4 * j + q:4 * j + q + 1]

        with nc.Block() as block:
            @block.gpsimd
            def _(pool):
                for t in range(NT):
                    for c in range(TOPK):
                        pool.indirect_dma_start(slot_x, bass.IndirectOffsetOnAxis(ap=route.slot[:, c, t:t + 1], axis=0), xn[:, t], None).then_inc(s_sent, 16)
                pool.wait_ge(s_sent, 16 * TOPK * NT)

            @block.tensor
            def _(pe):
                def body(i, first=False):
                    x = [(chip.x_block(chip.x_hi, k, i), chip.x_block(chip.x_lo, k, i)) for k in range(KT)]
                    for j in range(NJ):
                        pe_tile(pe, u, s, i, j, x, first)

                body(0, first=True)
                with pe.Fori(1, NB, 1) as i:
                    body(i)
                for j in range(NJ - LAG, NJ):
                    pe_down(pe, u, s, NB - 1, j)

            @block.scalar
            def _(act):
                for j in range(NJ):
                    act_tile(act, u, s, 0, j, bias, first=True)
                for j in range(NJ):
                    act_tile(act, u, s, 1, j, bias, second=True)
                with act.Fori(2, NB, 1) as i:
                    for j in range(NJ):
                        act_tile(act, u, s, i, j, bias)
                act_high(act, u, s, NB - 1, NJ - 1)

            @block.vector
            def _(dve):
                def results(i):
                    for t in range(BT):
                        h = chip.h[:, ds(BT * i + t, 1)]
                        dve.tensor_tensor(h, h, b2[:], ALU.add).then_inc(s_b2, 1)
                    dve.wait_ge(s.w2[NJ - 1], i + 1)
                    for t in range(BT):
                        h = chip.h[:, ds(BT * i + t, 1)]
                        dve.wait_ge(s_b2, BT * i + t + 1)
                        dve.tensor_tensor(h, h, u.p_y[:, t:t + 1], ALU.add).then_inc(s.out, 1)

                def body(i, first=False):
                    for j in range(NJ):
                        dve_tile(dve, u, s, i, j, bias, first)
                        if j == LAG - 1 and not first:
                            results(i - 1)

                body(0, first=True)
                with dve.Fori(1, NB, 1) as i:
                    body(i)
                dve_low(dve, u, s, NB - 1, NJ - 1)
                results(NB - 1)


def routed_experts_stage(chip, a, route, slot_x, slot_y):
    nc = chip.nc
    with ExitStack() as ctx:
        def sb(name, shape, dt=F32):
            return ctx.enter_context(nc.sbuf_tensor(name, shape, dt))

        sem = stage_semaphores(nc, ctx)
        u = ExpertBuffers(nc, ctx, "_r")
        s = ExpertSems(sem, "_r")
        w13_raw = sb("w13_raw", [P, NJ, KT, 4 * P])
        w2_raw = sb("w2_raw", [P, NJ, D])
        b13 = sb("b13", [P, 2, 4 * NJ])
        b2 = sb("b2", [P, 2, D])
        x_in = sb("x_in", [P, BT, D])
        x_hi = sb("xs_hi", [P, KT, 2, BLK], F32R)
        x_lo = sb("xs_lo", [P, KT, 2, BLK], F32R)
        y_out = sb("y_out", [P, 2, BT, D])
        p_t = [ctx.enter_context(nc.psum_tensor(f"p_t_r{k}", [P, BLK], F32)) for k in range(KT)]
        s_x = sem("slot_rows_loaded")
        s_b = sem("slot_biases_loaded")
        s_r13 = [sem(f"w13_loaded{j}") for j in range(NJ)]
        s_r2 = sem("w2_loaded")
        s_h13 = sem("w13_hi_ready")
        s_h2 = sem("w2_hi_ready")
        s_tr = sem("slots_transposed")
        s_xh = sem("slots_hi_ready")
        s_xl = sem("slots_lo_ready")
        s_y = [sem(f"y_stored{r}") for r in range(2)]

        with nc.Block() as block:
            @block.sync
            def _(sp):
                def expert_of(n):
                    return sp.value_load(route.expert[0:1, ds(n, 1)], min_val=0, max_val=E - 1)

                def load_rows(n, first=False):
                    e = expert_of(n)
                    if not first:
                        sp.wait_ge(s_tr, KT * n)
                    sp.dma_start(x_in[:], slot_x[ds(n * BLK, BLK), :].rearrange("(t p) d -> p t d", p=P)).then_inc(s_x, 16)
                    for j in range(NJ):
                        if not first:
                            sp.wait_ge(s.c13, NJ * (n - 1) + j + 1)
                        sp.dma_start(w13_raw[:, j], a["w13"][ds((e * NJ + j) * P, P), :].rearrange("p (k c) -> p k c", k=KT)).then_inc(s_r13[j], 16)

                def load_w2(n, first=False):
                    e = expert_of(n)
                    if not first:
                        sp.wait_ge(s.c2, n)
                        sp.wait_ge(s.st, 2 * NJ * (n - 1) + 1)
                    sp.dma_start(w2_raw[:], a["w2"][ds(e * P, P), :].rearrange("p (j d) -> p j d", j=NJ)).then_inc(s_r2, 16)
                    sp.dma_start(b13[:, ds(n % 2, 1)], a["b13"][ds(e * P, P), :].unsqueeze(1)).then_inc(s_b, 16)
                    sp.dma_start(b2[:, ds(n % 2, 1)], a["b_out"][ds(e * P, P), :].unsqueeze(1)).then_inc(s_b, 16)

                def store(n, parity):
                    sp.wait_ge(s.out, BT * (n + 1))
                    sp.dma_start(slot_y[ds(n * BLK, BLK), :].rearrange("(t p) d -> p t d", p=P), y_out[:, parity]).then_inc(s_y[parity], 16)

                load_rows(0, first=True)
                load_w2(0, first=True)
                load_rows(1)
                load_w2(1)
                with sp.Fori(0, (NRB - 3) // 2, 1) as m:
                    for parity in range(2):
                        load_rows(2 * m + 2 + parity)
                        store(2 * m + parity, parity)
                        load_w2(2 * m + 2 + parity)
                load_rows(NRB - 1)
                store(NRB - 3, 0)
                load_w2(NRB - 1)
                store(NRB - 2, 1)
                store(NRB - 1, 0)
                for parity in range(2):
                    sp.wait_ge(s_y[parity], 16 * ((NRB + 1 - parity) // 2))

            @block.gpsimd
            def _(pool):
                def split13(n, j):
                    pool.wait_ge(s_h13, NJ * n + j + 1)
                    pool.tensor_tensor(u.w13_lo[:, j], w13_raw[:, j], u.w13_hi[:, j].bitcast(F32), ALU.subtract).then_inc(s.c13, 1)

                def split2(n):
                    pool.wait_ge(s_h2, n + 1)
                    pool.tensor_tensor(u.w2_lo[:], w2_raw[:], u.w2_hi[:].bitcast(F32), ALU.subtract).then_inc(s.c2, 1)

                for j in range(NJ):
                    split13(0, j)
                split2(0)
                for j in range(NJ):
                    split13(1, j)
                with pool.Fori(1, NRB - 1, 1) as n:
                    for j in range(NJ):
                        if j == LAG - 1:
                            split2(n)
                        split13(n + 1, j)
                split2(NRB - 1)

            @block.tensor
            def _(pe):
                def x(n):
                    return [(x_hi[:, k, ds(n % 2, 1)], x_lo[:, k, ds(n % 2, 1)]) for k in range(KT)]

                def transposes(n, first=False):
                    pe.wait_ge(s_x, 16 * (n + 1))
                    if not first:
                        pe.wait_ge(s_xl, KT * n)
                    for kt in range(KT):
                        for t in range(BT):
                            mm = pe.transpose(p_t[kt][:, t * P:(t + 1) * P], x_in[:, t, kt * P:(kt + 1) * P], chip.ident[:, :])
                        mm.then_inc(s_tr, 1)

                def body(n, first=False, last=False):
                    x = [(x_hi[:, k, ds(n % 2, 1)], x_lo[:, k, ds(n % 2, 1)]) for k in range(KT)]
                    pe.wait_ge(s_xl, KT * (n + 1))
                    for j in range(NJ):
                        pe.wait_ge(s.c13, NJ * n + j + 1)
                        pe_tile(pe, u, s, n, j, x, first, n + 1)
                        if j == 1 and not last:
                            transposes(n + 1)

                transposes(0, first=True)
                body(0, first=True)
                with pe.Fori(1, NRB - 1, 1) as n:
                    body(n)
                body(NRB - 1, last=True)
                for j in range(NJ - LAG, NJ):
                    pe_down(pe, u, s, NRB - 1, j)

            @block.scalar
            def _(act):
                def high13(n, j, first=False):
                    act.wait_ge(s_r13[j], 16 * (n + 1))
                    if not first:
                        act.wait_ge(s.c13, NJ * n)
                    act.activation(u.w13_hi[:, j], w13_raw[:, j], ACT.Copy).then_inc(s_h13, 1)

                def high2(n):
                    act.wait_ge(s_r2, 16 * (n + 1))
                    act.activation(u.w2_hi[:], w2_raw[:], ACT.Copy).then_inc(s_h2, 1)

                def rows(n):
                    for kt in range(KT):
                        act.wait_ge(s_tr, KT * n + kt + 1)
                        act.activation(x_hi[:, kt, ds(n % 2, 1)], p_t[kt][:, :].unsqueeze(1), ACT.Copy).then_inc(s_xh, 1)

                def body(n, first=False, second=False, last=False):
                    def bias(j, q):
                        return b13[:, ds(n % 2, 1), 4 * j + q]

                    act.wait_ge(s_b, 32 * (n + 1))
                    for j in range(NJ):
                        act_tile(act, u, s, n, j, bias, first, second)
                        if j == LAG - 1 and not first:
                            act.wait_ge(s.w2[NJ - 1], n)
                            high2(n)
                        if not last:
                            high13(n + 1, j)
                        if j == 1 and not last:
                            rows(n + 1)

                rows(0)
                for j in range(NJ):
                    high13(0, j, first=True)
                high2(0)
                body(0, first=True)
                body(1, second=True)
                with act.Fori(2, NRB - 1, 1) as n:
                    body(n)
                body(NRB - 1, last=True)
                act_high(act, u, s, NRB - 1, NJ - 1)

            @block.vector
            def _(dve):
                def rows(n):
                    for kt in range(KT):
                        dve.wait_ge(s_xh, KT * n + kt + 1)
                        dve.tensor_tensor(x_lo[:, kt, ds(n % 2, 1)], p_t[kt][:, :].unsqueeze(1), x_hi[:, kt, ds(n % 2, 1)].bitcast(F32),
                                          ALU.subtract).then_inc(s_xl, 1)

                def results(n, parity):
                    dve.wait_ge(s.w2[NJ - 1], n + 1)
                    if not isinstance(n, int) or n > 1:
                        dve.wait_ge(s_y[parity], 8 * (n - parity))
                    for t in range(BT):
                        dve.tensor_tensor(y_out[:, parity, t:t + 1], u.p_y[:, t:t + 1], b2[:, ds(n % 2, 1)], ALU.add).then_inc(s.out, 1)

                def body(n, parity, first=False, last=False):
                    def bias(j, q):
                        return b13[:, ds(n % 2, 1), 4 * j + q]

                    dve.wait_ge(s_b, 32 * (n + 1))
                    for j in range(NJ):
                        dve_tile(dve, u, s, n, j, bias, first)
                        if j == LAG - 1 and not first:
                            results(n - 1, 1 - parity)
                        if j == 1 and not last:
                            rows(n + 1)

                rows(0)
                body(0, 0, first=True)
                body(1, 1)
                body(2, 0)
                with dve.Fori(1, (NRB - 3) // 2, 1) as m:
                    body(2 * m + 1, 1)
                    body(2 * m + 2, 0)
                body(NRB - 2, 1)
                body(NRB - 1, 0, last=True)
                dve_low(dve, u, s, NRB - 1, NJ - 1)
                results(NRB - 1, 0)


def combine_stage(chip, route, slot_y):
    nc = chip.nc
    RING = 8
    with ExitStack() as ctx:
        sem = stage_semaphores(nc, ctx)
        rows = ctx.enter_context(nc.sbuf_tensor("expert_rows", [P, RING, TOPK, D], F32))
        s_got = [sem(f"rows_gathered{r}") for r in range(RING)]
        s_add = sem("rows_added")
        h_stats = TileStats("h_stats", lambda name, shape: ctx.enter_context(nc.sbuf_tensor(name, shape, F32)), sem)
        with nc.Block() as block:
            @block.gpsimd
            def _(pool):
                for t in range(NT):
                    if t >= RING:
                        pool.wait_ge(s_add, TOPK * (t - RING + 1))
                    for c in range(TOPK):
                        pool.indirect_dma_start(rows[:, t % RING, c], None, slot_y, bass.IndirectOffsetOnAxis(ap=route.slot[:, c, t:t + 1], axis=0)).then_inc(s_got[t % RING], 16)

            @block.vector
            def _(dve):
                for t in range(NT):
                    dve.wait_ge(s_got[t % RING], 16 * TOPK * (t // RING + 1))
                    for c in range(TOPK):
                        if c:
                            dve.wait_ge(s_add, TOPK * t + c)
                        dve.scalar_tensor_tensor(out=chip.h[:, t], in0=rows[:, t % RING, c], scalar=route.weight[:, c, t:t + 1], in1=chip.h[:, t],
                                                 op0=ALU.mult, op1=ALU.add).then_inc(s_add, 1)
                    if t % BT == BT - 1:
                        dve.wait_ge(s_add, TOPK * (t + 1))
                        h_stats.block(dve, chip.h, chip.mv, t // BT)
                h_stats.finish(dve)


def ring_block(part, kt, i, first=1):
    return part[:, kt, ds(BI * (i % 2), BI), first:first + S]


def by_image(tile):
    return tile.rearrange("p (b s) -> p b s", b=BI)


def time_mix_stage(chip, a, x1, mv1):
    nc = chip.nc
    KV = 3
    NO_STATE = -1e38
    with ExitStack() as ctx:
        def sb(name, shape, dt=F32):
            return ctx.enter_context(nc.sbuf_tensor(name, shape, dt))

        def ps(name, shape):
            return ctx.enter_context(nc.psum_tensor(name, shape, F32))

        sem = stage_semaphores(nc, ctx)

        x_hi = sb("xa_hi", [P, KT, 2 * BI, XS], F32R)
        x_lo = sb("xa_lo", [P, KT, 2 * BI, XS], F32R)
        wm_hi = sb("wm_hi", [P, KT, 2, KV, D], F32R)
        wm_lo = sb("wm_lo", [P, KT, 2, KV, D], F32R)
        wo_hi = sb("wo_hi", [P, KT, D], F32R)
        wo_lo = sb("wo_lo", [P, KT, D], F32R)
        vecs = sb("vecs", [P, KT, 8])
        one_m = sb("one_m", [P, KT, KV])
        decay = sb("decay", [P, KT])
        rstd = sb("rstd1", [P, 2, NT])
        s_vec = sem("vectors_loaded")
        s_pd = sem("mix_prep_dve")
        s_pa = sem("mix_prep_act")
        s_bs = sem("variance_ready1")
        x1_stats = TileStats("x1_stats", sb, sem)

        with nc.sbuf_tensor("wm_raw", [P, KT, KV, D], F32) as w_raw, nc.sbuf_tensor("wo_raw", [P, KT, D], F32) as wo_raw, \
                nc.sbuf_tensor("wm_f", [P, KT, 2, KV, D], F32) as w_f, nc.Block() as block:
            @block.sync
            def _(sp):
                for dst, src in ((vecs[:], a["mix_vecs"].rearrange("(k p) v -> p k v", p=P)),
                                 (w_raw[:], a["w_kvr"].rearrange("(k p) (v o) -> p k v o", p=P, v=KV)),
                                 (wo_raw[:], a["w_o"].rearrange("(k p) o -> p k o", p=P))):
                    sp.dma_start(dst, src).then_inc(s_vec, 16)

            @block.scalar
            def _(act):
                act.wait_ge(s_vec, 48)
                act.activation(decay[:, :], vecs[:, :, 5], ACT.Exp).then_inc(s_pa, 1)
                act.wait_ge(s_pd, 1)
                act.activation(rstd[:], rstd[:], ACT.Sqrt).then_inc(s_pa, 1)

            @block.vector
            def _(dve):
                dve.tensor_scalar(rstd[:, 0], chip.mv[:, :, 1], LN_EPS, None, ALU.add).then_inc(s_bs, 1)
                dve.wait_ge(s_bs, 1)
                dve.scalar_tensor_tensor(out=rstd[:, 1], in0=rstd[:, 0], scalar=LN_EPS, in1=chip.mv[:, :, 1], op0=ALU.mult, op1=ALU.add).then_inc(s_pd, 1)
                dve.wait_ge(s_pa, 2)
                dve.reciprocal(rstd[:], rstd[:]).then_inc(s_pd, 1)
                dve.tensor_scalar(decay[:, :], decay[:, :], -1.0, None, ALU.mult).then_inc(s_pd, 1)
                dve.tensor_scalar(one_m[:], vecs[:, :, 0:KV], -1.0, 1.0, ALU.mult, ALU.add).then_inc(s_pd, 1)
                dve.memset(x_hi[:, :, :, 0:1].bitcast(F32), 0.0).then_inc(s_pd, 1)
                dve.memset(x_lo[:, :, :, 0:1].bitcast(F32), 0.0).then_inc(s_pd, 1)
                dve.wait_ge(s_pd, 4)
                for k in range(KT):
                    for v in range(KV):
                        dve.tensor_scalar(w_f[:, k, 0, v], w_raw[:, k, v], vecs[:, k, v:v + 1], None, ALU.mult).then_inc(s_pd, 1)
                        dve.tensor_scalar(w_f[:, k, 1, v], w_raw[:, k, v], one_m[:, k, v:v + 1], None, ALU.mult).then_inc(s_pd, 1)
                dve.wait_ge(s_pd, 6 + 2 * KT * KV)
                dve.tensor_copy(wm_hi[:].rearrange("p k m v d -> p (k m v d)"), w_f[:].rearrange("p k m v d -> p (k m v d)")).then_inc(s_pd, 1)
                dve.tensor_copy(wo_hi[:], wo_raw[:]).then_inc(s_pd, 1)
                dve.wait_ge(s_pd, 6 + 2 * KT * KV + 2)
                dve.tensor_tensor(wm_lo[:].rearrange("p k m v d -> p (k m v d)"), w_f[:].rearrange("p k m v d -> p (k m v d)"),
                                  wm_hi[:].bitcast(F32).rearrange("p k m v d -> p (k m v d)"), ALU.subtract).then_inc(s_pd, 1)
                dve.tensor_tensor(wo_lo[:], wo_raw[:], wo_hi[:].bitcast(F32), ALU.subtract).then_inc(s_pd, 1)

        def pair(name, shape):
            return [sb(f"{name}{m}", shape) for m in range(KT)]

        xn = sb("xn1", [P, BT, D])
        xa = sb("xa", [P, KT, BLK])
        key, val, gate = pair("key", [P, BLK]), pair("val", [P, BLK]), pair("gate", [P, BLK])
        top = pair("top_state", [P, BI, S + 1])
        keep, add = pair("keep", [P, BLK]), pair("add", [P, BLK])
        mix = pair("mix", [P, 2, BLK])
        addv = pair("addv", [P, BLK])
        num_s, den_s = pair("num_state", [P, BI, S + 1]), pair("den_state", [P, BI, S + 1])
        rw_hi = sb("rw_hi", [P, KT, BLK], F32R)
        rw_lo = sb("rw_lo", [P, KT, BLK], F32R)
        p_t = [ps(f"p_t1_{k}", [P, BLK]) for k in range(KT)]
        p_j = [ps(f"p_j1_{k}", [P, BLK]) for k in range(4)]
        p_y = ps("p_y1", [P, BT, D])

        s_x1 = sem("x1_ready")
        s_xn = sem("xn1_ready")
        s_tr = sem("transposed1")
        s_xa = sem("xa_ready")
        s_xh = sem("xa_hi_ready")
        s_xl = sem("xa_lo_ready")
        s_pj = sem("kvr_projected")
        s_kv = sem("kvr_kept")
        s_top = sem("top_scanned")
        s_kd = sem("keep_exponent")
        s_ad = sem("add_exponent")
        s_md = sem("mix_exponents")
        s_ch = sem("mix_chain")
        s_ke = sem("keep_ready")
        s_ae = sem("add_ready")
        s_me = sem("mix_ready")
        s_av = sem("addv_ready")
        s_sc = sem("states_scanned")
        s_n2 = sem("token_part_ready")
        s_nd = sem("num_den_chain")
        s_dn = sem("den_ready")
        s_ln = sem("log_den_ready")
        s_y0 = sem("first_guess_ready")
        s_q = sem("gated_num_ready")
        s_nw = sem("newton_chain")
        s_rw = sem("rwkv_ready")
        s_rh = sem("rwkv_hi_ready")
        s_rl = sem("rwkv_lo_ready")
        s_y = sem("wo_applied")
        s_xu = sem("x1_updated")
        s_zero = sem("initial_states")

        with nc.Block() as block:
            @block.tensor
            def _(pe):
                def transposes(i, first=False):
                    pe.wait_ge(s_xn, BT * (i + 1))
                    if not first:
                        pe.wait_ge(s_xa, KT * i)
                    for kt in range(KT):
                        for t in range(BT):
                            mm = pe.transpose(p_t[kt][:, t * P:(t + 1) * P], xn[:, t, kt * P:(kt + 1) * P], chip.ident[:, :])
                        mm.then_inc(s_tr, 1)

                def projections(i, ns, first=False):
                    pe.wait_ge(s_xl, KT * (i + 1))
                    for n in ns:
                        v, m = n // KT, n % KT
                        if n >= 4:
                            pe.wait_ge(s_kv, 6 * i + n - 3)
                        elif not first:
                            pe.wait_ge(s_kv, 6 * i + min(n - 1, 0))
                        w, x = [], []
                        for k in range(KT):
                            for shifted in range(2):
                                w.append((wm_hi[:, k, shifted, v, m * P:(m + 1) * P], wm_lo[:, k, shifted, v, m * P:(m + 1) * P]))
                                x.append((ring_block(x_hi, k, i, 1 - shifted), ring_block(x_lo, k, i, 1 - shifted)))
                        split_matmuls(pe, p_j[n % 4][:, :], w, x).then_inc(s_pj, 1)

                def outputs(i, first=False):
                    pe.wait_ge(s_rl, KT * (i + 1))
                    if not first:
                        pe.wait_ge(s_xu, BT * i)
                    for t in range(BT):
                        split_matmuls(pe, p_y[:, t], [(rw_hi[:, k, t * P:(t + 1) * P], rw_lo[:, k, t * P:(t + 1) * P]) for k in range(KT)],
                                      [(wo_hi[:, k], wo_lo[:, k]) for k in range(KT)]).then_inc(s_y, 1)

                def body(i, first=False, ahead=2):
                    projections(i, (4, 5))
                    if ahead >= 1:
                        projections(i + 1, (0, 1, 2, 3))
                    if ahead >= 2:
                        transposes(i + 2)
                    outputs(i, first)

                transposes(0, first=True)
                transposes(1)
                projections(0, (0, 1, 2, 3), first=True)
                body(0, first=True)
                with pe.Fori(1, NB - 2, 1) as i:
                    body(i)
                body(NB - 2, ahead=1)
                body(NB - 1, ahead=0)

            @block.scalar
            def _(act):
                def rows(i):
                    if not isinstance(i, int) or i > 0:
                        act.wait_ge(s_xl, KT * i)
                    if not isinstance(i, int) or i > 1:
                        act.wait_ge(s_pj, 6 * (i - 1))
                    for kt in range(KT):
                        act.wait_ge(s_tr, KT * i + kt + 1)
                        act.activation(xa[:, kt], p_t[kt][:, :], ACT.Identity, bias=vecs[:, kt, 4:5], scale=vecs[:, kt, 3:4]).then_inc(s_xa, 1)
                    for kt in range(KT):
                        act.wait_ge(s_xa, KT * i + kt + 1)
                        act.activation(ring_block(x_hi, kt, i), by_image(xa[:, kt]), ACT.Copy).then_inc(s_xh, 1)

                def body(i, first=False, ahead=2):
                    if not first:
                        act.wait_ge(s_rw, KT * i)
                    for n, dst in enumerate(key + val):
                        act.wait_ge(s_pj, 6 * i + n + 1)
                        act.activation(dst[:, :], p_j[n][:, :], ACT.Copy).then_inc(s_kv, 1)
                    for m in range(KT):
                        act.wait_ge(s_kd, KT * i + m + 1)
                        act.activation(keep[m][:, :], keep[m][:, :], ACT.Exp).then_inc(s_ke, 1)
                        act.wait_ge(s_ad, KT * i + m + 1)
                        act.activation(add[m][:, :], add[m][:, :], ACT.Exp).then_inc(s_ae, 1)
                        act.wait_ge(s_md, KT * i + m + 1)
                        act.activation(mix[m][:], mix[m][:], ACT.Exp).then_inc(s_me, 1)
                    for m in range(KT):
                        n = 2 * KT + m
                        act.wait_ge(s_pj, 6 * i + n + 1)
                        act.activation(gate[m][:, :], p_j[n % 4][:, :], ACT.Sigmoid).then_inc(s_kv, 1)
                    for m in range(KT):
                        act.wait_ge(s_dn, KT * i + m + 1)
                        act.activation(key[m][:, :], mix[m][:, 0], ACT.Ln).then_inc(s_ln, 1)
                    for m in range(KT):
                        act.wait_ge(s_ln, KT * i + m + 1)
                        act.activation(key[m][:, :], key[m][:, :], ACT.Exp, scale=-1.0).then_inc(s_y0, 1)
                    if ahead >= 2:
                        rows(i + 2)
                    if not first:
                        act.wait_ge(s_y, BT * i)
                    for m in range(KT):
                        act.wait_ge(s_rw, KT * i + m + 1)
                        act.activation(rw_hi[:, m], addv[m][:, :], ACT.Copy).then_inc(s_rh, 1)

                rows(0)
                rows(1)
                body(0, first=True)
                with act.Fori(1, NB - 2, 1) as i:
                    body(i)
                body(NB - 2, ahead=1)
                body(NB - 1, ahead=0)

            @block.gpsimd
            def _(pool):
                def rows(i):
                    for kt in range(KT):
                        pool.wait_ge(s_xh, KT * i + kt + 1)
                        pool.tensor_tensor(ring_block(x_lo, kt, i), by_image(xa[:, kt]), ring_block(x_hi, kt, i).bitcast(F32), ALU.subtract).then_inc(s_xl, 1)

                def body(i, ahead=2):
                    for m in range(KT):
                        pool.wait_ge(s_top, BI * (KT * i + m + 1))
                        pool.tensor_tensor(by_image(add[m][:, :]), by_image(key[m][:, :]), top[m][:, :, 1:], ALU.subtract).then_inc(s_ad, 1)
                    for m in range(KT):
                        pool.wait_ge(s_kv, 6 * i + KT + m + 1)
                        pool.wait_ge(s_ae, KT * i + m + 1)
                        pool.tensor_tensor(addv[m][:, :], add[m][:, :], val[m][:, :], ALU.mult).then_inc(s_av, 1)
                    for m in range(KT):
                        pool.wait_ge(s_me, KT * i + m + 1)
                        pool.wait_ge(s_av, KT * i + m + 1)
                        pool.tensor_tensor(val[m][:, :], mix[m][:, 1], val[m][:, :], ALU.mult).then_inc(s_n2, 1)
                    if ahead >= 2:
                        rows(i + 2)
                    for m in range(KT):
                        pool.wait_ge(s_rh, KT * i + m + 1)
                        pool.tensor_tensor(rw_lo[:, m], addv[m][:, :], rw_hi[:, m].bitcast(F32), ALU.subtract).then_inc(s_rl, 1)

                rows(0)
                rows(1)
                with pool.Fori(0, NB - 2, 1) as i:
                    body(i)
                body(NB - 2, ahead=1)
                body(NB - 1, ahead=0)

            @block.vector
            def _(dve):
                for m in range(KT):
                    dve.memset(top[m][:, :, 0:1], NO_STATE).then_inc(s_zero, 1)
                    dve.memset(num_s[m][:, :, 0:1], 0.0).then_inc(s_zero, 1)
                    dve.memset(den_s[m][:, :, 0:1], 0.0).then_inc(s_zero, 1)
                dve.wait_ge(s_zero, 3 * KT)

                def rows(i, first=False):
                    if not first:
                        dve.wait_ge(s_tr, KT * i)
                    for t in range(BT):
                        tile = ds(BT * i + t, 1)
                        dve.tensor_scalar(xn[:, t:t + 1], chip.h[:, tile], chip.mv[:, tile, 0], rstd[:, 1, tile], ALU.subtract, ALU.mult).then_inc(s_xn, 1)
                    for t in range(BT):
                        tile = ds(BT * i + t, 1)
                        dve.tensor_scalar(x1[:, tile], chip.h[:, tile], chip.mv[:, tile, 0], rstd[:, 0, tile], ALU.subtract, ALU.mult).then_inc(s_x1, 1)

                def results(i):
                    for t in range(BT):
                        tile = ds(BT * i + t, 1)
                        dve.wait_ge(s_y, BT * i + t // 2 * 2 + 2)
                        dve.tensor_tensor(x1[:, tile], x1[:, tile], p_y[:, t:t + 1], ALU.add).then_inc(s_xu, 1)
                    dve.wait_ge(s_xu, BT * (i + 1))
                    x1_stats.block(dve, x1, mv1, i)

                def body(i, first=False, ahead=2):
                    two = KT * i
                    for m in range(KT):
                        u = vecs[:, m, 6:7]
                        before, after = top[m][:, :, 0:S], top[m][:, :, 1:]
                        dve.wait_ge(s_kv, 6 * i + m + 1)
                        for b in range(BI):
                            dve.tensor_tensor_scan(top[m][:, b, 1:], decay[:, m:m + 1].to_broadcast([P, S]), key[m][:, b * S:(b + 1) * S],
                                                   initial=NO_STATE, op0=ALU.add, op1=ALU.max).then_inc(s_top, 1)
                        dve.wait_ge(s_top, BI * (two + m + 1))
                        dve.scalar_tensor_tensor(out=by_image(keep[m][:, :]), in0=before, scalar=decay[:, m:m + 1], in1=after,
                                                 op0=ALU.add, op1=ALU.subtract).then_inc(s_kd, 1)
                        dve.scalar_tensor_tensor(out=by_image(mix[m][:, 1]), in0=by_image(key[m][:, :]), scalar=u, in1=before,
                                                 op0=ALU.add, op1=ALU.subtract).then_inc(s_ch, 1)
                        dve.wait_ge(s_ch, 2 * (two + m) + 1)
                        dve.tensor_scalar(mix[m][:, 0], mix[m][:, 1], 0.0, -1.0, ALU.max, ALU.mult).then_inc(s_ch, 1)
                        dve.wait_ge(s_ch, 2 * (two + m) + 2)
                        dve.tensor_scalar(mix[m][:, 1], mix[m][:, 1], 0.0, None, ALU.min).then_inc(s_md, 1)
                    if not first:
                        results(i - 1)
                    for m in range(KT):
                        dve.wait_ge(s_ke, two + m + 1)
                        dve.wait_ge(s_ae, two + m + 1)
                        for b in range(BI):
                            dve.tensor_tensor_scan(den_s[m][:, b, 1:], keep[m][:, b * S:(b + 1) * S], add[m][:, b * S:(b + 1) * S],
                                                   initial=0.0, op0=ALU.mult, op1=ALU.add).then_inc(s_sc, 1)
                        dve.wait_ge(s_av, two + m + 1)
                        for b in range(BI):
                            dve.tensor_tensor_scan(num_s[m][:, b, 1:], keep[m][:, b * S:(b + 1) * S], addv[m][:, b * S:(b + 1) * S],
                                                   initial=0.0, op0=ALU.mult, op1=ALU.add).then_inc(s_sc, 1)
                    if ahead >= 2:
                        rows(i + 2)
                    for m in range(KT):
                        dve.wait_ge(s_me, two + m + 1)
                        dve.wait_ge(s_sc, 2 * BI * (two + m + 1))
                        dve.tensor_tensor(by_image(addv[m][:, :]), by_image(mix[m][:, 0]), num_s[m][:, :, 0:S], ALU.mult).then_inc(s_nd, 1)
                        dve.tensor_tensor(by_image(mix[m][:, 0]), by_image(mix[m][:, 0]), den_s[m][:, :, 0:S], ALU.mult).then_inc(s_nd, 1)
                        dve.wait_ge(s_nd, 3 * two + 2 * m + 2)
                        dve.tensor_tensor(mix[m][:, 0], mix[m][:, 0], mix[m][:, 1], ALU.add).then_inc(s_dn, 1)
                    for m in range(KT):
                        dve.wait_ge(s_n2, two + m + 1)
                        dve.tensor_tensor(addv[m][:, :], addv[m][:, :], val[m][:, :], ALU.add).then_inc(s_nd, 1)
                        dve.wait_ge(s_nd, 3 * two + 2 * KT + m + 1)
                        dve.wait_ge(s_kv, 6 * i + 2 * KT + m + 1)
                        dve.tensor_tensor(addv[m][:, :], addv[m][:, :], gate[m][:, :], ALU.mult).then_inc(s_q, 1)
                    for m in range(KT):
                        base = 2 * (two + m)
                        dve.wait_ge(s_y0, two + m + 1)
                        dve.wait_ge(s_dn, two + m + 1)
                        dve.tensor_tensor(mix[m][:, 0], mix[m][:, 0], key[m][:, :], ALU.mult).then_inc(s_nw, 1)
                        dve.wait_ge(s_nw, base + 1)
                        dve.scalar_tensor_tensor(out=mix[m][:, 0], in0=mix[m][:, 0], scalar=2.0, in1=key[m][:, :], op0=ALU.subtract, op1=ALU.mult).then_inc(s_nw, 1)
                        dve.wait_ge(s_nw, base + 2)
                        dve.wait_ge(s_q, two + m + 1)
                        dve.scalar_tensor_tensor(out=addv[m][:, :], in0=addv[m][:, :], scalar=-1.0, in1=mix[m][:, 0], op0=ALU.mult, op1=ALU.mult).then_inc(s_rw, 1)

                rows(0, first=True)
                rows(1)
                body(0, first=True)
                with dve.Fori(1, NB - 2, 1) as i:
                    body(i)
                body(NB - 2, ahead=1)
                body(NB - 1, ahead=0)
                results(NB - 1)
                x1_stats.finish(dve)


def channel_mix_stage(chip, a, x1, mv1):
    nc = chip.nc
    NH = 4 * D // P
    with ExitStack() as ctx:
        def sb(name, shape, dt=F32):
            return ctx.enter_context(nc.sbuf_tensor(name, shape, dt))

        def ps(name, shape):
            return ctx.enter_context(nc.psum_tensor(name, shape, F32))

        sem = stage_semaphores(nc, ctx)

        wk_hi = sb("wk_hi", [P, KT, NH * P], F32R)
        wk_lo = sb("wk_lo", [P, KT, NH * P], F32R)
        wv_hi = sb("wv_hi", [P, NH, D], F32R)
        wv_lo = sb("wv_lo", [P, NH, D], F32R)
        wr_hi = sb("wr_hi", [P, KT, D], F32R)
        wr_lo = sb("wr_lo", [P, KT, D], F32R)
        vecs = sb("vecs2", [P, KT, 4])
        one_m = sb("one_m2", [P, KT, 2])
        rstd = sb("rstd2", [P, NT])
        xc = sb("xc", [P, KT, BI, XS])
        s_vec = sem("vectors2_loaded")
        s_pd = sem("cm_prep_dve")
        s_pa = sem("cm_prep_act")

        with nc.sbuf_tensor("wk_raw", [P, KT, NH * P], F32) as wk_raw, nc.sbuf_tensor("wv_raw", [P, NH, D], F32) as wv_raw, \
                nc.sbuf_tensor("wr_raw", [P, KT, D], F32) as wr_raw, nc.Block() as block:
            @block.sync
            def _(sp):
                for dst, src in ((vecs[:], a["cm_vecs"].rearrange("(k p) v -> p k v", p=P)),
                                 (wr_raw[:], a["w_r2"].rearrange("(k p) o -> p k o", p=P)),
                                 (wk_raw[:], a["w_k2"].rearrange("(k p) o -> p k o", p=P)),
                                 (wv_raw[:], a["w_v2"].rearrange("(k p) o -> p k o", p=P))):
                    sp.dma_start(dst, src).then_inc(s_vec, 16)

            @block.scalar
            def _(act):
                act.wait_ge(s_pd, 1)
                act.activation(rstd[:, :], rstd[:, :], ACT.Sqrt).then_inc(s_pa, 1)
                act.wait_ge(s_vec, 64)
                act.activation(wk_hi[:], wk_raw[:], ACT.Copy).then_inc(s_pa, 1)
                act.activation(wv_hi[:], wv_raw[:], ACT.Copy).then_inc(s_pa, 1)
                act.activation(wr_hi[:], wr_raw[:], ACT.Copy).then_inc(s_pa, 1)

            @block.vector
            def _(dve):
                dve.tensor_scalar(rstd[:, :], mv1[:, :, 1], LN_EPS, None, ALU.add).then_inc(s_pd, 1)
                dve.memset(xc[:, :, :, 0:1], 0.0).then_inc(s_pd, 1)
                dve.wait_ge(s_pa, 1)
                dve.reciprocal(rstd[:, :], rstd[:, :]).then_inc(s_pd, 1)
                dve.wait_ge(s_vec, 64)
                dve.tensor_scalar(one_m[:], vecs[:, :, 0:2], -1.0, 1.0, ALU.mult, ALU.add).then_inc(s_pd, 1)
                for n, (lo, raw, hi) in enumerate(((wk_lo, wk_raw, wk_hi), (wv_lo, wv_raw, wv_hi), (wr_lo, wr_raw, wr_hi))):
                    dve.wait_ge(s_pa, n + 2)
                    dve.tensor_tensor(lo[:], raw[:], hi[:].bitcast(F32), ALU.subtract).then_inc(s_pd, 1)

        xn = sb("xn2", [P, BT, D])
        old = sb("old", [P, 2, KT, BLK])
        mixed = sb("mixed", [P, 2, KT, BLK])
        xk_hi = sb("xk_hi", [P, KT, 2, BLK], F32R)
        xk_lo = sb("xk_lo", [P, KT, 2, BLK], F32R)
        xr_hi = sb("xr_hi", [P, KT, BLK], F32R)
        xr_lo = sb("xr_lo", [P, KT, BLK], F32R)
        pos = sb("pos", [P, 2, BLK])
        sqr = sb("sqr", [P, 2, BLK])
        hid_hi = sb("hid2_hi", [P, NH, BLK], F32R)
        hid_lo = sb("hid2_lo", [P, NH, BLK], F32R)
        gate = sb("gate2", [P, BT, D])
        stats = TileStats("h_stats2", sb, sem)
        p_t = [ps(f"p_t2_{k}", [P, BLK]) for k in range(KT)]
        p_u = [ps(f"p_u2_{k}", [P, BLK]) for k in range(2)]
        p_y = ps("p_y2", [P, BT, D])
        p_r = ps("p_r2", [P, BT, D])

        s_xn = sem("xn2_ready")
        s_tr = sem("transposed2")
        s_xc = sem("xc_ready")
        s_old = sem("old_ready")
        s_mx = sem("mixed_ready")
        s_xh = sem("x2_hi_ready")
        s_xl = sem("x2_lo_ready")
        s_r = sem("r_projected")
        s_g = sem("gate2_ready")
        s_up = sem("up_projected")
        s_po = sem("relu_ready")
        s_sq = sem("square_ready")
        s_hh = sem("hid2_hi_ready")
        s_hl = sem("hid2_lo_ready")
        s_dn = [sem(f"down_applied{j}") for j in range(NH)]
        s_hx = sem("h_plus_x1")
        s_ry = sem("gated")
        s_h = sem("h_updated2")

        with nc.Block() as block:
            @block.tensor
            def _(pe):
                def transposes(i):
                    pe.wait_ge(s_xn, BT * (i + 1))
                    for kt in range(KT):
                        for t in range(BT):
                            mm = pe.transpose(p_t[kt][:, t * P:(t + 1) * P], xn[:, t, kt * P:(kt + 1) * P], chip.ident[:, :])
                        mm.then_inc(s_tr, 1)

                def up(i, j, first):
                    if j >= 2 or not first:
                        pe.wait_ge(s_po, NH * i + j - 1)
                    if j == 0:
                        pe.wait_ge(s_xl, 2 * KT * (i + 1))
                    split_matmuls(pe, p_u[j % 2][:, :], [(wk_hi[:, k, j * P:(j + 1) * P], wk_lo[:, k, j * P:(j + 1) * P]) for k in range(KT)],
                                  [(xk_hi[:, k, ds(i % 2, 1)], xk_lo[:, k, ds(i % 2, 1)]) for k in range(KT)]).then_inc(s_up, 1)

                def down(i, j, first=False):
                    pe.wait_ge(s_hl, NH * i + j + 1)
                    if j == 0 and not first:
                        pe.wait_ge(s_ry, BT * i)
                    for t in range(BT):
                        hi, lo = hid_hi[:, j, t * P:(t + 1) * P], hid_lo[:, j, t * P:(t + 1) * P]
                        pe.matmul(p_y[:, t], hi, wv_hi[:, j], start=(j == 0 and t % 2 == 0), stop=False, skip_group_check=True)
                        pe.matmul(p_y[:, t], hi, wv_lo[:, j], start=False, stop=False, skip_group_check=True)
                        mm = pe.matmul(p_y[:, t], lo, wv_hi[:, j], start=False, stop=(j == NH - 1), skip_group_check=True)
                    mm.then_inc(s_dn[j], 1)

                def gates(i, first):
                    if not first:
                        pe.wait_ge(s_g, 2 * i)
                    for t in range(BT):
                        mm = split_matmuls(pe, p_r[:, t], [(xr_hi[:, k, t * P:(t + 1) * P], xr_lo[:, k, t * P:(t + 1) * P]) for k in range(KT)],
                                           [(wr_hi[:, k], wr_lo[:, k]) for k in range(KT)])
                        if t % 2:
                            mm.then_inc(s_r, 1)

                def body(i, first=False, last=False):
                    for j in range(NH):
                        up(i, j, first)
                        if j >= 2:
                            down(i, j - 2, first)
                        elif not first:
                            down(i - 1, NH + j - 2)
                        if j == 1:
                            gates(i, first)
                        if j == 4 and not last:
                            transposes(i + 1)

                transposes(0)
                body(0, first=True)
                with pe.Fori(1, NB - 1, 1) as i:
                    body(i)
                body(NB - 1, last=True)
                for j in range(NH - 2, NH):
                    down(NB - 1, j)

            @block.scalar
            def _(act):
                def rows(i, first=False):
                    if not first:
                        act.wait_ge(s_mx, 2 * KT * i)
                    for kt in range(KT):
                        act.wait_ge(s_tr, KT * i + kt + 1)
                        act.activation(xc[:, kt, :, 1:1 + S], by_image(p_t[kt][:, :]), ACT.Identity, bias=vecs[:, kt, 3:4], scale=vecs[:, kt, 2:3]).then_inc(s_xc, 1)
                    act.wait_ge(s_xc, KT * (i + 1))
                    for kt in range(KT):
                        for v in range(2):
                            act.activation(by_image(old[:, v, kt]), xc[:, kt, :, 0:S], ACT.Copy, scale=one_m[:, kt, v:v + 1]).then_inc(s_old, 1)

                def high_parts(i, first=False):
                    if not first:
                        act.wait_ge(s_r, 2 * i)
                    for kt in range(KT):
                        for v in range(2):
                            act.wait_ge(s_mx, 2 * KT * i + 2 * kt + v + 1)
                            dst = xk_hi[:, kt, ds(i % 2, 1)] if v == 0 else xr_hi[:, kt:kt + 1]
                            act.activation(dst, mixed[:, v, kt:kt + 1], ACT.Copy).then_inc(s_xh, 1)

                def gates(i, first):
                    if not first:
                        act.wait_ge(s_h, BT * i)
                    for n in range(2):
                        act.wait_ge(s_r, 2 * i + n + 1)
                        act.activation(gate[:, 2 * n:2 * n + 2], p_r[:, 2 * n:2 * n + 2], ACT.Sigmoid).then_inc(s_g, 1)

                def high(i, j, first=False):
                    act.wait_ge(s_sq, NH * i + j + 1)
                    if not first:
                        act.wait_ge(s_dn[j], i)
                    act.activation(hid_hi[:, j], sqr[:, j % 2], ACT.Copy).then_inc(s_hh, 1)

                def body(i, first=False, last=False):
                    for j in range(NH):
                        act.wait_ge(s_up, NH * i + j + 1)
                        if j >= 2 or not first:
                            act.wait_ge(s_sq, NH * i + j - 1)
                        act.activation(pos[:, j % 2], p_u[j % 2][:, :], ACT.Relu).then_inc(s_po, 1)
                        if j:
                            high(i, j - 1, first)
                        elif not first:
                            high(i - 1, NH - 1)
                        if j == 3:
                            gates(i, first)
                        if not last:
                            if j == 4:
                                rows(i + 1)
                            if j == 5:
                                high_parts(i + 1)

                rows(0, first=True)
                high_parts(0, first=True)
                body(0, first=True)
                with act.Fori(1, NB - 1, 1) as i:
                    body(i)
                body(NB - 1, last=True)
                high(NB - 1, NH - 1)

            @block.gpsimd
            def _(pool):
                with pool.Fori(0, NB, 1) as i:
                    for kt in range(KT):
                        for v in range(2):
                            pool.wait_ge(s_xh, 2 * KT * i + 2 * kt + v + 1)
                            hi = xk_hi[:, kt, ds(i % 2, 1)] if v == 0 else xr_hi[:, kt:kt + 1]
                            dst = xk_lo[:, kt, ds(i % 2, 1)] if v == 0 else xr_lo[:, kt:kt + 1]
                            pool.tensor_tensor(dst, mixed[:, v, kt:kt + 1], hi.bitcast(F32), ALU.subtract).then_inc(s_xl, 1)
                    for t in range(BT):
                        tile = ds(BT * i + t, 1)
                        pool.tensor_tensor(chip.h[:, tile], chip.h[:, tile], x1[:, tile], ALU.add).then_inc(s_hx, 1)

            @block.vector
            def _(dve):
                def rows(i, first=False):
                    if not first:
                        dve.wait_ge(s_tr, KT * i)
                    for t in range(BT):
                        tile = ds(BT * i + t, 1)
                        dve.tensor_scalar(xn[:, t:t + 1], x1[:, tile], mv1[:, tile, 0], rstd[:, tile], ALU.subtract, ALU.mult).then_inc(s_xn, 1)

                def mixes(i, first=False):
                    if not first:
                        dve.wait_ge(s_xl, 2 * KT * i)
                    for kt in range(KT):
                        for v in range(2):
                            dve.wait_ge(s_old, 2 * KT * i + 2 * kt + v + 1)
                            dve.scalar_tensor_tensor(out=by_image(mixed[:, v, kt]), in0=xc[:, kt, :, 1:1 + S], scalar=vecs[:, kt, v:v + 1],
                                                     in1=by_image(old[:, v, kt]), op0=ALU.mult, op1=ALU.add).then_inc(s_mx, 1)

                def low(i, j):
                    dve.wait_ge(s_hh, NH * i + j + 1)
                    dve.tensor_tensor(hid_lo[:, j], sqr[:, j % 2], hid_hi[:, j].bitcast(F32), ALU.subtract).then_inc(s_hl, 1)

                def results(i):
                    dve.wait_ge(s_g, 2 * (i + 1))
                    dve.wait_ge(s_dn[NH - 1], i + 1)
                    for t in range(BT):
                        dve.tensor_tensor(gate[:, t], gate[:, t], p_y[:, t], ALU.mult).then_inc(s_ry, 1)
                    dve.wait_ge(s_hx, BT * (i + 1))
                    for t in range(BT):
                        h = chip.h[:, ds(BT * i + t, 1)]
                        dve.wait_ge(s_ry, BT * i + t + 1)
                        dve.tensor_tensor(h, h, gate[:, t:t + 1], ALU.add).then_inc(s_h, 1)

                def statistics(i):
                    dve.wait_ge(s_h, BT * (i + 1))
                    stats.block(dve, chip.h, chip.mv, i)

                def body(i, first=False, last=False):
                    for j in range(NH):
                        dve.wait_ge(s_po, NH * i + j + 1)
                        if j >= 2 or not first:
                            dve.wait_ge(s_hl, NH * i + j - 1)
                        dve.tensor_tensor(sqr[:, j % 2], pos[:, j % 2], pos[:, j % 2], ALU.mult).then_inc(s_sq, 1)
                        if j:
                            low(i, j - 1)
                        elif not first:
                            low(i - 1, NH - 1)
                        if j == 1 and not first:
                            results(i - 1)
                        if j == 2 and not last:
                            rows(i + 1)
                        if j == 3 and not first:
                            statistics(i - 1)
                        if j == 4 and not last:
                            mixes(i + 1)

                rows(0, first=True)
                mixes(0, first=True)
                body(0, first=True)
                with dve.Fori(1, NB - 1, 1) as i:
                    body(i)
                body(NB - 1, last=True)
                low(NB - 1, NH - 1)
                results(NB - 1)
                statistics(NB - 1)
                stats.finish(dve)


def ternary_stage(chip, a, out):
    nc = chip.nc
    EPS = 1e-8
    NH = 4 * D // P
    LAG = 3
    RING = 4
    with ExitStack() as ctx:
        def sb(name, shape, dt=F32):
            return ctx.enter_context(nc.sbuf_tensor(name, shape, dt))

        def ps(name, shape):
            return ctx.enter_context(nc.psum_tensor(name, shape, F32))

        sem = stage_semaphores(nc, ctx)

        x_hi = sb("xt_hi", [P, KT, 2 * BI, XS], F32R)
        x_lo = sb("xt_lo", [P, KT, 2 * BI, XS], F32R)
        w_up = sb("w_up", [P, KT, NH * P], F32R)
        w_down = sb("w_down", [P, NH, D], F32R)
        ones = sb("ones3", [P, P])
        root = sb("root", [P, 2, NT])
        scale = sb("scale3", [P, NT])
        s_ld = sem("ternary_loaded")
        s_pd = sem("ternary_prep_dve")
        s_tot = sem("weight_sums")
        s_pa = sem("ternary_prep_act")

        with nc.sbuf_tensor("up_raw", [P, KT, NH * P], F32) as up_raw, nc.sbuf_tensor("down_raw", [P, NH, D], F32) as down_raw, \
                nc.sbuf_tensor("above", [P, KT * NH * P], F32) as above, nc.sbuf_tensor("below", [P, KT * NH * P], F32) as below, \
                nc.sbuf_tensor("abs_sum", [P, 2], F32) as abs_sum, nc.sbuf_tensor("limits", [P, 2, 2], F32) as limits, \
                nc.psum_tensor("total", [P, 2], F32) as total, nc.Block() as block:
            @block.sync
            def _(sp):
                for dst, src in ((up_raw[:], a["w_up"].rearrange("(k p) o -> p k o", p=P)),
                                 (down_raw[:], a["w_down"].rearrange("(k p) o -> p k o", p=P)), (ones[:], a["ones"])):
                    sp.dma_start(dst, src).then_inc(s_ld, 16)

            @block.tensor
            def _(pe):
                pe.wait_ge(s_pd, 2)
                pe.matmul(total[:, :], ones[:, :], abs_sum[:, :], start=True, stop=True).then_inc(s_tot, 1)

            @block.scalar
            def _(act):
                act.wait_ge(s_pa, 1)
                act.activation(root[:], root[:], ACT.Sqrt).then_inc(s_pa, 1)

            @block.vector
            def _(dve):
                dve.wait_ge(s_ld, 48)
                for n, raw in enumerate((up_raw, down_raw)):
                    dve.tensor_reduce(abs_sum[:, n:n + 1], raw[:], AX.XY, ALU.add, apply_absolute_value=True).then_inc(s_pd, 1)
                dve.tensor_copy(root[:, 0], chip.mv[:, :, 1]).then_inc(s_pd, 1)
                dve.wait_ge(s_pd, 3)
                dve.tensor_scalar(root[:, 1], chip.mv[:, :, 1], LN_EPS, None, ALU.add).then_inc(s_pa, 1)
                dve.wait_ge(s_pa, 2)
                dve.scalar_tensor_tensor(out=scale[:, :], in0=root[:, 1], scalar=EPS, in1=root[:, 0], op0=ALU.mult, op1=ALU.add).then_inc(s_pd, 1)
                dve.wait_ge(s_pd, 4)
                dve.reciprocal(scale[:, :], scale[:, :]).then_inc(s_pd, 1)
                dve.wait_ge(s_tot, 1)
                half_mean = 0.5 / (D * NH * P)
                dve.tensor_scalar(limits[:, 0], total[:, :], half_mean, None, ALU.mult).then_inc(s_pd, 1)
                dve.tensor_scalar(limits[:, 1], total[:, :], -half_mean, None, ALU.mult).then_inc(s_pd, 1)
                n = 7
                for k, (raw, dst) in enumerate(((up_raw, w_up), (down_raw, w_down))):
                    flat = raw[:].rearrange("p a b -> p (a b)")
                    dve.wait_ge(s_pd, n)
                    dve.tensor_scalar(above[:, :], flat, limits[:, 0, k:k + 1], None, ALU.is_gt).then_inc(s_pd, 1)
                    dve.tensor_scalar(below[:, :], flat, limits[:, 1, k:k + 1], None, ALU.is_lt).then_inc(s_pd, 1)
                    dve.wait_ge(s_pd, n + 2)
                    dve.tensor_tensor(dst[:].rearrange("p a b -> p (a b)"), above[:, :], below[:, :], ALU.subtract).then_inc(s_pd, 1)
                    n += 3

        xn = sb("xn3", [P, BT, D])
        act_out = sb("act_out", [P, RING, BLK])
        squares = sb("squares", [P, RING, BLK])
        acc = sb("squares_sum", [P, BLK])
        hid_hi = sb("hid3_hi", [P, NH, BLK], F32R)
        hid_lo = sb("hid3_lo", [P, NH, BLK], F32R)
        rms = sb("rms", [P, BT])
        p_t = ps("p_t3", [P, BLK])
        p_u = [ps(f"p_u3_{k}", [P, BLK]) for k in range(2)]
        p_y = [ps(f"p_y3_{n}", [P, BT, D]) for n in range(2)]
        p_s = ps("p_s3", [P, BT])

        s_xn = sem("xn3_ready")
        s_tr = sem("transposed3")
        s_xh = sem("x3_hi_ready")
        s_xl = sem("x3_lo_ready")
        s_up = sem("up3_projected")
        s_ge = sem("gelu_ready")
        s_sq = sem("gelu_squared")
        s_ac = sem("squares_added")
        s_hh = sem("hid3_hi_ready")
        s_hl = sem("hid3_lo_ready")
        s_ss = sem("squares_summed")
        s_dn = [sem(f"down3_applied{j}") for j in range(NH)]
        s_rt = sem("rms_ready")
        s_rc = sem("rms_chain")
        s_h = sem("h_updated3")
        s_o = sem("out_stored")

        with nc.Block() as block:
            @block.sync
            def _(sp):
                with sp.Fori(0, NB, 1) as i:
                    sp.wait_ge(s_h, BT * (i + 1))
                    sp.dma_start(out[ds(i * BLK, BLK), :].rearrange("(t p) c -> p t c", p=P), chip.h[:, ds(BT * i, BT)]).then_inc(s_o, 16)
                sp.wait_ge(s_o, 16 * NB)

            @block.tensor
            def _(pe):
                def transposes(i, kt, first=False):
                    if kt == 0:
                        pe.wait_ge(s_xn, BT * (i + 1))
                    if kt or not first:
                        pe.wait_ge(s_xl, KT * i + kt)
                    for t in range(BT):
                        mm = pe.transpose(p_t[:, t * P:(t + 1) * P], xn[:, t, kt * P:(kt + 1) * P], chip.ident[:, :])
                    mm.then_inc(s_tr, 1)

                def up(i, j, first):
                    if j == 0:
                        pe.wait_ge(s_xl, KT * (i + 1))
                    if j >= 2 or not first:
                        pe.wait_ge(s_ge, NH * i + j - 1)
                    for k in range(KT):
                        w = w_up[:, k, j * P:(j + 1) * P]
                        pe.matmul(p_u[j % 2][:, :], w, ring_block(x_hi, k, i), start=(k == 0), stop=False)
                        mm = pe.matmul(p_u[j % 2][:, :], w, ring_block(x_lo, k, i), start=False, stop=(k == KT - 1))
                    mm.then_inc(s_up, 1)

                def down(i, j, parity):
                    pe.wait_ge(s_hl, NH * i + j + 1)
                    for t in range(BT):
                        y = p_y[parity][:, t]
                        pe.matmul(y, hid_hi[:, j, t * P:(t + 1) * P], w_down[:, j], start=(j == 0 and t % 2 == 0), stop=False, skip_group_check=True)
                        mm = pe.matmul(y, hid_lo[:, j, t * P:(t + 1) * P], w_down[:, j], start=False, stop=(j == NH - 1), skip_group_check=True)
                    mm.then_inc(s_dn[j], 1)

                def sums(i, first=False):
                    pe.wait_ge(s_ac, (NH - 1) * (i + 1))
                    if not first:
                        pe.wait_ge(s_rt, i)
                    for t in range(BT):
                        mm = pe.matmul(p_s[:, t:t + 1], acc[:, t * P:(t + 1) * P], ones[:, 0:1], start=(t == 0), stop=(t == BT - 1), skip_group_check=True)
                    mm.then_inc(s_ss, 1)

                def body(i, parity, first=False, second=False, last=False):
                    for j in range(NH):
                        up(i, j, first)
                        if j == LAG and not first and not second:
                            pe.wait_ge(s_h, BT * (i - 1))
                        if j >= LAG:
                            down(i, j - LAG, parity)
                        elif not first:
                            down(i - 1, NH + j - LAG, 1 - parity)
                        if j == 0 and not last:
                            transposes(i + 1, 0)
                        if j == 3 and not last:
                            transposes(i + 1, 1)
                        if j == 4 and not first:
                            sums(i - 1, second)

                for kt in range(KT):
                    transposes(0, kt, first=True)
                body(0, 0, first=True)
                body(1, 1, second=True)
                with pe.Fori(1, NB // 2 - 1, 1) as n:
                    body(2 * n, 0)
                    body(2 * n + 1, 1)
                body(NB - 2, 0)
                body(NB - 1, 1, last=True)
                for j in range(NH - LAG, NH):
                    down(NB - 1, j, 1)
                sums(NB - 1)

            @block.scalar
            def _(act):
                def rows(i, kt):
                    act.wait_ge(s_tr, KT * i + kt + 1)
                    act.activation(ring_block(x_hi, kt, i), by_image(p_t[:, :]), ACT.Copy).then_inc(s_xh, 1)

                def high(i, j, first):
                    act.wait_ge(s_ge, NH * i + j + 1)
                    if not first:
                        act.wait_ge(s_dn[j], i)
                    act.activation(hid_hi[:, j], act_out[:, j % RING], ACT.Copy).then_inc(s_hh, 1)

                def root_mean(i, first=False):
                    act.wait_ge(s_ss, i + 1)
                    if not first:
                        act.wait_ge(s_h, BT * i)
                    act.activation(rms[:, :], p_s[:, :], ACT.Sqrt, scale=1.0 / (NH * P)).then_inc(s_rt, 1)

                def body(i, first=False, second=False, last=False):
                    for j in range(NH):
                        act.wait_ge(s_up, NH * i + j + 1)
                        if j >= RING or not first:
                            act.wait_ge(s_hl, NH * i + j - RING + 1)
                            act.wait_ge(s_sq, NH * i + j - RING + 1)
                        act.activation(act_out[:, j % RING], p_u[j % 2][:, :], ACT.Gelu).then_inc(s_ge, 1)
                        if j:
                            high(i, j - 1, first)
                        elif not first:
                            high(i - 1, NH - 1, second)
                        if j == 1 and not last:
                            rows(i + 1, 0)
                        if j == 4 and not last:
                            rows(i + 1, 1)
                        if j == 5 and not first:
                            root_mean(i - 1, second)

                for kt in range(KT):
                    rows(0, kt)
                body(0, first=True)
                body(1, second=True)
                with act.Fori(2, NB - 1, 1) as i:
                    body(i)
                body(NB - 1, last=True)
                high(NB - 1, NH - 1, False)
                root_mean(NB - 1)

            @block.gpsimd
            def _(pool):
                def body(i, first=False):
                    for j in range(1, NH):
                        pool.wait_ge(s_sq, NH * i + j + 1)
                        if j == 1:
                            if not first:
                                pool.wait_ge(s_ss, i)
                            pool.tensor_tensor(acc[:, :], squares[:, 0], squares[:, 1], ALU.add).then_inc(s_ac, 1)
                        else:
                            pool.wait_ge(s_ac, (NH - 1) * i + j - 1)
                            pool.tensor_tensor(acc[:, :], acc[:, :], squares[:, j % RING], ALU.add).then_inc(s_ac, 1)

                body(0, first=True)
                with pool.Fori(1, NB, 1) as i:
                    body(i)

            @block.vector
            def _(dve):
                def rows(i, first=False):
                    if not first:
                        dve.wait_ge(s_tr, KT * i)
                    for t in range(BT):
                        tile = ds(BT * i + t, 1)
                        dve.tensor_scalar(xn[:, t:t + 1], chip.h[:, tile], chip.mv[:, tile, 0], scale[:, tile], ALU.subtract, ALU.mult).then_inc(s_xn, 1)

                def rows_low(i, kt):
                    dve.wait_ge(s_xh, KT * i + kt + 1)
                    dve.tensor_tensor(ring_block(x_lo, kt, i), by_image(p_t[:, :]), ring_block(x_hi, kt, i).bitcast(F32), ALU.subtract).then_inc(s_xl, 1)

                def low(i, j):
                    dve.wait_ge(s_hh, NH * i + j + 1)
                    dve.tensor_tensor(hid_lo[:, j], act_out[:, j % RING], hid_hi[:, j].bitcast(F32), ALU.subtract).then_inc(s_hl, 1)

                def results(i, parity):
                    dve.wait_ge(s_rt, i + 1)
                    dve.tensor_scalar(rms[:, :], rms[:, :], EPS, None, ALU.add).then_inc(s_rc, 1)
                    dve.wait_ge(s_rc, 2 * i + 1)
                    dve.reciprocal(rms[:, :], rms[:, :]).then_inc(s_rc, 1)
                    dve.wait_ge(s_rc, 2 * i + 2)
                    dve.wait_ge(s_dn[NH - 1], i + 1)
                    for t in range(BT):
                        h = chip.h[:, ds(BT * i + t, 1)]
                        dve.scalar_tensor_tensor(out=h, in0=p_y[parity][:, t:t + 1], scalar=rms[:, t:t + 1], in1=h, op0=ALU.mult, op1=ALU.add).then_inc(s_h, 1)

                def body(i, parity, first=False, ahead=2):
                    for j in range(NH):
                        dve.wait_ge(s_ge, NH * i + j + 1)
                        if j >= RING:
                            dve.wait_ge(s_ac, (NH - 1) * i + max(j - RING, 1))
                        elif not first:
                            dve.wait_ge(s_ac, (NH - 1) * i + j - RING + 1)
                        dve.tensor_tensor(squares[:, j % RING], act_out[:, j % RING], act_out[:, j % RING], ALU.mult).then_inc(s_sq, 1)
                        if j:
                            low(i, j - 1)
                        elif not first:
                            low(i - 1, NH - 1)
                        if j == 2 and ahead >= 1:
                            rows_low(i + 1, 0)
                        if j == 5 and ahead >= 1:
                            rows_low(i + 1, 1)
                        if j == 5 and ahead >= 2:
                            rows(i + 2)
                        if j == 7 and not first:
                            results(i - 1, 1 - parity)

                rows(0, first=True)
                for kt in range(KT):
                    rows_low(0, kt)
                rows(1)
                body(0, 0, first=True)
                with dve.Fori(0, NB // 2 - 2, 1) as n:
                    body(2 * n + 1, 1)
                    body(2 * n + 2, 0)
                body(NB - 3, 1)
                body(NB - 2, 0, ahead=1)
                body(NB - 1, 1, ahead=0)
                low(NB - 1, NH - 1)
                results(NB - 1, 1)


def build_program(nc, a, out, scratch, stop=9, start=0):
    with ExitStack() as ctx:
        chip = Chip(nc, ctx)
        route = Routing(nc, ctx)
        with nc.sbuf_tensor("x_hi", [P, KT, B, XS], F32R) as chip.x_hi, nc.sbuf_tensor("x_lo", [P, KT, B, XS], F32R) as chip.x_lo:
            wavelet_stage(chip, a["x"], [a["wd_fine"], a["wd_mid"], a["wd_coarse"]], a["wa"], a["wave_bias"], scratch["h_rows"], scratch["slot_x"], a)
            if stop > 0:
                attention_stage(chip, a)
            if stop > 1:
                with nc.sbuf_tensor("xn_rows", [P, NT, D], F32) as xn:
                    gate_stage(chip, a, route, xn)
                    shared_expert_stage(chip, a, route, xn, scratch["slot_x"])
        if stop > 1:
            routed_experts_stage(chip, a, route, scratch["slot_x"], scratch["slot_y"])
            combine_stage(chip, route, scratch["slot_y"])
        if stop > 2:
            with nc.sbuf_tensor("x1", [P, NT, D], F32) as x1, nc.sbuf_tensor("mv1", [P, NT, 2], F32) as mv1:
                time_mix_stage(chip, a, x1, mv1)
                channel_mix_stage(chip, a, x1, mv1)
        if stop <= 3:
            return store_h(chip, out)
        ternary_stage(chip, a, out)


def store_h(chip, out):
    nc = chip.nc
    with nc.semaphore("out_stored") as s_out, nc.Block() as block:
        @block.sync
        def _(sp):
            sp.dma_start(out.rearrange("(t p) c -> p t c", p=P), chip.h[:]).then_inc(s_out, 16)
            sp.wait_ge(s_out, 16)


def layout(inputs):
    import numpy as np

    f = {k: np.asarray(v) for k, v in inputs.items()}
    a = {"x": f["x"].reshape(B * S // 8, 8 * 256)}
    for name, w, rows, cols in (("wd_fine", f["L0_tok_Wd3"], 4, 128), ("wd_mid", f["L0_tok_Wd2"], 2, 64), ("wd_coarse", f["L0_tok_Wd1"], 1, 32)):
        a[name] = w.reshape(3, 32, rows, cols, 3).transpose(1, 4, 0, 2, 3).reshape(32, -1)
    a["wa"] = f["L0_tok_Wa"].reshape(32, 32)
    a["wave_bias"] = np.concatenate([f["L0_tok_bd3"], f["L0_tok_bd2"], f["L0_tok_bd1"], f["L0_tok_ba"]])
    level = np.array([1, 1, 1, 2, 2, 2, 3, 3, 3, 3])
    a["scale_in"] = np.broadcast_to(0.5 ** level, (P, 10)).astype(np.float32)
    a["scale_out"] = np.broadcast_to(0.25 ** level, (P, 10)).astype(np.float32)
    a["group"] = np.kron(np.eye(4), np.ones((32, 32))).astype(np.float32)
    a["ident"] = np.eye(P, dtype=np.float32)
    a["w_qkv"] = np.concatenate([f["L0_attn_Wq"], f["L0_attn_Wk"], f["L0_attn_Wv"]])
    a["b_qkv"] = np.stack([f["L0_attn_bq"], f["L0_attn_bk"], f["L0_attn_bv"], np.zeros(D, np.float32)], axis=1)
    e, n = np.arange(D)[:, None], np.arange(P)[None, :]
    turn = 2 * np.pi * (e * n % D) / D
    sign = np.where(np.arange(D) % 2, -1.0, 1.0)
    a["fourier"] = np.concatenate([np.cos(turn), -np.sin(turn), sign[:, None], np.zeros((D, 1))], axis=1).astype(np.float32)
    twice = np.where(np.arange(P) == 0, 1.0, 2.0)[:, None] / D
    a["inverse"] = np.concatenate([-twice * np.cos(turn).T, twice * np.sin(turn).T]).astype(np.float32)
    a["alt_cols"] = np.broadcast_to(sign[:P, None], (P, P)).astype(np.float32)
    a["alt_row"] = np.broadcast_to(sign[None, :] / D, (P, D)).astype(np.float32)
    a["tri"] = np.triu(np.ones((P, P), np.float32))
    a["ones"] = np.ones((P, P), np.float32)
    a["gate_w"] = f["L0_ffn_gate_w"].T
    a["gate_b"] = f["L0_ffn_gate_b"]
    b2 = np.concatenate([f["L0_ffn_b2"], f["L0_ffn_sb2"][None]])
    a["b_out"] = np.broadcast_to(b2[:, None], (E + 1, P, D)).reshape((E + 1) * P, D)
    a["before"] = np.broadcast_to(np.tril(np.ones((E, E), np.float32), -1).reshape(1, -1), (P, E * E))
    w1 = np.concatenate([f["L0_ffn_w1"], f["L0_ffn_sw1"][None]]).reshape(E + 1, KT, P, I // P, P, 2)
    w3 = np.concatenate([f["L0_ffn_w3"], f["L0_ffn_sw3"][None]]).reshape(E + 1, KT, P, I // P, P, 2)
    a["w13"] = np.stack([w1, w3], axis=-1).transpose(0, 3, 2, 1, 5, 6, 4).reshape((E + 1) * NJ * P, -1)
    b1 = np.concatenate([f["L0_ffn_b1"], f["L0_ffn_sb1"][None]]).reshape(E + 1, I // P, P, 2)
    b3 = np.concatenate([f["L0_ffn_b3"], f["L0_ffn_sb3"][None]]).reshape(E + 1, I // P, P, 2)
    a["b13"] = np.stack([b1, b3], axis=-1).transpose(0, 2, 1, 3, 4).reshape((E + 1) * P, -1)
    a["counts"] = np.broadcast_to(np.arange(NT // BT, dtype=np.float32) * BLK, (P, NT // BT))
    a["numbers"] = np.broadcast_to(np.arange(NRB, dtype=np.float32), (P, NRB))
    w2 = np.concatenate([f["L0_ffn_w2"], f["L0_ffn_sw2"][None]]).reshape(E + 1, I // P, P, D)
    a["w2"] = w2.transpose(0, 2, 1, 3).reshape((E + 1) * P, -1)
    g = {k[8:]: v for k, v in f.items() if k.startswith("L1_attn_")}
    zero = np.zeros(D, np.float32)
    a["mix_vecs"] = np.stack([g["time_mix_k"], g["time_mix_v"], g["time_mix_r"], g["ln1_g"], g["ln1_b"], g["time_decay"], g["time_first"], zero], axis=1)
    a["w_kvr"] = np.concatenate([g["att_Wk"].T, g["att_Wv"].T, g["att_Wr"].T], axis=1)
    a["w_o"] = g["att_Wo"].T
    a["cm_vecs"] = np.stack([g["cm_k"], g["cm_r"], g["ln2_g"], g["ln2_b"]], axis=1)
    a["w_r2"] = g["ffn_Wr"].T
    a["w_k2"] = g["ffn_Wk"].T
    a["w_v2"] = g["ffn_Wv"].T
    a["w_up"] = f["L1_ffn_w_up"].T
    a["w_down"] = f["L1_ffn_w_down"].T
    return {k: np.ascontiguousarray(v) for k, v in a.items()}


def kernel(stop=9, runner=None, **inputs):
    import numpy as np
    import concourse.bacc as bacc
    from concourse.bass_utils import run_bass_kernel_spmd

    arrays = layout(inputs)
    nc = bacc.Bacc("TRN2", target_bir_lowering=False, num_devices=1)
    args = {k: nc.dram_tensor(f"in_{k}", v.shape, mybir.dt.from_np(v.dtype), kind="ExternalInput").ap() for k, v in arrays.items()}
    out = nc.dram_tensor("out_h", (B * S, D), F32, kind="ExternalOutput").ap()
    scratch = {"h_rows": nc.dram_tensor("h_rows", (B * S, D), F32, kind="Internal").ap(),
               "slot_x": nc.dram_tensor("slot_x", (NRB * BLK, D), F32, kind="Internal").ap(),
               "slot_y": nc.dram_tensor("slot_y", (NRB * BLK, D), F32, kind="Internal").ap()}
    build_program(nc, args, out, scratch, stop)
    feed = {f"in_{k}": v for k, v in arrays.items()}
    if runner:
        return runner(nc, feed, ["out_h"])
    r = run_bass_kernel_spmd(nc, [feed], core_ids=[0])
    return r.results[0]["out_h"].reshape(B, S, D)
```
